# Optimizing a Trainium2 kernel written in Bass

```python
import numpy as np
import jax
import jax.numpy as jnp

def _softmax(x, axis=-1):
    return jax.nn.softmax(x, axis=axis)

def _gelu(x):
    return jax.nn.gelu(x, approximate=True)

def _silu(x):
    return jax.nn.silu(x)

def _sigmoid(x):
    return jax.nn.sigmoid(x)

def _layernorm(x, axis=-1, eps=1e-05):
    m = jnp.mean(x, axis=axis, keepdims=True)
    v = jnp.var(x, axis=axis, keepdims=True)
    return (x - m) / jnp.sqrt(v + eps)

def _scatter_add(tgt, idx, src, axis=0):
    return tgt.at[idx].add(src)

def _segment_sum(src, seg, n):
    return jax.ops.segment_sum(src, seg, n)
kernel_name = 'mk_macaron_d2_jaxref_r8_1540da'

def setup_inputs(seed: int=0):
    np.random.seed(seed)
    _w = jnp.asarray

    def _L0_attn_setup():
        import jax, jax.numpy as jnp
        import numpy as np
        GROUP = 64
        MAX_REL = 32

        def _silu(x):
            return x * jax.nn.sigmoid(x)

        def _ln(x, w, b, eps=1e-05):
            m = x.mean(-1, keepdims=True)
            v = ((x - m) ** 2).mean(-1, keepdims=True)
            return (x - m) / jnp.sqrt(v + eps) * w + b

        def _rope(x):
            n, d = (x.shape[-2], x.shape[-1])
            half = d // 2
            pos = jnp.arange(n, dtype=x.dtype)
            inv_freq = 10000.0 ** (-jnp.arange(half, dtype=x.dtype) / half)
            sinusoid = pos[:, None] * inv_freq[None, :]
            sin, cos = (jnp.sin(sinusoid), jnp.cos(sinusoid))
            x1, x2 = (x[..., :half], x[..., half:])
            return jnp.concatenate([x1 * cos - x2 * sin, x2 * cos + x1 * sin], axis=-1)
        key = jax.random.key(seed)
        ks = jax.random.split(key, 8)
        B, N, D, QK, H = (4, 512, 128, 32, 256)
        s = 0.02
        return {'x': jax.random.normal(ks[0], (B, N, D), dtype=jnp.float32), 'ln1_w': jnp.ones((D,), jnp.float32), 'ln1_b': jnp.zeros((D,), jnp.float32), 'Wqk': jax.random.normal(ks[1], (QK, D), jnp.float32) * s, 'bqk': jnp.zeros((QK,), jnp.float32), 'Wv': jax.random.normal(ks[2], (H, D), jnp.float32) * s, 'bv': jnp.zeros((H,), jnp.float32), 'Wg': jax.random.normal(ks[3], (H, D), jnp.float32) * s, 'bg': jnp.zeros((H,), jnp.float32), 'Wo': jax.random.normal(ks[4], (D, H), jnp.float32) * s, 'bo': jnp.zeros((D,), jnp.float32), 'ln2_w': jnp.ones((D,), jnp.float32), 'ln2_b': jnp.zeros((D,), jnp.float32), 'gamma': jax.random.normal(ks[5], (4, QK), jnp.float32) * 0.02, 'beta': jnp.zeros((4, QK), jnp.float32), 'pos_emb': jax.random.normal(ks[6], (2 * MAX_REL + 1,), jnp.float32)}
    _L0_attn_in = _L0_attn_setup()

    def _L0_ffn_setup():
        import jax, jax.numpy as jnp
        import numpy as np
        E = 8
        K = 2
        D = 128
        F = 512
        EPS = 1e-05

        def _layernorm(h, g, b):
            mu = h.mean(axis=-1, keepdims=True)
            var = ((h - mu) ** 2).mean(axis=-1, keepdims=True)
            return (h - mu) * jax.lax.rsqrt(var + EPS) * g[:, None, :] + b[:, None, :]
        key = jax.random.key(seed)
        ks = jax.random.split(key, 8)
        B, S = (2, 256)
        x = jax.random.normal(ks[0], (B, S, D), dtype=jnp.float32)
        Wr = jax.random.normal(ks[1], (D, E), dtype=jnp.float32) / np.sqrt(D)
        br = jnp.zeros((E,), dtype=jnp.float32)
        W1 = jax.random.normal(ks[2], (E, D, F), dtype=jnp.float32) / np.sqrt(D)
        b1 = jnp.zeros((E, F), dtype=jnp.float32)
        g1 = jnp.ones((E, F), dtype=jnp.float32)
        be1 = jnp.zeros((E, F), dtype=jnp.float32)
        W2 = jax.random.normal(ks[3], (E, F, D), dtype=jnp.float32) / np.sqrt(F)
        b2 = jnp.zeros((E, D), dtype=jnp.float32)
        g2 = jnp.ones((E, D), dtype=jnp.float32)
        be2 = jnp.zeros((E, D), dtype=jnp.float32)
        return {'x': x, 'Wr': Wr, 'br': br, 'W1': W1, 'b1': b1, 'g1': g1, 'be1': be1, 'W2': W2, 'b2': b2, 'g2': g2, 'be2': be2}
    _L0_ffn_in = _L0_ffn_setup()

    def _L1_attn_setup():
        import jax, jax.numpy as jnp
        import numpy as np
        NUM_HEAD = 16
        D_Q = 64
        D_KV = 64
        ROPE_BASE = 10000.0

        def _cos_sin(seq_len, dim):
            pos = jnp.arange(seq_len, dtype=jnp.float32)[:, None]
            ids = jnp.arange(dim // 2, dtype=jnp.float32)
            theta = ROPE_BASE ** (-2.0 * ids) / (dim // 2)
            r = pos * theta[None, :]
            return (jnp.cos(r), jnp.sin(r))

        def _rope(x, cos, sin):
            b, s, d = x.shape
            xv = x.reshape(b, s, d // 2, 2)
            x0, x1 = (xv[..., 0], xv[..., 1])
            out = jnp.stack([x0 * cos - x1 * sin, x1 * cos + x0 * sin], axis=-1)
            return out.reshape(b, s, d)
        key = jax.random.key(seed)
        ks = jax.random.split(key, 10)
        d_model, d_q, d_kv = (128, D_Q, D_KV)
        b, s = (2, 256)
        w = lambda k, i, o: jax.random.normal(k, (i, o), dtype=jnp.float32) * 0.02
        return {'x': jax.random.normal(ks[0], (b, s, d_model), dtype=jnp.float32), 'Wd_q_w': w(ks[1], d_model, d_q), 'Wd_q_b': jnp.zeros((d_q,), jnp.float32), 'Wu_q_w': w(ks[2], d_q, d_model), 'Wu_q_b': jnp.zeros((d_model,), jnp.float32), 'Wq_r_w': w(ks[3], d_q, d_model), 'Wq_r_b': jnp.zeros((d_model,), jnp.float32), 'Wk_r_w': w(ks[4], d_model, d_model), 'Wk_r_b': jnp.zeros((d_model,), jnp.float32), 'Wd_kv_w': w(ks[5], d_model, d_kv), 'Wd_kv_b': jnp.zeros((d_kv,), jnp.float32), 'Wu_k_w': w(ks[6], d_kv, d_model), 'Wu_k_b': jnp.zeros((d_model,), jnp.float32), 'Wu_v_w': w(ks[7], d_kv, d_model), 'Wu_v_b': jnp.zeros((d_model,), jnp.float32), 'Wo_w': w(ks[8], d_model, d_model), 'Wo_b': jnp.zeros((d_model,), jnp.float32)}
    _L1_attn_in = _L1_attn_setup()

    def _L1_ffn_setup():
        import jax, jax.numpy as jnp
        import numpy as np
        HIDDEN_SIZE = 128
        NUM_EXPERTS = 8
        MOE_INTERMEDIATE_SIZE = 176
        NUM_EXPERTS_PER_TOK = 2
        SHARED_EXPERT_INTERMEDIATE_SIZE = 352
        B, T = (2, 128)
        W_SCALE = 0.02
        key = jax.random.key(seed)
        ks = jax.random.split(key, 8)
        H, E, I, SI = (HIDDEN_SIZE, NUM_EXPERTS, MOE_INTERMEDIATE_SIZE, SHARED_EXPERT_INTERMEDIATE_SIZE)
        return {'x': jax.random.normal(ks[0], (B, T, H), jnp.float32), 'gate_w': jax.random.normal(ks[1], (E, H), jnp.float32) * W_SCALE, 'experts_gate_up': jax.random.normal(ks[2], (E, 2 * I, H), jnp.float32) * W_SCALE, 'experts_down': jax.random.normal(ks[3], (E, H, I), jnp.float32) * W_SCALE, 'shared_gate_w': jax.random.normal(ks[4], (SI, H), jnp.float32) * W_SCALE, 'shared_up_w': jax.random.normal(ks[5], (SI, H), jnp.float32) * W_SCALE, 'shared_down_w': jax.random.normal(ks[6], (H, SI), jnp.float32) * W_SCALE, 'shared_expert_gate_w': jax.random.normal(ks[7], (1, H), jnp.float32) * W_SCALE}
    _L1_ffn_in = _L1_ffn_setup()
    _d = {'L0_attn_x': _L0_attn_in['x'], 'L0_attn_ln1_w': _L0_attn_in['ln1_w'], 'L0_attn_ln1_b': _L0_attn_in['ln1_b'], 'L0_attn_Wqk': _L0_attn_in['Wqk'], 'L0_attn_bqk': _L0_attn_in['bqk'], 'L0_attn_Wv': _L0_attn_in['Wv'], 'L0_attn_bv': _L0_attn_in['bv'], 'L0_attn_Wg': _L0_attn_in['Wg'], 'L0_attn_bg': _L0_attn_in['bg'], 'L0_attn_Wo': _L0_attn_in['Wo'], 'L0_attn_bo': _L0_attn_in['bo'], 'L0_attn_ln2_w': _L0_attn_in['ln2_w'], 'L0_attn_ln2_b': _L0_attn_in['ln2_b'], 'L0_attn_gamma': _L0_attn_in['gamma'], 'L0_attn_beta': _L0_attn_in['beta'], 'L0_attn_pos_emb': _L0_attn_in['pos_emb'], 'L0_ffn_Wr': _L0_ffn_in['Wr'], 'L0_ffn_br': _L0_ffn_in['br'], 'L0_ffn_W1': _L0_ffn_in['W1'], 'L0_ffn_b1': _L0_ffn_in['b1'], 'L0_ffn_g1': _L0_ffn_in['g1'], 'L0_ffn_be1': _L0_ffn_in['be1'], 'L0_ffn_W2': _L0_ffn_in['W2'], 'L0_ffn_b2': _L0_ffn_in['b2'], 'L0_ffn_g2': _L0_ffn_in['g2'], 'L0_ffn_be2': _L0_ffn_in['be2'], 'L1_attn_Wd_q_w': _L1_attn_in['Wd_q_w'], 'L1_attn_Wd_q_b': _L1_attn_in['Wd_q_b'], 'L1_attn_Wu_q_w': _L1_attn_in['Wu_q_w'], 'L1_attn_Wu_q_b': _L1_attn_in['Wu_q_b'], 'L1_attn_Wq_r_w': _L1_attn_in['Wq_r_w'], 'L1_attn_Wq_r_b': _L1_attn_in['Wq_r_b'], 'L1_attn_Wk_r_w': _L1_attn_in['Wk_r_w'], 'L1_attn_Wk_r_b': _L1_attn_in['Wk_r_b'], 'L1_attn_Wd_kv_w': _L1_attn_in['Wd_kv_w'], 'L1_attn_Wd_kv_b': _L1_attn_in['Wd_kv_b'], 'L1_attn_Wu_k_w': _L1_attn_in['Wu_k_w'], 'L1_attn_Wu_k_b': _L1_attn_in['Wu_k_b'], 'L1_attn_Wu_v_w': _L1_attn_in['Wu_v_w'], 'L1_attn_Wu_v_b': _L1_attn_in['Wu_v_b'], 'L1_attn_Wo_w': _L1_attn_in['Wo_w'], 'L1_attn_Wo_b': _L1_attn_in['Wo_b'], 'L1_ffn_gate_w': _L1_ffn_in['gate_w'], 'L1_ffn_experts_gate_up': _L1_ffn_in['experts_gate_up'], 'L1_ffn_experts_down': _L1_ffn_in['experts_down'], 'L1_ffn_shared_gate_w': _L1_ffn_in['shared_gate_w'], 'L1_ffn_shared_up_w': _L1_ffn_in['shared_up_w'], 'L1_ffn_shared_down_w': _L1_ffn_in['shared_down_w'], 'L1_ffn_shared_expert_gate_w': _L1_ffn_in['shared_expert_gate_w']}
    _x0 = _d['L0_attn_x']
    _d['L0_attn_x'] = jax.random.normal(jax.random.fold_in(jax.random.key(seed), 1), (16, 256, 128), dtype=_x0.dtype)
    del _x0
    return _d

def reference(L0_attn_x, L0_attn_ln1_w, L0_attn_ln1_b, L0_attn_Wqk, L0_attn_bqk, L0_attn_Wv, L0_attn_bv, L0_attn_Wg, L0_attn_bg, L0_attn_Wo, L0_attn_bo, L0_attn_ln2_w, L0_attn_ln2_b, L0_attn_gamma, L0_attn_beta, L0_attn_pos_emb, L0_ffn_Wr, L0_ffn_br, L0_ffn_W1, L0_ffn_b1, L0_ffn_g1, L0_ffn_be1, L0_ffn_W2, L0_ffn_b2, L0_ffn_g2, L0_ffn_be2, L1_attn_Wd_q_w, L1_attn_Wd_q_b, L1_attn_Wu_q_w, L1_attn_Wu_q_b, L1_attn_Wq_r_w, L1_attn_Wq_r_b, L1_attn_Wk_r_w, L1_attn_Wk_r_b, L1_attn_Wd_kv_w, L1_attn_Wd_kv_b, L1_attn_Wu_k_w, L1_attn_Wu_k_b, L1_attn_Wu_v_w, L1_attn_Wu_v_b, L1_attn_Wo_w, L1_attn_Wo_b, L1_ffn_gate_w, L1_ffn_experts_gate_up, L1_ffn_experts_down, L1_ffn_shared_gate_w, L1_ffn_shared_up_w, L1_ffn_shared_down_w, L1_ffn_shared_expert_gate_w):

    def _L0_attn_ref(x, ln1_w, ln1_b, Wqk, bqk, Wv, bv, Wg, bg, Wo, bo, ln2_w, ln2_b, gamma, beta, pos_emb):
        import jax, jax.numpy as jnp
        import numpy as np
        GROUP = 64
        MAX_REL = 32

        def _silu(x):
            return x * jax.nn.sigmoid(x)

        def _ln(x, w, b, eps=1e-05):
            m = x.mean(-1, keepdims=True)
            v = ((x - m) ** 2).mean(-1, keepdims=True)
            return (x - m) / jnp.sqrt(v + eps) * w + b

        def _rope(x):
            n, d = (x.shape[-2], x.shape[-1])
            half = d // 2
            pos = jnp.arange(n, dtype=x.dtype)
            inv_freq = 10000.0 ** (-jnp.arange(half, dtype=x.dtype) / half)
            sinusoid = pos[:, None] * inv_freq[None, :]
            sin, cos = (jnp.sin(sinusoid), jnp.cos(sinusoid))
            x1, x2 = (x[..., :half], x[..., half:])
            return jnp.concatenate([x1 * cos - x2 * sin, x2 * cos + x1 * sin], axis=-1)
        b, n, d = x.shape
        G = GROUP
        x = _ln(x, ln1_w, ln1_b)
        qk = _silu(x @ Wqk.T + bqk)
        v = _silu(x @ Wv.T + bv)
        heads = qk[..., None, :] * gamma + beta
        quad_q, lin_q, quad_k, lin_k = (heads[..., i, :] for i in range(4))
        quad_q, lin_q, quad_k, lin_k = map(_rope, (quad_q, lin_q, quad_k, lin_k))
        g = n // G
        rs = lambda t: t.reshape(b, g, G, t.shape[-1])
        qq, lq, qkk, lk, vg = map(rs, (quad_q, lin_q, quad_k, lin_k, v))
        idx = jnp.arange(G)
        dist = jnp.clip(jnp.abs(idx[:, None] - idx[None, :]), 0, MAX_REL)
        bias = pos_emb[dist]
        quad_att = jnp.einsum('bgid,bgjd->bgij', qq, qkk) / G + bias
        attn = jax.nn.relu(quad_att) ** 2
        quad_out = jnp.einsum('bgij,bgje->bgie', attn, vg)
        lin_kv = jnp.einsum('bgnd,bgne->bde', lk, vg) / n
        lin_out = jnp.einsum('bgnd,bde->bgne', lq, lin_kv)
        qo = quad_out.reshape(b, n, -1)
        lo = lin_out.reshape(b, n, -1)
        gate = _silu(x @ Wg.T + bg)
        out = gate * (qo + lo)
        out = out @ Wo.T + bo
        return _ln(out, ln2_w, ln2_b)

    def _L0_ffn_ref(x, Wr, br, W1, b1, g1, be1, W2, b2, g2, be2):
        import jax, jax.numpy as jnp
        import numpy as np
        E = 8
        K = 2
        D = 128
        F = 512
        EPS = 1e-05

        def _layernorm(h, g, b):
            mu = h.mean(axis=-1, keepdims=True)
            var = ((h - mu) ** 2).mean(axis=-1, keepdims=True)
            return (h - mu) * jax.lax.rsqrt(var + EPS) * g[:, None, :] + b[:, None, :]
        B, S, _ = x.shape
        xt = x.reshape(-1, D)
        logits = xt @ Wr + br
        p = jax.nn.softmax(logits, axis=-1)
        probs, idx = jax.lax.top_k(p, K)
        probs = probs / probs.sum(axis=-1, keepdims=True)
        h = jnp.einsum('td,edf->etf', xt, W1) + b1[:, None, :]
        h = _layernorm(jax.nn.relu(h), g1, be1)
        y = jnp.einsum('etf,efd->etd', h, W2) + b2[:, None, :]
        y = _layernorm(jax.nn.relu(y), g2, be2)
        gate = (jax.nn.one_hot(idx, E, dtype=x.dtype) * probs[..., None]).sum(axis=1)
        out = jnp.einsum('te,etd->td', gate, y)
        return out.reshape(B, S, D)

    def _L1_attn_ref(x, Wd_q_w, Wd_q_b, Wu_q_w, Wu_q_b, Wq_r_w, Wq_r_b, Wk_r_w, Wk_r_b, Wd_kv_w, Wd_kv_b, Wu_k_w, Wu_k_b, Wu_v_w, Wu_v_b, Wo_w, Wo_b):
        import jax, jax.numpy as jnp
        import numpy as np
        NUM_HEAD = 16
        D_Q = 64
        D_KV = 64
        ROPE_BASE = 10000.0

        def _cos_sin(seq_len, dim):
            pos = jnp.arange(seq_len, dtype=jnp.float32)[:, None]
            ids = jnp.arange(dim // 2, dtype=jnp.float32)
            theta = ROPE_BASE ** (-2.0 * ids) / (dim // 2)
            r = pos * theta[None, :]
            return (jnp.cos(r), jnp.sin(r))

        def _rope(x, cos, sin):
            b, s, d = x.shape
            xv = x.reshape(b, s, d // 2, 2)
            x0, x1 = (xv[..., 0], xv[..., 1])
            out = jnp.stack([x0 * cos - x1 * sin, x1 * cos + x0 * sin], axis=-1)
            return out.reshape(b, s, d)
        b, s, d_model = x.shape
        h = NUM_HEAD
        hd = d_model // h
        scale = jnp.sqrt(jnp.float32(h + D_KV + D_Q))

        def heads(t):
            return t.reshape(b, s, h, hd).transpose(0, 2, 1, 3)
        cos, sin = _cos_sin(s, d_model)
        ct_q = x @ Wd_q_w + Wd_q_b
        qt_c = heads(ct_q @ Wu_q_w + Wu_q_b)
        qt_r = heads(_rope(ct_q @ Wq_r_w + Wq_r_b, cos, sin))
        query = qt_c + qt_r
        ct_kv = x @ Wd_kv_w + Wd_kv_b
        kt_c = heads(ct_kv @ Wu_k_w + Wu_k_b)
        kt_r = heads(_rope(x @ Wk_r_w + Wk_r_b, cos, sin))
        key = kt_c + kt_r
        value = heads(ct_kv @ Wu_v_w + Wu_v_b)
        attn = jnp.einsum('bhqd,bhkd->bhqk', query, key) / scale
        attn = jax.nn.softmax(attn, axis=-1)
        out = jnp.einsum('bhqk,bhkd->bhqd', attn, value)
        out = out.transpose(0, 2, 1, 3).reshape(b, s, d_model)
        return out @ Wo_w + Wo_b

    def _L1_ffn_ref(x, gate_w, experts_gate_up, experts_down, shared_gate_w, shared_up_w, shared_down_w, shared_expert_gate_w):
        import jax, jax.numpy as jnp
        import numpy as np
        HIDDEN_SIZE = 128
        NUM_EXPERTS = 8
        MOE_INTERMEDIATE_SIZE = 176
        NUM_EXPERTS_PER_TOK = 2
        SHARED_EXPERT_INTERMEDIATE_SIZE = 352
        B, T = (2, 128)
        W_SCALE = 0.02
        Bx, Tx, H = x.shape
        E = gate_w.shape[0]
        I = experts_down.shape[2]
        x_flat = x.reshape(Bx * Tx, H)
        logits = x_flat @ gate_w.T
        scores = jax.nn.softmax(logits, axis=-1)
        _, topk_ids = jax.lax.top_k(scores, NUM_EXPERTS_PER_TOK)
        in_topk = jax.nn.one_hot(topk_ids, E, dtype=x.dtype).sum(axis=1)
        w = scores * in_topk
        gu = jnp.einsum('nh,eih->nei', x_flat, experts_gate_up)
        g, u = (gu[..., :I], gu[..., I:])
        h = jax.nn.silu(g) * u
        expert_out = jnp.einsum('nei,ehi->neh', h, experts_down)
        out = jnp.einsum('neh,ne->nh', expert_out, w)
        shared = jax.nn.silu(x_flat @ shared_gate_w.T) * (x_flat @ shared_up_w.T) @ shared_down_w.T
        shared_weight = jax.nn.sigmoid(x_flat @ shared_expert_gate_w.T)
        out = out + shared_weight * shared
        return out.reshape(Bx, Tx, H)
    x = L0_attn_x
    x = x + 0.5 * _L0_ffn_ref(_layernorm(x, axis=-1), L0_ffn_Wr, L0_ffn_br, L0_ffn_W1, L0_ffn_b1, L0_ffn_g1, L0_ffn_be1, L0_ffn_W2, L0_ffn_b2, L0_ffn_g2, L0_ffn_be2)
    x = x + _L0_attn_ref(_layernorm(x, axis=-1), L0_attn_ln1_w, L0_attn_ln1_b, L0_attn_Wqk, L0_attn_bqk, L0_attn_Wv, L0_attn_bv, L0_attn_Wg, L0_attn_bg, L0_attn_Wo, L0_attn_bo, L0_attn_ln2_w, L0_attn_ln2_b, L0_attn_gamma, L0_attn_beta, L0_attn_pos_emb)
    x = x + 0.5 * _L0_ffn_ref(_layernorm(x, axis=-1), L0_ffn_Wr, L0_ffn_br, L0_ffn_W1, L0_ffn_b1, L0_ffn_g1, L0_ffn_be1, L0_ffn_W2, L0_ffn_b2, L0_ffn_g2, L0_ffn_be2)
    x = x + 0.5 * _L1_ffn_ref(_layernorm(x, axis=-1), L1_ffn_gate_w, L1_ffn_experts_gate_up, L1_ffn_experts_down, L1_ffn_shared_gate_w, L1_ffn_shared_up_w, L1_ffn_shared_down_w, L1_ffn_shared_expert_gate_w)
    x = x + _L1_attn_ref(_layernorm(x, axis=-1), L1_attn_Wd_q_w, L1_attn_Wd_q_b, L1_attn_Wu_q_w, L1_attn_Wu_q_b, L1_attn_Wq_r_w, L1_attn_Wq_r_b, L1_attn_Wk_r_w, L1_attn_Wk_r_b, L1_attn_Wd_kv_w, L1_attn_Wd_kv_b, L1_attn_Wu_k_w, L1_attn_Wu_k_b, L1_attn_Wu_v_w, L1_attn_Wu_v_b, L1_attn_Wo_w, L1_attn_Wo_b)
    x = x + 0.5 * _L1_ffn_ref(_layernorm(x, axis=-1), L1_ffn_gate_w, L1_ffn_experts_gate_up, L1_ffn_experts_down, L1_ffn_shared_gate_w, L1_ffn_shared_up_w, L1_ffn_shared_down_w, L1_ffn_shared_expert_gate_w)
    return x

_drawn_inputs = setup_inputs


def setup_inputs(seed=0):
    import zlib

    import numpy as np

    out = dict(_drawn_inputs(seed))
    spreads = {'L0_attn_ln1_w': (1.0, 0.2),
     'L0_attn_ln1_b': (0.0, 0.1),
     'L0_attn_bqk': (0.0, 0.8),
     'L0_attn_bv': (0.0, 0.1),
     'L0_attn_bg': (0.0, 0.1),
     'L0_attn_bo': (0.0, 0.1),
     'L0_attn_ln2_w': (1.0, 0.2),
     'L0_attn_ln2_b': (0.0, 0.1),
     'L0_attn_beta': (0.0, 0.8),
     'L0_ffn_br': (0.0, 0.1),
     'L0_ffn_b1': (0.0, 0.1),
     'L0_ffn_g1': (1.0, 0.2),
     'L0_ffn_be1': (0.0, 0.1),
     'L0_ffn_b2': (0.0, 0.1),
     'L0_ffn_g2': (1.0, 0.2),
     'L0_ffn_be2': (0.0, 0.1),
     'L1_attn_Wd_q_b': (0.0, 0.8),
     'L1_attn_Wu_q_b': (0.0, 0.8),
     'L1_attn_Wq_r_b': (0.0, 0.8),
     'L1_attn_Wk_r_b': (0.0, 0.8),
     'L1_attn_Wd_kv_b': (0.0, 0.8),
     'L1_attn_Wu_k_b': (0.0, 0.8),
     'L1_attn_Wu_v_b': (0.0, 0.589),
     'L1_attn_Wo_b': (0.0, 0.1)}
    factors = {'L0_attn_Wqk': 8.0,
     'L0_attn_gamma': 8.0,
     'L1_attn_Wd_q_w': 8.0,
     'L1_attn_Wu_q_w': 8.0,
     'L1_attn_Wq_r_w': 8.0,
     'L1_attn_Wk_r_w': 8.0,
     'L1_attn_Wd_kv_w': 8.0,
     'L1_attn_Wu_k_w': 8.0,
     'L1_attn_Wu_v_w': 8.0,
     'L1_attn_Wo_w': 3.671,
     'L1_ffn_gate_w': 8.0,
     'L1_ffn_experts_gate_up': 8.0,
     'L1_ffn_experts_down': 8.0,
     'L1_ffn_shared_gate_w': 8.0,
     'L1_ffn_shared_up_w': 8.0,
     'L1_ffn_shared_down_w': 8.0,
     'L1_ffn_shared_expert_gate_w': 8.0}
    for name, (base, spread) in spreads.items():
        noise = np.random.default_rng([zlib.crc32(name.encode()), seed]).standard_normal(out[name].shape)
        drawn = base * np.exp(spread * noise) if base else spread * noise
        out[name] = jnp.asarray(drawn.astype(out[name].dtype))
    for name, factor in factors.items():
        out[name] = (out[name] * factor).astype(out[name].dtype)
    return out
```

```python
from collections import namedtuple
from contextlib import ExitStack

import numpy as np

import concourse.bass as bass
from concourse import mybir

F32 = mybir.dt.float32
F32R = mybir.dt.float32r
U32 = mybir.dt.uint32
ALU = mybir.AluOpType
ACT = mybir.ActivationFunctionType
AX = mybir.AxisListType

P = 128
B, S, D = 16, 256, 128
NT = B * S // P
TG = 4
NG = NT // TG
W = TG * P
E = 8
F = 512
FC = F // P
EPS = 1e-5
NCONST = 4


def f32(ap):
    return ap.bitcast(F32)


class Tally:

    def __init__(self, sem):
        self.sem, self.base = sem, 0

    def at(self, n):
        return n + self.base


def begin(eng, p, phase):
    for uses in USES.values():
        for n in uses:
            p.tally[n].base = sum(USES[k].get(n, 0) for k in p.phases[:phase])
    if phase:
        eng.wait_ge(p.phase_end.sem, ENGINES * phase)


def end(eng, p):
    eng.drain().then_inc(p.phase_end.sem, 1)


class Space:

    def __init__(self, tensor, at=0):
        self.tensor, self.at = tensor, at

    def take(self, parts, *shape):
        n = int(np.prod(shape))
        ap = self.tensor[0:parts, self.at:self.at + n]
        self.at += n
        assert self.at <= self.tensor.shape[1]
        names = "abcd"[:len(shape)]
        if len(shape) > 1:
            ap = ap.rearrange(f"p ({' '.join(names)}) -> p {' '.join(names)}", **dict(zip(names, shape)))
        return ap


def tiles(p, g):
    return p.X[:, bass.ds(g * TG, TG), :]


def flat(ap):
    return ap.rearrange("p a b -> p (a b)")


def per_tile(ap):
    return ap.unsqueeze(2).to_broadcast([P, TG, D])


def ln_stats(dve, p, g, n=TG):
    dve.wait_ge(p.ln_free.sem, p.ln_free.at(g))
    for j in range(n):
        dve.bn_stats(p.ln_st[:, j, :], p.X[:, g * n + j, :]).then_inc(p.ln_stat.sem, 1)
    dve.wait_ge(p.ln_stat.sem, p.ln_stat.at(2 * n * g + n))
    dve.sem_inc(p.dve_passed.sem, 1)
    for j in range(n):
        dve.bn_aggr(p.ln_mv[:, j, :], p.ln_st[:, j, :]).then_inc(p.ln_stat.sem, 1)


def ln_scale(pool, p, g, n=TG, twice=False):
    per = 6 if twice else 2
    pool.wait_ge(p.ln_stat.sem, p.ln_stat.at(2 * n * (g + 1)))
    r, ve, var = p.ln_r[:, 0:n], p.ln_ve[:, 0:n], p.ln_mv[:, 0:n, 1]
    pool.tensor_tensor(ve, var, p.eps8[:, 0:n], ALU.add).then_inc(p.ln_rs.sem, 1)
    pool.wait_ge(p.ln_rs.sem, p.ln_rs.at(per * g + 1))
    pool.tensor_tensor(r, ve, p.neg_half[:, 0:n], ALU.pow).then_inc(p.ln_rs.sem, 1)
    if twice:
        pool.wait_ge(p.ln_rs.sem, p.ln_rs.at(per * g + 2))
        pool.tensor_tensor(ve, r, r, ALU.mult).then_inc(p.ln_rs.sem, 1)
        pool.wait_ge(p.ln_rs.sem, p.ln_rs.at(per * g + 3))
        pool.tensor_tensor(ve, ve, var, ALU.mult).then_inc(p.ln_rs.sem, 1)
        pool.wait_ge(p.ln_rs.sem, p.ln_rs.at(per * g + 4))
        pool.tensor_tensor(ve, ve, p.eps8[:, 0:n], ALU.add).then_inc(p.ln_rs.sem, 1)
        pool.wait_ge(p.ln_rs.sem, p.ln_rs.at(per * g + 5))
        pool.tensor_tensor(ve, ve, p.neg_half[:, 0:n], ALU.pow).then_inc(p.ln_rs.sem, 1)


def ln_apply(dve, p, g, xn, width, n=TG, twice=False):
    dve.wait_ge(p.ln_rs.sem, p.ln_rs.at((6 if twice else 2) * (g + 1)))
    dve.wait_ge(p.xt.sem, p.xt.at(g))
    if twice:
        dve.tensor_tensor(p.ln_r2[:, 0:n], p.ln_r[:, 0:n], p.ln_ve[:, 0:n], ALU.mult).then_inc(p.ln_both.sem, 1)
        dve.wait_ge(p.ln_both.sem, p.ln_both.at(g + 1))
    for j in range(n):
        r = p.ln_r2 if twice else p.ln_r
        ins = dve.tensor_scalar(xn[:, j, 0:width], p.X[:, g * n + j, 0:width], p.ln_mv[:, j, 0:1],
                                r[:, j:j + 1], ALU.subtract, ALU.mult)
    ins.then_inc(p.ln_free.sem, 1)


def x_transpose(pe, p, g, xn, bank, n=TG):
    pe.wait_ge(p.ln_free.sem, p.ln_free.at(g + 1))
    for j in range(n):
        ins = pe.transpose(bank[:, j * P:(j + 1) * P], xn[:, j, :], p.ident[:])
    ins.then_inc(p.xt.sem, 1)


def x_high(act, p, g, par, bank):
    act.wait_ge(p.xt.sem, p.xt.at(g + 1))
    act.activation(p.xh[:, par, :], bank[:], ACT.Copy).then_inc(p.xhd.sem, 1)


def x_low(dve, p, g, par, bank):
    dve.wait_ge(p.xhd.sem, p.xhd.at(g + 1))
    dve.tensor_tensor(p.xl[:, par, :], bank[:], f32(p.xh[:, par, :]), ALU.subtract).then_inc(p.xld.sem, 1)


NL = 10


def router_logits(pe, p, g, par, bank, wh, wl, n):
    pe.wait_ge(p.xld.sem, p.xld.at(g + 1))
    for j in range(TG):
        c = slice(j * P, (j + 1) * P)
        out = bank[:, j * NL:j * NL + n]
        pe.matmul(out, p.xh[:, par, c], wh, start=True, stop=False)
        pe.matmul(out, p.xh[:, par, c], wl, start=False, stop=False)
        ins = pe.matmul(out, p.xl[:, par, c], wh, start=False, stop=True)
    ins.then_inc(p.lg.sem, 1)


def router_exp(act, p, g):
    act.wait_ge(p.rt1.sem, p.rt1.at(10 * g + 6))
    act.activation(p.rt_e[:], p.rt_d[:], ACT.Exp).then_inc(p.rte.sem, 1)


def router_top(dve, p, g, bank, n):
    dve.wait_ge(p.lg.sem, p.lg.at(g + 1))
    dve.wait_ge(p.rt2.sem, p.rt2.at(7 * g))
    lg = p.rt_l
    dve.tensor_copy(lg[:, :, 0:n], bank[:, 0:TG * NL].rearrange("p (j n) -> p j n", n=NL)[:, :, 0:n])\
       .then_inc(p.rt1.sem, 1)
    dve.wait_ge(p.rt1.sem, p.rt1.at(10 * g + 1))
    dve.sem_inc(p.dve_passed.sem, 1)
    for j in range(TG):
        dve.max(p.rt_m[:, j, :], lg[:, j, 0:E]).then_inc(p.rt1.sem, 1)
    dve.wait_ge(p.rt1.sem, p.rt1.at(10 * g + 5))
    dve.tensor_tensor(p.rt_d[:], lg[:, :, 0:E], p.rt_m[:, :, 0:1].to_broadcast([P, TG, E]), ALU.subtract)\
       .then_inc(p.rt1.sem, 1)
    for j in range(TG):
        dve.max_index(p.rt_i[:, j, :], p.rt_m[:, j, :], lg[:, j, 0:E]).then_inc(p.rt1.sem, 1)
    dve.wait_ge(p.rt1.sem, p.rt1.at(10 * g + 10))
    for k, sel in ((0, p.rt_s0), (1, p.rt_s1)):
        dve.tensor_tensor(sel[:], p.iota8[:].unsqueeze(1).to_broadcast([P, TG, E]),
                          p.rt_i[:, :, k:k + 1].to_broadcast([P, TG, E]), ALU.is_equal).then_inc(p.rt2.sem, 1)
    dve.wait_ge(p.rt2.sem, p.rt2.at(7 * g + 2))
    dve.tensor_tensor(p.rt_s0[:], p.rt_s0[:], p.rt_s1[:], ALU.add).then_inc(p.rt2.sem, 1)


def router_gate(dve, p, g, gate, top_only):
    dve.wait_ge(p.rte.sem, p.rte.at(g + 1))
    dve.wait_ge(p.rt2.sem, p.rt2.at(7 * g + 3))
    dve.tensor_tensor(p.rt_s1[:], p.rt_e[:], p.rt_s0[:], ALU.mult).then_inc(p.rt2.sem, 1)
    dve.wait_ge(p.rt2.sem, p.rt2.at(7 * g + 4))
    dve.tensor_reduce(p.rt_z[:], p.rt_s1[:] if top_only else p.rt_e[:], AX.X, ALU.add).then_inc(p.rt2.sem, 1)
    dve.wait_ge(p.rt2.sem, p.rt2.at(7 * g + 5))
    dve.reciprocal(p.rt_r[:], p.rt_z[:]).then_inc(p.rt2.sem, 1)
    dve.wait_ge(p.rt2.sem, p.rt2.at(7 * g + 6))
    dve.scalar_tensor_tensor(out=gate[:, :, 0:E], in0=p.rt_s1[:], scalar=0.5,
                             in1=p.rt_r[:].unsqueeze(2).to_broadcast([P, TG, E]),
                             op0=ALU.mult, op1=ALU.mult).then_inc(p.rt2.sem, 1)


NA, NB, NC = 8, 13, 4
NR, NGT, NU = 2, 3, 2


def moe_t1(pe, p, par, e, j):
    c = slice(j * P, (j + 1) * P)
    out = p.bk[j % 2][:]
    w = bass.ds(e * F, F)
    pe.matmul(out, p.xh[:, par, c], p.w1h[:, w], start=True, stop=False)
    pe.matmul(out, p.xh[:, par, c], p.w1l[:, w], start=False, stop=False)
    pe.matmul(out, p.xl[:, par, c], p.w1h[:, w], start=False, stop=True).then_inc(p.hid.sem, 1)


def moe_t2(pe, p, k, j, first):
    pe.wait_ge(p.act_r.sem, p.act_r.at(4 * k + j + 1))
    pe.wait_ge(p.act_t.sem, p.act_t.at(4 * k if first and j < 2 else 4 * k + j - 1))
    for c in range(FC):
        ins = pe.transpose(p.bk[2 + j % 2][:, c * P:(c + 1) * P], p.r[:, j, c * P:(c + 1) * P], p.ident[:])
    ins.then_inc(p.hidT.sem, 1)


def moe_t3(pe, p, k, e, par, j):
    pe.wait_ge(p.act_t.sem, p.act_t.at(4 * k + j + 1))
    for c in range(FC):
        ins = pe.matmul(p.bk[4 + par][:, j * P:(j + 1) * P], p.rT[:, j % 2, c * P:(c + 1) * P],
                        p.w2c[:, bass.ds((e * FC + c) * D, D)], start=(c == 0), stop=(c == FC - 1))
    ins.then_inc(p.outl.sem, 1)


def moe_pe_unit(pe, p, u0, e, par, xpar, nxt):
    k = u0 + e
    first = isinstance(e, int) and e == 0
    for j in range(TG):
        moe_t2(pe, p, k, j, first)
        if j == 0 and not first:
            moe_t3(pe, p, k - 1, e - 1, 1 - par, TG - 1)
        if j == 1:
            if isinstance(e, int) and e < 2:
                pe.wait_ge(p.dve_b.sem, p.dve_b.at(NB * u0))
            else:
                pe.wait_ge(p.dve_b.sem, p.dve_b.at(NB * (k - 2) + 4))
        if j >= 1:
            moe_t3(pe, p, k, e, par, j - 1)
        if j < 2:
            moe_t1(pe, p, xpar, e, j + 2)
        elif nxt is not None:
            moe_t1(pe, p, nxt[1], nxt[0], j - 2)


def moe_pe_group(pe, p, g, xpar, last):
    u0 = g * E
    moe_pe_unit(pe, p, u0, 0, 0, xpar, (1, xpar))
    pe.wait_ge(p.rt2.sem, p.rt2.at(7 * g + 7))
    if not last:
        x_transpose(pe, p, g + 1, p.xn, p.bk[6])
    pe.wait_ge(p.fin.sem, p.fin.at(g))
    pe.transpose(p.bk[7][0:TG * E, 0:P], p.gate[:, xpar, :], p.ident[:]).then_inc(p.gtT.sem, 1)
    moe_pe_unit(pe, p, u0, 1, 1, xpar, (2, xpar))
    pe.wait_ge(p.gts.sem, p.gts.at(g + 1))
    for j in range(TG):
        ins = pe.matmul(p.bk[7][:, j * P:(j + 1) * P], p.gT[:], p.be2p[:, j, :], start=True, stop=True)
    ins.then_inc(p.shf.sem, 1)
    with pe.Fori(0, 2) as i:
        moe_pe_unit(pe, p, u0, 2 * i + 2, 0, xpar, (2 * i + 3, xpar))
        moe_pe_unit(pe, p, u0, 2 * i + 3, 1, xpar, (2 * i + 4, xpar))
    moe_pe_unit(pe, p, u0, 6, 0, xpar, (7, xpar))
    if not last:
        router_logits(pe, p, g + 1, 1 - xpar, p.bk[6], p.wrh[:], p.wrl[:], E)
    moe_pe_unit(pe, p, u0, 7, 1, xpar, None if last else (0, 1 - xpar))
    moe_t3(pe, p, u0 + 7, 7, 1, TG - 1)


def moe_pe(pe, p):
    x_transpose(pe, p, 0, p.xn, p.bk[6])
    router_logits(pe, p, 0, 0, p.bk[6], p.wrh[:], p.wrl[:], E)
    for j in range(2):
        moe_t1(pe, p, 0, 0, j)
    with pe.Fori(0, NG // 2 - 1) as i:
        moe_pe_group(pe, p, 2 * i, 0, False)
        moe_pe_group(pe, p, 2 * i + 1, 1, False)
    moe_pe_group(pe, p, NG - 2, 0, False)
    moe_pe_group(pe, p, NG - 1, 1, True)


def moe_relu(act, p, k, j):
    act.wait_ge(p.hid.sem, p.hid.at(4 * k + j + 1))
    act.activation(p.r[:, j, :], p.bk[j % 2][:], ACT.Relu).then_inc(p.act_r.sem, 1)


def moe_act_unit(act, p, k, last=False):
    for j in range(TG):
        act.wait_ge(p.hidT.sem, p.hidT.at(4 * k + j + 1))
        act.activation(p.rT[:, j % 2, :], p.bk[2 + j % 2][:], ACT.Copy).then_inc(p.act_t.sem, 1)
        if j < 2:
            act.wait_ge(p.dve_a.sem, p.dve_a.at(NA * k))
            moe_relu(act, p, k, j + 2)
        elif not last:
            act.wait_ge(p.dve_a.sem, p.dve_a.at(NA * k + j - 1))
            moe_relu(act, p, k + 1, j - 2)


def moe_act_group(act, p, g, xpar, last):
    u0 = g * E
    moe_act_unit(act, p, u0)
    if not last:
        x_high(act, p, g + 1, 1 - xpar, p.bk[6])
    act.wait_ge(p.gtT.sem, p.gtT.at(g + 1))
    act.activation(p.gT[:], p.bk[7][0:TG * E, 0:P], ACT.Copy).then_inc(p.gts.sem, 1)
    with act.Fori(0, 6) as i:
        moe_act_unit(act, p, u0 + 1 + i)
    moe_act_unit(act, p, u0 + 7, last)
    if not last:
        router_exp(act, p, g + 1)


def moe_act(act, p):
    x_high(act, p, 0, 0, p.bk[6])
    router_exp(act, p, 0)
    for j in range(2):
        moe_relu(act, p, 0, j)
    with act.Fori(0, NG // 2 - 1) as i:
        moe_act_group(act, p, 2 * i, 0, False)
        moe_act_group(act, p, 2 * i + 1, 1, False)
    moe_act_group(act, p, NG - 2, 0, False)
    moe_act_group(act, p, NG - 1, 1, True)


def moe_a(dve, p, k, par):
    for j in range(TG):
        dve.wait_ge(p.act_r.sem, p.act_r.at(4 * k + j + 1))
        dve.bn_stats(p.st1[:, par, j, :], p.r[:, j, :]).then_inc(p.dve_a.sem, 1)
    dve.wait_ge(p.dve_a.sem, p.dve_a.at(NA * k + 4))
    dve.sem_inc(p.dve_passed.sem, 1)
    for j in range(TG):
        dve.bn_aggr(p.mv1[:, par, j, :], p.st1[:, par, j, :]).then_inc(p.dve_a.sem, 1)


def moe_b(dve, p, k, e, par):
    dve.wait_ge(p.outl.sem, p.outl.at(4 * k + 4))
    dve.wait_ge(p.pl_r.sem, p.pl_r.at(NR * k + 2))
    y = p.y[:, par]
    c2 = p.c2b[:, bass.ds(e * D, D)]
    for j in range(TG):
        dve.scalar_tensor_tensor(out=y[:, j, :], in0=p.bk[4 + par][:, j * P:(j + 1) * P],
                                 scalar=p.rs1[:, par, j:j + 1], in1=c2, op0=ALU.mult, op1=ALU.add)\
           .then_inc(p.dve_b.sem, 1)
    dve.wait_ge(p.dve_b.sem, p.dve_b.at(NB * k + 4))
    dve.tensor_scalar(flat(y), flat(y), 0.0, None, ALU.max).then_inc(p.dve_b.sem, 1)
    dve.wait_ge(p.dve_b.sem, p.dve_b.at(NB * k + 5))
    for j in range(TG):
        dve.bn_stats(p.st2[:, j, :], y[:, j, :]).then_inc(p.dve_b.sem, 1)
    dve.wait_ge(p.dve_b.sem, p.dve_b.at(NB * k + 9))
    dve.sem_inc(p.dve_passed.sem, 1)
    for j in range(TG):
        dve.bn_aggr(p.mv2[:, par, j, :], p.st2[:, j, :]).then_inc(p.dve_b.sem, 1)


def moe_c(dve, p, k, par):
    dve.wait_ge(p.pl_g.sem, p.pl_g.at(NGT * k + 3))
    y = p.y[:, par]
    for j in range(TG):
        dve.tensor_scalar(y[:, j, :], y[:, j, :], p.mv2[:, par, j, 0:1], p.ga[:, par, j:j + 1],
                          ALU.subtract, ALU.mult).then_inc(p.dve_c.sem, 1)


def moe_dve_group(dve, p, g, xpar, last):
    u0 = g * E
    if not last:
        ln_stats(dve, p, g + 1)
    moe_a(dve, p, u0, 0)
    if not last:
        ln_apply(dve, p, g + 1, p.xn, P - 1)
    moe_a(dve, p, u0 + 1, 1)
    moe_b(dve, p, u0, 0, 0)
    if not last:
        x_low(dve, p, g + 1, 1 - xpar, p.bk[6])
    moe_a(dve, p, u0 + 2, 0)
    moe_b(dve, p, u0 + 1, 1, 1)
    moe_c(dve, p, u0, 0)
    with dve.Fori(0, 2) as i:
        for m in range(2):
            k = u0 + 2 * i + 3 + m
            par = (1 + m) % 2
            moe_a(dve, p, k, par)
            dve.wait_ge(p.pl_u.sem, p.pl_u.at(NU * (k - 3) + 1))
            moe_b(dve, p, k - 1, 2 * i + 2 + m, 1 - par)
            moe_c(dve, p, k - 2, par)
    moe_a(dve, p, u0 + 7, 1)
    dve.wait_ge(p.pl_u.sem, p.pl_u.at(NU * (u0 + 4) + 1))
    moe_b(dve, p, u0 + 6, 6, 0)
    moe_c(dve, p, u0 + 5, 1)
    if not last:
        router_top(dve, p, g + 1, p.bk[6], E)
    dve.wait_ge(p.pl_u.sem, p.pl_u.at(NU * (u0 + 5) + 1))
    moe_b(dve, p, u0 + 7, 7, 1)
    moe_c(dve, p, u0 + 6, 0)
    if not last:
        router_gate(dve, p, g + 1, p.gate4[:, 1 - xpar], True)
    moe_c(dve, p, u0 + 7, 1)
    dve.wait_ge(p.shf.sem, p.shf.at(g + 1))
    x = flat(tiles(p, g))
    dve.tensor_tensor(x, x, p.bk[7][:], ALU.add).then_inc(p.res.sem, 1)
    dve.wait_ge(p.res.sem, p.res.at(g + 1))
    dve.wait_ge(p.pl_u.sem, p.pl_u.at(NU * (u0 + 8)))
    dve.tensor_tensor(x, x, flat(p.acc), ALU.add).then_inc(p.fin.sem, 1)


def moe_dve(dve, p):
    ln_stats(dve, p, 0)
    ln_apply(dve, p, 0, p.xn, P - 1)
    x_low(dve, p, 0, 0, p.bk[6])
    router_top(dve, p, 0, p.bk[6], E)
    router_gate(dve, p, 0, p.gate4[:, 0], True)
    with dve.Fori(0, NG // 2 - 1) as i:
        moe_dve_group(dve, p, 2 * i, 0, False)
        moe_dve_group(dve, p, 2 * i + 1, 1, False)
    moe_dve_group(dve, p, NG - 2, 0, False)
    moe_dve_group(dve, p, NG - 1, 1, True)


def moe_r(pool, p, k, par):
    pool.wait_ge(p.dve_a.sem, p.dve_a.at(NA * k + NA))
    pool.tensor_tensor(p.ve1[:, par, :], p.mv1[:, par, :, 1], p.eps8[:, 0:TG], ALU.add).then_inc(p.pl_r.sem, 1)
    pool.wait_ge(p.pl_r.sem, p.pl_r.at(NR * k + 1))
    pool.tensor_tensor(p.rs1[:, par, :], p.ve1[:, par, :], p.neg_half[:, 0:TG], ALU.pow).then_inc(p.pl_r.sem, 1)


def moe_g(pool, p, k, e, par, xpar):
    pool.wait_ge(p.dve_b.sem, p.dve_b.at(NB * k + NB))
    pool.tensor_tensor(p.ve2[:], p.mv2[:, par, :, 1], p.eps8[:, 0:TG], ALU.add).then_inc(p.pl_g.sem, 1)
    pool.wait_ge(p.pl_g.sem, p.pl_g.at(NGT * k + 1))
    pool.tensor_tensor(p.rs2[:], p.ve2[:], p.neg_half[:, 0:TG], ALU.pow).then_inc(p.pl_g.sem, 1)
    pool.wait_ge(p.pl_g.sem, p.pl_g.at(NGT * k + 2))
    pool.sem_inc(p.pool_passed.sem, 1)
    pool.tensor_tensor(p.ga[:, par, :], p.rs2[:], p.gate_e[:, xpar, bass.ds(e, 1), :].rearrange("p a j -> p (a j)"), ALU.mult)\
        .then_inc(p.pl_g.sem, 1)


def moe_u(pool, p, k, e, par):
    pool.wait_ge(p.dve_c.sem, p.dve_c.at(NC * k + NC))
    g2 = p.g2b[:, bass.ds(e * D, D)].unsqueeze(1).to_broadcast([P, TG, D])
    pool.wait_ge(p.pl_u.sem, p.pl_u.at(NU * k))
    pool.sem_inc(p.pool_passed.sem, 1)
    pool.tensor_tensor(p.gy, p.y[:, par], g2, ALU.mult).then_inc(p.pl_u.sem, 1)
    pool.wait_ge(p.pl_u.sem, p.pl_u.at(NU * k + 1))
    pool.tensor_tensor(p.acc, p.acc, p.gy, ALU.add).then_inc(p.pl_u.sem, 1)


def moe_pool_group(pool, p, g, xpar, last):
    u0 = g * E
    if not last:
        ln_scale(pool, p, g + 1)
    pool.wait_ge(p.rt2.sem, p.rt2.at(7 * g + 7))
    pool.sem_inc(p.pool_passed.sem, 1)
    pool.tensor_copy(p.gate_e[:, xpar], p.gate4[:, xpar].rearrange("p j e -> p e j")).then_inc(p.gcp.sem, 1)
    moe_r(pool, p, u0, 0)
    moe_r(pool, p, u0 + 1, 1)
    pool.wait_ge(p.gcp.sem, p.gcp.at(2 * g + 1))
    moe_g(pool, p, u0, 0, 0, xpar)
    pool.wait_ge(p.fin.sem, p.fin.at(g))
    pool.sem_inc(p.pool_passed.sem, 1)
    pool.memset(p.acc, 0.0).then_inc(p.gcp.sem, 1)
    moe_r(pool, p, u0 + 2, 0)
    moe_g(pool, p, u0 + 1, 1, 1, xpar)
    pool.wait_ge(p.gcp.sem, p.gcp.at(2 * g + 2))
    moe_u(pool, p, u0, 0, 0)
    with pool.Fori(0, 2) as i:
        for m in range(2):
            e = 2 * i + 3 + m
            par = (1 + m) % 2
            moe_r(pool, p, u0 + e, par)
            moe_g(pool, p, u0 + e - 1, e - 1, 1 - par, xpar)
            moe_u(pool, p, u0 + e - 2, e - 2, par)
    moe_r(pool, p, u0 + 7, 1)
    moe_g(pool, p, u0 + 6, 6, 0, xpar)
    moe_u(pool, p, u0 + 5, 5, 1)
    moe_g(pool, p, u0 + 7, 7, 1, xpar)
    moe_u(pool, p, u0 + 6, 6, 0)
    moe_u(pool, p, u0 + 7, 7, 1)


def moe_pool(pool, p):
    ln_scale(pool, p, 0)
    with pool.Fori(0, NG // 2 - 1) as i:
        moe_pool_group(pool, p, 2 * i, 0, False)
        moe_pool_group(pool, p, 2 * i + 1, 1, False)
    moe_pool_group(pool, p, NG - 2, 0, False)
    moe_pool_group(pool, p, NG - 1, 1, True)


def moe_weights_dve(dve, p):
    s = p.wts
    dve.wait_ge(p.dma_w1.sem, p.dma_w1.at(80))
    dve.scalar_tensor_tensor(out=p.sa[:], in0=p.sb_[:], scalar=p.neg_but_last[:, 0:1], in1=p.sa[:],
                             op0=ALU.mult, op1=ALU.add).then_inc(s.sem, 1)
    dve.scalar_tensor_tensor(out=p.wr_f[:], in0=p.wr_last[:], scalar=p.neg_but_last[:, 0:1], in1=p.wr_f[:],
                             op0=ALU.mult, op1=ALU.add).then_inc(s.sem, 1)
    dve.wait_ge(s.sem, s.at(2))
    dve.tensor_copy(p.w1h[:], p.sa[:]).then_inc(s.sem, 1)
    dve.tensor_copy(p.wrh[:], p.wr_f[:]).then_inc(s.sem, 1)
    dve.wait_ge(s.sem, s.at(4))
    dve.tensor_tensor(p.w1l[:], p.sa[:], f32(p.w1h[:]), ALU.subtract).then_inc(s.sem, 1)
    dve.tensor_tensor(p.wrl[:], p.wr_f[:], f32(p.wrh[:]), ALU.subtract).then_inc(s.sem, 1)
    dve.wait_ge(p.dma_w2.sem, p.dma_w2.at(32))
    w2 = p.sc[:].rearrange("p (a d) -> p a d", d=D)
    g1 = p.g1[:].unsqueeze(2).to_broadcast([P, E * FC, D])
    dve.tensor_tensor(p.w2c[:].rearrange("p (a d) -> p a d", d=D), w2, g1, ALU.mult).then_inc(s.sem, 1)
    dve.wait_ge(p.dma_small.sem, p.dma_small.at(p.nsmall))
    dve.wait_ge(s.sem, s.at(6))
    dve.tensor_copy(p.sa[:].rearrange("p (a d) -> p a d", d=D),
                    p.be1[:].unsqueeze(2).to_broadcast([P, E * FC, D])).then_inc(s.sem, 1)
    dve.wait_ge(p.wpe.sem, p.wpe.at(1))
    dve.wait_ge(s.sem, s.at(8))
    for h in range(2):
        for e in range(4):
            w = p.w2c[:].rearrange("p (e c d) -> p e c d", c=FC, d=D)[:, 4 * h + e]
            m = p.bk[h][:, e * D:(e + 1) * D].unsqueeze(1).to_broadcast([P, FC, D])
            dve.tensor_tensor(w, w, m, ALU.subtract).then_inc(s.sem, 1)
        c = slice(h * 4 * D, (h + 1) * 4 * D)
        dve.tensor_tensor(p.c2b[:, c], p.c2b[:, c], p.bk[2 + h][:], ALU.add).then_inc(s.sem, 1)


def moe_weights_pe(pe, p):
    pe.wait_ge(p.wts.sem, p.wts.at(8))
    for e in range(E):
        for c in range(FC):
            a = slice((e * FC + c) * D, (e * FC + c + 1) * D)
            o = slice((e % 4) * D, (e % 4 + 1) * D)
            pe.matmul(p.bk[e // 4][:, o], p.ones_f[:], p.w2c[:, a], start=(c == 0), stop=(c == FC - 1))
    for e in range(E):
        for c in range(FC):
            a = slice((e * FC + c) * D, (e * FC + c + 1) * D)
            o = slice((e % 4) * D, (e % 4 + 1) * D)
            ins = pe.matmul(p.bk[2 + e // 4][:, o], p.sa[:, a], p.sc[:, a], start=(c == 0), stop=(c == FC - 1))
    ins.then_inc(p.wpe.sem, 1)
    pe.wait_ge(p.wts.sem, p.wts.at(18))


I1, SI = 176, 352
ROWS = E * I1 + SI
NCH = -(-ROWS // P)
HRING = 7
E1 = E + 1
PIECES = [(c, e) for c in range(NCH) for e in range(E1)
          if e * I1 < (c + 1) * P and c * P < (e * I1 + I1 if e < E else ROWS)]
FIRST = {e: min(c for c, x in PIECES if x == e) for e in range(E1)}
LAST = {e: max(c for c, x in PIECES if x == e) for e in range(E1)}
DBANK = [4, 5, 7]


def rows_of(c):
    return slice(c * P, min((c + 1) * P, ROWS))


def sw_gu(pe, p, g, c, par):
    n, rows = NCH * g + c, rows_of(c)
    m = rows.stop - rows.start
    for w_h, w_l, bank, done, freed in ((p.wgh, p.wgl, p.bk[c % 2], p.gt_rows, p.silu_d),
                                        (p.wuh, p.wul, p.bk[2 + c % 2], p.up_rows, p.hid_d)):
        if not isinstance(n, int) or n >= 2:
            pe.wait_ge(freed.sem, freed.at(n - 1))
        pe.matmul(bank[0:m, :], w_h[:, rows], p.xh[:, par, :], start=True, stop=False)
        pe.matmul(bank[0:m, :], w_l[:, rows], p.xh[:, par, :], start=False, stop=False)
        pe.matmul(bank[0:m, :], w_h[:, rows], p.xl[:, par, :], start=False, stop=True).then_inc(done.sem, 1)


def sw_down(pe, p, g, c):
    n, m = NCH * g + c, rows_of(c).stop - c * P
    pe.wait_ge(p.hid_d.sem, p.hid_d.at(n + 1))
    for q, (cc, e) in enumerate(PIECES):
        if cc != c:
            continue
        bank = p.bk[DBANK[e % 3]]
        if c == FIRST[e]:
            pe.wait_ge(p.exp_add.sem, p.exp_add.at(TG * (E1 * g + e - 2) if e >= 2 else TG * E1 * g))
        for j in range(TG):
            ins = pe.matmul(bank[:, j * P:(j + 1) * P], p.hT[0:m, c % HRING, j * P:(j + 1) * P],
                            p.wd[0:m, q * D:(q + 1) * D], start=(c == FIRST[e] and j == 0),
                            stop=(c == LAST[e]), skip_group_check=True)
        if c == LAST[e]:
            ins.then_inc(p.exp_d.sem, 1)


def sw_pe_group(pe, p, g, par, last):
    for c in range(2, NCH):
        sw_gu(pe, p, g, c, par)
        sw_down(pe, p, g, c - 2)
        if c == 3 and not last:
            pe.wait_ge(p.rt2.sem, p.rt2.at(7 * g + 7))
            x_transpose(pe, p, g + 1, p.xf, p.bk[6])
        if c == 7 and not last:
            router_logits(pe, p, g + 1, 1 - par, p.bk[6], p.wr1h[:], p.wr1l[:], NL)
    for c in range(2):
        if not last:
            sw_gu(pe, p, g + 1, c, 1 - par)
        sw_down(pe, p, g, NCH - 2 + c)


def sw_pe(pe, p):
    x_transpose(pe, p, 0, p.xf, p.bk[6])
    router_logits(pe, p, 0, 0, p.bk[6], p.wr1h[:], p.wr1l[:], NL)
    for c in range(2):
        sw_gu(pe, p, 0, c, 0)
    with pe.Fori(0, NG // 2 - 1) as i:
        sw_pe_group(pe, p, 2 * i, 0, False)
        sw_pe_group(pe, p, 2 * i + 1, 1, False)
    sw_pe_group(pe, p, NG - 2, 0, False)
    sw_pe_group(pe, p, NG - 1, 1, True)


def sw_silu(act, p, g, c):
    n, m = NCH * g + c, rows_of(c).stop - c * P
    act.wait_ge(p.gt_rows.sem, p.gt_rows.at(n + 1))
    if not isinstance(n, int) or n >= 2:
        act.wait_ge(p.hid_d.sem, p.hid_d.at(n - 1))
    act.activation(p.sg[0:m, c % 2, :], p.bk[c % 2][0:m, :], ACT.Silu).then_inc(p.silu_d.sem, 1)


def router_shared_exp(act, p, g):
    act.activation(p.rt_g[:], p.rt_l[:, :, E], ACT.Exp, scale=-1.0).then_inc(p.rtg.sem, 1)


def sw_act_group(act, p, g, par, last):
    for c in range(2, NCH):
        sw_silu(act, p, g, c)
        if c == 5 and not last:
            x_high(act, p, g + 1, 1 - par, p.bk[6])
        if c == 10 and not last:
            router_exp(act, p, g + 1)
            router_shared_exp(act, p, g + 1)
    if not last:
        for c in range(2):
            sw_silu(act, p, g + 1, c)


def sw_act(act, p):
    x_high(act, p, 0, 0, p.bk[6])
    router_exp(act, p, 0)
    router_shared_exp(act, p, 0)
    for c in range(2):
        sw_silu(act, p, 0, c)
    with act.Fori(0, NG // 2 - 1) as i:
        sw_act_group(act, p, 2 * i, 0, False)
        sw_act_group(act, p, 2 * i + 1, 1, False)
    sw_act_group(act, p, NG - 2, 0, False)
    sw_act_group(act, p, NG - 1, 1, True)


def router_shared_gate(dve, p, g, gate):
    dve.wait_ge(p.rtg.sem, p.rtg.at(g + 1))
    dve.tensor_scalar(p.rt_g[:], p.rt_g[:], 2.0, 2.0, ALU.mult, ALU.add).then_inc(p.rt3.sem, 1)
    dve.wait_ge(p.rt3.sem, p.rt3.at(2 * g + 1))
    dve.reciprocal(gate[:, :, E], p.rt_g[:]).then_inc(p.rt3.sem, 1)


def sw_product(dve, p, g, c):
    n, m = NCH * g + c, rows_of(c).stop - c * P
    dve.wait_ge(p.silu_d.sem, p.silu_d.at(n + 1))
    dve.wait_ge(p.up_rows.sem, p.up_rows.at(n + 1))
    dve.tensor_tensor(p.hT[0:m, c % HRING, :], p.sg[0:m, c % 2, :], p.bk[2 + c % 2][0:m, :], ALU.mult)\
       .then_inc(p.hid_d.sem, 1)


def sw_add(dve, p, g, e, par):
    n = E1 * g + e
    dve.wait_ge(p.exp_d.sem, p.exp_d.at(n + 1))
    dve.wait_ge(p.exp_add.sem, p.exp_add.at(TG * n))
    if e == 0:
        dve.wait_ge(p.rt2.sem, p.rt2.at(7 * g + 7))
        dve.wait_ge(p.rt3.sem, p.rt3.at(2 * g + 2))
    for j in range(TG):
        x = p.X[:, g * TG + j, :]
        dve.scalar_tensor_tensor(out=x, in0=p.bk[DBANK[e % 3]][:, j * P:(j + 1) * P],
                                 scalar=p.gate1[:, par, j, e:e + 1], in1=x, op0=ALU.mult, op1=ALU.add)\
           .then_inc(p.exp_add.sem, 1)


def sw_router(dve, p, g, par):
    router_top(dve, p, g, p.bk[6], NL)
    router_gate(dve, p, g, p.gate1[:, par], False)
    router_shared_gate(dve, p, g, p.gate1[:, par])


def sw_dve_group(dve, p, g, par, last):
    if not last:
        ln_stats(dve, p, g + 1)
    for c in range(2, NCH):
        sw_product(dve, p, g, c)
        if c == 2 and not last:
            ln_apply(dve, p, g + 1, p.xf, P)
        if c == 6 and not last:
            x_low(dve, p, g + 1, 1 - par, p.bk[6])
        if c == 10 and not last:
            sw_router(dve, p, g + 1, 1 - par)
        for e in range(E1):
            if LAST[e] == c - 3:
                sw_add(dve, p, g, e, par)
    for c in range(2):
        if not last:
            sw_product(dve, p, g + 1, c)
        for e in range(E1):
            if LAST[e] == NCH - 3 + c:
                sw_add(dve, p, g, e, par)
    sw_add(dve, p, g, E, par)


def sw_dve(dve, p):
    ln_stats(dve, p, 0)
    ln_apply(dve, p, 0, p.xf, P)
    x_low(dve, p, 0, 0, p.bk[6])
    sw_router(dve, p, 0, 0)
    for c in range(2):
        sw_product(dve, p, 0, c)
    with dve.Fori(0, NG // 2 - 1) as i:
        sw_dve_group(dve, p, 2 * i, 0, False)
        sw_dve_group(dve, p, 2 * i + 1, 1, False)
    sw_dve_group(dve, p, NG - 2, 0, False)
    sw_dve_group(dve, p, NG - 1, 1, True)


def sw_pool(pool, p):
    with pool.Fori(0, NG) as g:
        ln_scale(pool, p, g)


def sw_weights_dve(dve, p):
    dve.wait_ge(p.dma_sw.sem, p.dma_sw.at(48))
    s = p.wsw
    for w, h, l in ((p.sa[:, 0:ROWS], p.wgh, p.wgl), (p.sa[:, ROWS:2 * ROWS], p.wuh, p.wul),
                    (p.wr1_f[:], p.wr1h, p.wr1l)):
        dve.tensor_copy(h[:], w).then_inc(s.sem, 1)
    dve.wait_ge(s.sem, s.at(3))
    for w, h, l in ((p.sa[:, 0:ROWS], p.wgh, p.wgl), (p.sa[:, ROWS:2 * ROWS], p.wuh, p.wul),
                    (p.wr1_f[:], p.wr1h, p.wr1l)):
        dve.tensor_tensor(l[:], w, f32(h[:]), ALU.subtract).then_inc(s.sem, 1)


QK, H, GROUP, MAXREL = 32, 256, 64, 32
NB2 = 2
NQ = 2 * QK


def ga_project_pe(pe, p, b):
    pe.wait_ge(p.ga_xc.sem, p.ga_xc.at(b + 1))
    pe.wait_ge(p.ga_qk.sem, p.ga_qk.at(b))
    pe.matmul(p.bk[0][0:NQ, S:2 * S], p.ga_w[:, 0:NQ], p.ga_xa[:], start=True, stop=True).then_inc(p.ga_qkp.sem, 1)
    pe.wait_ge(p.ga_vg.sem, p.ga_vg.at(NB2 * b))
    for t in range(NB2):
        pe.matmul(p.bk[1 + t][:], p.ga_xa[:, t * P:(t + 1) * P], p.ga_w[:, NQ:], start=True, stop=True)\
          .then_inc(p.ga_vgp.sem, 1)


def ga_swap_pe(pe, p, b):
    pe.wait_ge(p.ga_hd.sem, p.ga_hd.at(2 * b + 2))
    pe.sem_inc(p.pe_passed.sem, 1)
    pe.matmul(p.bk[3][0:NQ, :], p.ga_perm[:], flat(p.ga_h[:]), start=True, stop=True).then_inc(p.ga_sw.sem, 1)


def ga_x_pe(pe, p, b):
    pe.wait_ge(p.ga_xc.sem, p.ga_xc.at(b))
    x_transpose(pe, p, b, p.xn, p.bk[0], NB2)


def ga_pe_element(pe, p, b, par, last):
    rp, vg = p.ga_r[:, par], p.ga_v[:, par]
    pe.wait_ge(p.ga_rp.sem, p.ga_rp.at(3 * b + 3))
    pe.wait_ge(p.ga_at.sem, p.ga_at.at(2 * b))
    for t in range(NB2):
        c = slice(t * P, (t + 1) * P)
        ins = pe.matmul(p.bk[5][:, c], rp[0:QK, 1, c], rp[0:QK, 0, c], start=True, stop=True)
    ins.then_inc(p.ga_scp.sem, 1)
    for t in range(NB2):
        ins = pe.transpose(p.bk[6][:, t * NQ:(t + 1) * NQ], rp[:, 1, t * P:(t + 1) * P], p.ident[0:NQ, 0:NQ])
    ins.then_inc(p.ga_lkp.sem, 1)
    if not last:
        ga_x_pe(pe, p, b + 1)
    pe.wait_ge(p.ga_lk.sem, p.ga_lk.at(b + 1))
    pe.wait_ge(p.ga_y.sem, p.ga_y.at(5 * b))
    pe.wait_ge(p.ga_vg.sem, p.ga_vg.at(NB2 * b + NB2))
    for t in range(NB2):
        ins = pe.matmul(p.bk[4][0:NQ, 0:H], p.ga_k[:, t * NQ:(t + 1) * NQ], vg[:, t, 0:H],
                        start=(t == 0), stop=(t == NB2 - 1))
    ins.then_inc(p.ga_kvp.sem, 1)
    if not last:
        ga_project_pe(pe, p, b + 1)
    pe.wait_ge(p.ga_at.sem, p.ga_at.at(2 * b + 2))
    pe.wait_ge(p.ga_kv.sem, p.ga_kv.at(b + 1))
    pe.wait_ge(p.ga_o.sem, p.ga_o.at(b))
    for t in range(NB2):
        o, c = p.bk[6][:, t * H:(t + 1) * H], slice(t * P, (t + 1) * P)
        pe.matmul(o, p.ga_a[:, t, :], vg[:, t, 0:H], start=True, stop=False)
        ins = pe.matmul(o, rp[QK:NQ, 0, c], p.ga_s[QK:NQ, :], start=False, stop=True)
    ins.then_inc(p.ga_op.sem, 1)
    if not last:
        ga_swap_pe(pe, p, b + 1)
    pe.wait_ge(p.ga_o.sem, p.ga_o.at(b + 1))
    pe.wait_ge(p.ga_ot.sem, p.ga_ot.at(b))
    for q in range(NB2 * 2):
        ins = pe.transpose(p.bk[7][:, q * P:(q + 1) * P], p.ga_g[:, q // 2, (q % 2) * P:(q % 2 + 1) * P], p.ident[:])
    ins.then_inc(p.ga_otp.sem, 1)
    pe.wait_ge(p.ga_ot.sem, p.ga_ot.at(b + 1))
    for t in range(NB2):
        for c in range(2):
            q = t * 2 + c
            ins = pe.matmul(p.bk[4][:, P + t * P:P + (t + 1) * P], p.ga_t[:, q * P:(q + 1) * P],
                            p.ga_wo[:, c * P:(c + 1) * P], start=(c == 0), stop=(c == 1))
    ins.then_inc(p.ga_wop.sem, 1)


def ga_pe(pe, p):
    ga_x_pe(pe, p, 0)
    ga_project_pe(pe, p, 0)
    ga_swap_pe(pe, p, 0)
    with pe.Fori(0, B // 2 - 1) as i:
        ga_pe_element(pe, p, 2 * i, 0, False)
        ga_pe_element(pe, p, 2 * i + 1, 1, False)
    ga_pe_element(pe, p, B - 2, 0, False)
    ga_pe_element(pe, p, B - 1, 1, True)


def ga_x_act(act, p, b):
    act.wait_ge(p.xt.sem, p.xt.at(b + 1))
    act.wait_ge(p.ga_vgp.sem, p.ga_vgp.at(NB2 * b))
    act.activation(p.ga_xa[:], p.bk[0][:, 0:S], ACT.Copy).then_inc(p.ga_xc.sem, 1)


def ga_silu_act(act, p, b, par):
    act.wait_ge(p.ga_qkp.sem, p.ga_qkp.at(b + 1))
    act.wait_ge(p.ga_hd.sem, p.ga_hd.at(2 * b))
    act.activation(p.ga_q[:], p.bk[0][0:NQ, S:2 * S], ACT.Silu).then_inc(p.ga_qk.sem, 1)
    if not isinstance(b, int) or b >= 1:
        act.wait_ge(p.ga_o.sem, p.ga_o.at(b - 1))
    for t in range(NB2):
        act.wait_ge(p.ga_vgp.sem, p.ga_vgp.at(NB2 * b + t + 1))
        act.activation(p.ga_v[:, par, t, :], p.bk[1 + t][:], ACT.Silu).then_inc(p.ga_vg.sem, 1)


def ga_act_element(act, p, b, par, last):
    act.wait_ge(p.ga_lkp.sem, p.ga_lkp.at(b + 1))
    act.activation(p.ga_k[:], p.bk[6][:, 0:P], ACT.Copy).then_inc(p.ga_lk.sem, 1)
    if not last:
        ga_x_act(act, p, b + 1)
    act.wait_ge(p.ga_kvp.sem, p.ga_kvp.at(b + 1))
    act.activation(p.ga_s[:], p.bk[4][0:NQ, 0:H], ACT.Copy, scale=1.0 / S).then_inc(p.ga_kv.sem, 1)
    if not last:
        ga_silu_act(act, p, b + 1, 1 - par)
    act.wait_ge(p.ga_otp.sem, p.ga_otp.at(b + 1))
    act.activation(p.ga_t[:], p.bk[7][:], ACT.Copy).then_inc(p.ga_ot.sem, 1)


def ga_act(act, p):
    ga_x_act(act, p, 0)
    ga_silu_act(act, p, 0, 0)
    with act.Fori(0, B // 2 - 1) as i:
        ga_act_element(act, p, 2 * i, 0, False)
        ga_act_element(act, p, 2 * i + 1, 1, False)
    ga_act_element(act, p, B - 2, 0, False)
    ga_act_element(act, p, B - 1, 1, True)


def ga_heads_dve(dve, p, b):
    dve.wait_ge(p.ga_qk.sem, p.ga_qk.at(b + 1))
    dve.wait_ge(p.ga_sw.sem, p.ga_sw.at(b))
    for n in range(2):
        dve.tensor_scalar(p.ga_h[:, n, :], p.ga_q[:], p.ga_gb[:, 2 * n:2 * n + 1], p.ga_gb[:, 2 * n + 1:2 * n + 2],
                          ALU.mult, ALU.add).then_inc(p.ga_hd.sem, 1)


def ga_rope_dve(dve, p, b, par):
    def table(t):
        return t[:].unsqueeze(1).to_broadcast([NQ, 2, S])
    dve.wait_ge(p.ga_hd.sem, p.ga_hd.at(2 * b + 2))
    dve.tensor_tensor(p.ga_r1[:], p.ga_h[:], table(p.ga_cos), ALU.mult).then_inc(p.ga_rp.sem, 1)
    dve.wait_ge(p.ga_sw.sem, p.ga_sw.at(b + 1))
    dve.tensor_tensor(p.ga_r2[:], p.bk[3][0:NQ, :].rearrange("p (a s) -> p a s", a=2), table(p.ga_sin), ALU.mult)\
       .then_inc(p.ga_rp.sem, 1)
    dve.wait_ge(p.ga_rp.sem, p.ga_rp.at(3 * b + 2))
    dve.tensor_tensor(p.ga_r[:, par], p.ga_r1[:], p.ga_r2[:], ALU.add).then_inc(p.ga_rp.sem, 1)


def ga_dve_element(dve, p, b, par, last, more):
    if not last:
        ln_apply(dve, p, b + 1, p.xn, P - 1, NB2, True)
    dve.wait_ge(p.ga_scp.sem, p.ga_scp.at(b + 1))
    dve.scalar_tensor_tensor(out=p.ga_a1[:], in0=p.bk[5][:, 0:S].rearrange("p (t k) -> p t k", t=NB2),
                             scalar=1.0 / GROUP, in1=p.ga_bias[:].unsqueeze(1).to_broadcast([P, NB2, P]),
                             op0=ALU.mult, op1=ALU.add).then_inc(p.ga_at.sem, 1)
    dve.wait_ge(p.ga_at.sem, p.ga_at.at(2 * b + 1))
    dve.scalar_tensor_tensor(out=p.ga_a[:], in0=p.ga_a1[:], scalar=0.0, in1=p.ga_a1[:],
                             op0=ALU.max, op1=ALU.mult).then_inc(p.ga_at.sem, 1)
    if not last:
        ga_heads_dve(dve, p, b + 1)
    dve.wait_ge(p.ga_op.sem, p.ga_op.at(b + 1))
    dve.wait_ge(p.ga_otp.sem, p.ga_otp.at(b))
    dve.tensor_tensor(p.ga_g[:], p.bk[6][:].rearrange("p (t h) -> p t h", t=NB2), p.ga_v[:, par, :, H:], ALU.mult)\
       .then_inc(p.ga_o.sem, 1)
    if not last:
        ga_rope_dve(dve, p, b + 1, 1 - par)
    dve.wait_ge(p.ga_wop.sem, p.ga_wop.at(b + 1))
    dve.wait_ge(p.ga_px.sem, p.ga_px.at(3 * b))
    dve.tensor_tensor(p.ga_yy[:], p.bk[4][:, P:3 * P].rearrange("p (t d) -> p t d", t=NB2),
                      p.ga_bo[:].unsqueeze(1).to_broadcast([P, NB2, D]), ALU.add).then_inc(p.ga_y.sem, 1)
    dve.wait_ge(p.ga_y.sem, p.ga_y.at(5 * b + 1))
    for t in range(NB2):
        dve.bn_stats(p.ga_st[:, t, :], p.ga_yy[:, t, :]).then_inc(p.ga_y.sem, 1)
    dve.wait_ge(p.ga_y.sem, p.ga_y.at(5 * b + 3))
    dve.sem_inc(p.dve_passed.sem, 1)
    for t in range(NB2):
        dve.bn_aggr(p.ga_mv[:, t, :], p.ga_st[:, t, :]).then_inc(p.ga_y.sem, 1)
    if more:
        ln_stats(dve, p, b + 2, NB2)
    dve.wait_ge(p.ga_rs.sem, p.ga_rs.at(2 * b + 2))
    for t in range(NB2):
        ins = dve.tensor_scalar(p.ga_yy[:, t, :], p.ga_yy[:, t, :], p.ga_mv[:, t, 0:1], p.ga_sc[:, t:t + 1],
                                ALU.subtract, ALU.mult)
    ins.then_inc(p.ga_yn.sem, 1)


def ga_dve(dve, p):
    ln_stats(dve, p, 0, NB2)
    ln_apply(dve, p, 0, p.xn, P - 1, NB2, True)
    ln_stats(dve, p, 1, NB2)
    ga_heads_dve(dve, p, 0)
    ga_rope_dve(dve, p, 0, 0)
    with dve.Fori(0, B // 2 - 1) as i:
        ga_dve_element(dve, p, 2 * i, 0, False, True)
        ga_dve_element(dve, p, 2 * i + 1, 1, False, True)
    ga_dve_element(dve, p, B - 2, 0, False, False)
    ga_dve_element(dve, p, B - 1, 1, True, False)


def ga_pool_element(pool, p, b, more):
    pool.wait_ge(p.ga_y.sem, p.ga_y.at(5 * b + 5))
    pool.tensor_tensor(p.ga_ve[:], p.ga_mv[:, :, 1], p.eps8[:, 0:NB2], ALU.add).then_inc(p.ga_rs.sem, 1)
    pool.wait_ge(p.ga_rs.sem, p.ga_rs.at(2 * b + 1))
    pool.tensor_tensor(p.ga_sc[:], p.ga_ve[:], p.neg_half[:, 0:NB2], ALU.pow).then_inc(p.ga_rs.sem, 1)
    if more:
        ln_scale(pool, p, b + 2, NB2, True)
    x = p.X[:, bass.ds(b * NB2, NB2), :]
    pool.wait_ge(p.ga_yn.sem, p.ga_yn.at(b + 1))
    pool.tensor_tensor(p.ga_z[:], p.ga_yy[:], p.ga_w2[:].unsqueeze(1).to_broadcast([P, NB2, D]), ALU.mult)\
        .then_inc(p.ga_px.sem, 1)
    pool.tensor_tensor(x, x, p.ga_b2[:].unsqueeze(1).to_broadcast([P, NB2, D]), ALU.add).then_inc(p.ga_px.sem, 1)
    pool.wait_ge(p.ga_px.sem, p.ga_px.at(3 * b + 2))
    pool.sem_inc(p.pool_passed.sem, 1)
    pool.tensor_tensor(x, x, p.ga_z[:], ALU.add).then_inc(p.ga_px.sem, 1)


def ga_pool(pool, p):
    ln_scale(pool, p, 0, NB2, True)
    ln_scale(pool, p, 1, NB2, True)
    with pool.Fori(0, B - 2) as b:
        ga_pool_element(pool, p, b, True)
    ga_pool_element(pool, p, B - 2, False)
    ga_pool_element(pool, p, B - 1, False)


def ga_bias_pool(pool, p):
    pool.wait_ge(p.dma_ga.sem, p.dma_ga.at(p.nga))
    for d in range(MAXREL + 1):
        pool.wait_ge(p.gab.sem, p.gab.at(2 * d))
        pool.tensor_scalar(p.ga_bt[:], p.ga_dist[:], float(d), p.ga_pos[:, d:d + 1], ALU.is_equal, ALU.mult)\
            .then_inc(p.gab.sem, 1)
        pool.wait_ge(p.gab.sem, p.gab.at(2 * d + 1))
        pool.tensor_tensor(p.ga_bias[:], p.ga_bias[:], p.ga_bt[:], ALU.add).then_inc(p.gab.sem, 1)


def ga_weights_pe(pe, p):
    pe.wait_ge(p.dma_ga.sem, p.dma_ga.at(p.nga))
    for n, c in enumerate((slice(0, NQ), slice(NQ, NQ + 2 * H))):
        out = p.bk[n][:, 0:c.stop - c.start]
        pe.matmul(out, p.ga_ln_b[:], p.ga_w[:, c], start=True, stop=False)
        ins = pe.matmul(out, p.e_last[:], p.ga_brow[:, c], start=False, stop=True)
    ins.then_inc(p.gaw.sem, 1)
    pe.wait_ge(p.gaw.sem, p.gaw.at(6))


def ga_weights_dve(dve, p):
    dve.wait_ge(p.dma_ga.sem, p.dma_ga.at(p.nga))
    dve.wait_ge(p.gaw.sem, p.gaw.at(1))
    dve.tensor_scalar(p.ga_w[:], p.ga_w[:], p.ga_ln_w[:, 0:1], None, ALU.mult).then_inc(p.gaw.sem, 1)
    dve.tensor_scalar(p.ga_last[:], p.ga_last[:], p.ga_ln_w[:, 1:2], None, ALU.mult).then_inc(p.gaw.sem, 1)
    dve.wait_ge(p.gaw.sem, p.gaw.at(3))
    dve.tensor_tensor(p.ga_w[:], p.ga_w[:], p.ga_last[:], ALU.subtract).then_inc(p.gaw.sem, 1)
    dve.wait_ge(p.gaw.sem, p.gaw.at(4))
    dve.tensor_tensor(p.ga_w[:, 0:NQ], p.ga_w[:, 0:NQ], p.bk[0][:, 0:NQ], ALU.add).then_inc(p.gaw.sem, 1)
    dve.tensor_tensor(p.ga_w[:, NQ:], p.ga_w[:, NQ:], p.bk[1][:], ALU.add).then_inc(p.gaw.sem, 1)


NH, HD = 16, 8
HR = 32
HQ = P // HR
NHQ = NH // HQ
NPROD = 3 * HD
LATENT = 64
ATT_SCALE = 1.0 / float(np.sqrt(NH + 2 * LATENT))
NS1 = 12


def at_x_pe(pe, p, b):
    pe.wait_ge(p.at_kr.sem, p.at_kr.at(b))
    x_transpose(pe, p, b, p.xn, p.bk[0], NB2)


def at_latent_pe(pe, p, b):
    pe.wait_ge(p.at_xc.sem, p.at_xc.at(b + 1))
    pe.matmul(p.bk[0][:, S:2 * S], p.at_w[:, 0:P], p.at_xa[:], start=True, stop=True).then_inc(p.at_ctp.sem, 1)


def at_project_pe(pe, p, b):
    pe.wait_ge(p.at_ct.sem, p.at_ct.at(b + 1))
    for t in range(NB2):
        c = slice(t * P, (t + 1) * P)
        ins = pe.matmul(p.bk[0][:, c], p.at_xa[:, c], p.at_w[:, P:2 * P], start=True, stop=True)
    ins.then_inc(p.at_krp.sem, 1)
    pe.wait_ge(p.at_qt.sem, p.at_qt.at(NB2 * b))
    for n in range(2):
        r = slice(n * LATENT, (n + 1) * LATENT)
        for t in range(NB2):
            ins = pe.matmul(p.bk[1 + n][:, 2 * t * D:2 * (t + 1) * D], p.at_c[r, t * P:(t + 1) * P], p.at_u[r, :],
                            start=True, stop=True)
        ins.then_inc(p.at_prp.sem, 1)


def at_turn_pe(pe, p, t, which, bank):
    for q in range(NHQ):
        src = p.at_sk[:, which, t, q * HQ:(q + 1) * HQ, :].rearrange("p h r -> p (h r)")
        ins = pe.transpose(bank[:, q * P:(q + 1) * P], src, p.ident[:])
    return ins


def at_keys_pe(pe, p, b):
    pe.wait_ge(p.at_q.sem, p.at_q.at(NS1 * b + NS1))
    pe.wait_ge(p.at_hc.sem, p.at_hc.at(2 * b + 2))
    for t in range(NB2):
        at_turn_pe(pe, p, t, 1, p.bk[1 + t]).then_inc(p.at_ktp.sem, 1)


def at_queries_pe(pe, p, b):
    for t in range(NB2):
        pe.wait_ge(p.at_kt.sem, p.at_kt.at(NB2 * b + t + 1))
        at_turn_pe(pe, p, t, 0, p.bk[1 + t]).then_inc(p.at_qtp.sem, 1)


def head_rows(h, n):
    return slice(HR * (h % HQ), HR * (h % HQ) + n)


def at_pe_element(pe, p, b, par, last):
    pe.wait_ge(p.at_qt.sem, p.at_qt.at(NB2 * b + NB2))
    pe.wait_ge(p.at_x.sem, p.at_x.at(b))
    for f in range(NH):
        t, pair = divmod(f, NH // 2)
        if f >= 4:
            pe.wait_ge(p.at_mx.sem, p.at_mx.at(NH * b + f - 3))
        for n in range(2):
            h = pair % HQ + HQ * (2 * (pair // HQ) + n)
            r = head_rows(h, NPROD)
            ins = pe.matmul(p.bk[3 + f % 4][:, n * S:(n + 1) * S], p.at_qT[r, h // HQ, t * P:(t + 1) * P],
                            p.at_kT[par][r, h // HQ, :], start=True, stop=True)
        ins.then_inc(p.at_s1.sem, 1)
        if f == 8 and not last:
            at_x_pe(pe, p, b + 1)
    pe.wait_ge(p.at_nm.sem, p.at_nm.at(2 * b + 2))
    for t in range(NB2):
        at_turn_pe(pe, p, t, 0, p.bk[3 + t]).then_inc(p.at_q2p.sem, 1)
    if not last:
        at_latent_pe(pe, p, b + 1)
    pe.wait_ge(p.at_q2.sem, p.at_q2.at(NB2 * b + NB2))
    for h in range(NH + 2):
        if h < NH:
            if h >= 4:
                pe.wait_ge(p.at_ex.sem, p.at_ex.at(NH * b + h - 3))
            r = head_rows(h, NPROD + 2)
            for t in range(NB2):
                ins = pe.matmul(p.bk[3 + (h + 2) % 4][:, t * S:(t + 1) * S],
                                p.at_kT[par][r, h // HQ, t * P:(t + 1) * P], p.at_qT2[r, h // HQ, :],
                                start=True, stop=True)
            ins.then_inc(p.at_s2.sem, 1)
        if h >= 2:
            a = h - 2
            pe.wait_ge(p.at_ex.sem, p.at_ex.at(NH * b + a + 1))
            if a % 8 == 0:
                pe.wait_ge(p.at_op.sem, p.at_op.at(2 * b + a // 8))
            o = p.bk[7][HR * (a % HQ):HR * (a % HQ + 1), (a // HQ) % 2 * S:((a // HQ) % 2 + 1) * S]
            for t in range(NB2):
                ins = pe.matmul(o, p.at_v[:, par, t, a, :], p.at_e[:, a % 4, t * S:(t + 1) * S],
                                start=(t == 0), stop=(t == NB2 - 1))
            ins.then_inc(p.at_av.sem, 1)
        if not last:
            if h == 2:
                at_project_pe(pe, p, b + 1)
            if h == 12:
                at_keys_pe(pe, p, b + 1)
            if h == 15:
                at_queries_pe(pe, p, b + 1)
    pe.wait_ge(p.at_op.sem, p.at_op.at(2 * b + 2))
    for t in range(NB2):
        for q in range(NHQ):
            ins = pe.transpose(p.bk[3 + t][:, q * P:(q + 1) * P], p.at_o[:, q, t * P:(t + 1) * P], p.ident[:])
    ins.then_inc(p.at_otp.sem, 1)
    pe.wait_ge(p.at_on.sem, p.at_on.at(4 * b + 4))
    for t in range(NB2):
        ins = pe.transpose(p.bk[5][:, t * P:(t + 1) * P], p.at_n[:, t, :], p.ident[:])
    ins.then_inc(p.at_tp.sem, 1)
    pe.wait_ge(p.at_ot.sem, p.at_ot.at(b + 1))
    for t in range(NB2):
        c = slice(t * P, (t + 1) * P)
        ins = pe.matmul(p.bk[6][:, c], p.at_t[:, c], p.at_wo[:], start=True, stop=True)
    ins.then_inc(p.at_wp.sem, 1)


def at_pe(pe, p):
    pe.wait_ge(p.at_init.sem, p.at_init.at(5))
    at_x_pe(pe, p, 0)
    at_latent_pe(pe, p, 0)
    at_project_pe(pe, p, 0)
    at_keys_pe(pe, p, 0)
    at_queries_pe(pe, p, 0)
    with pe.Fori(0, B // 2 - 1) as i:
        at_pe_element(pe, p, 2 * i, 0, False)
        at_pe_element(pe, p, 2 * i + 1, 1, False)
    at_pe_element(pe, p, B - 2, 0, False)
    at_pe_element(pe, p, B - 1, 1, True)


def at_x_act(act, p, b):
    act.wait_ge(p.xt.sem, p.xt.at(b + 1))
    act.wait_ge(p.at_prp.sem, p.at_prp.at(NB2 * b))
    act.activation(p.at_xa[:], p.bk[0][:, 0:S], ACT.Copy).then_inc(p.at_xc.sem, 1)


def at_latent_act(act, p, b):
    act.wait_ge(p.at_ctp.sem, p.at_ctp.at(b + 1))
    act.activation(p.at_c[:], p.bk[0][:, S:2 * S], ACT.Copy).then_inc(p.at_ct.sem, 1)


def at_kr_act(act, p, b):
    act.wait_ge(p.at_krp.sem, p.at_krp.at(b + 1))
    act.wait_ge(p.at_q.sem, p.at_q.at(NS1 * b))
    act.activation(p.at_r[:, 1], p.bk[0][:, 0:S].rearrange("p (t d) -> p t d", t=NB2), ACT.Copy)\
       .then_inc(p.at_kr.sem, 1)


def at_parts_act(act, p, b):
    act.wait_ge(p.at_q.sem, p.at_q.at(NS1 * b + 10))
    for which, c in ((0, HD), (1, 2 * HD)):
        act.activation(p.at_sk_r[:, which, :, :, c:c + HD], p.at_sk[:, which, :, :, 0:HD], ACT.Copy)\
           .then_inc(p.at_hc.sem, 1)


def at_turned_act(act, src, dst, t):
    return act.activation(dst[:, :, t * P:(t + 1) * P], src[:].rearrange("p (q t) -> p q t", q=NHQ), ACT.Copy)


def at_keys_act(act, p, b, par):
    for t in range(NB2):
        act.wait_ge(p.at_ktp.sem, p.at_ktp.at(NB2 * b + t + 1))
        at_turned_act(act, p.bk[1 + t], p.at_kT[par], t).then_inc(p.at_kt.sem, 1)


def at_queries_act(act, p, b):
    for t in range(NB2):
        act.wait_ge(p.at_qtp.sem, p.at_qtp.at(NB2 * b + t + 1))
        at_turned_act(act, p.bk[1 + t], p.at_qT, t).then_inc(p.at_qt.sem, 1)


def at_act_element(act, p, b, par, last):
    if not last:
        at_x_act(act, p, b + 1)
    for t in range(NB2):
        act.wait_ge(p.at_q2p.sem, p.at_q2p.at(NB2 * b + t + 1))
        at_turned_act(act, p.bk[3 + t], p.at_qT2, t).then_inc(p.at_q2.sem, 1)
    if not last:
        at_latent_act(act, p, b + 1)
    for h in range(NH):
        act.wait_ge(p.at_s2.sem, p.at_s2.at(NH * b + h + 1))
        if h >= 4:
            act.wait_ge(p.at_av.sem, p.at_av.at(NH * b + h - 3))
        act.activation(p.at_e[:, h % 4, :], p.bk[3 + (h + 2) % 4][:], ACT.Exp, scale=ATT_SCALE)\
           .then_inc(p.at_ex.sem, 1)
        if not last:
            if h == 3:
                at_kr_act(act, p, b + 1)
            if h == 10:
                at_parts_act(act, p, b + 1)
            if h == 13:
                at_keys_act(act, p, b + 1, 1 - par)
    if not last:
        at_queries_act(act, p, b + 1)
    act.wait_ge(p.at_tp.sem, p.at_tp.at(b + 1))
    act.activation(p.at_t[:], p.bk[5][:, 0:S], ACT.Copy).then_inc(p.at_ot.sem, 1)


def at_act(act, p):
    act.wait_ge(p.at_init.sem, p.at_init.at(5))
    at_x_act(act, p, 0)
    at_latent_act(act, p, 0)
    at_kr_act(act, p, 0)
    at_parts_act(act, p, 0)
    at_keys_act(act, p, 0, 0)
    at_queries_act(act, p, 0)
    with act.Fori(0, B // 2 - 1) as i:
        at_act_element(act, p, 2 * i, 0, False)
        at_act_element(act, p, 2 * i + 1, 1, False)
    at_act_element(act, p, B - 2, 0, False)
    at_act_element(act, p, B - 1, 1, True)


def at_project_dve(dve, p, b, par):
    n = NS1 * b
    heads = "p t (h d) -> p t h d"
    for m, dst in ((0, p.at_r[:, 0]), (1, p.at_s[:, 0]), (2, p.at_s[:, 1]), (3, p.at_v[:, par, :, :, 0:HD])):
        dve.wait_ge(p.at_prp.sem, p.at_prp.at(2 * b + m // 2 + 1))
        src = p.bk[1 + m // 2][:].rearrange("p (t d) -> p t d", t=NB2)[:, :, (m % 2) * D:(m % 2 + 1) * D]
        bias = p.at_b[:, m * D:(m + 1) * D].unsqueeze(1).to_broadcast([P, NB2, D])
        if m == 3:
            src, bias = src.rearrange(heads, d=HD), bias.rearrange(heads, d=HD)
        dve.tensor_tensor(dst, src, bias, ALU.add).then_inc(p.at_q.sem, 1)
    dve.wait_ge(p.at_kr.sem, p.at_kr.at(b + 1))
    dve.wait_ge(p.at_q.sem, p.at_q.at(n + 4))
    r, t1, t2 = (x.rearrange("p w t d -> p w (t d)") for x in (p.at_r, p.at_t1, p.at_t2))
    pairs = "p w (i two) -> p w i two"
    rp, tp = r.rearrange(pairs, two=2), t2.rearrange(pairs, two=2)
    dve.tensor_tensor(t1, r, p.at_cos[:].unsqueeze(1).to_broadcast([P, 2, S]), ALU.mult).then_inc(p.at_q.sem, 1)
    for k in range(2):
        sin = p.at_sin[:, k, :].unsqueeze(1).to_broadcast([P, 2, S // 2])
        dve.tensor_tensor(tp[:, :, :, k], rp[:, :, :, 1 - k], sin, ALU.mult).then_inc(p.at_q.sem, 1)
    dve.wait_ge(p.at_q.sem, p.at_q.at(n + 7))
    dve.tensor_tensor(t1, t1, t2, ALU.add).then_inc(p.at_q.sem, 1)
    dve.wait_ge(p.at_q.sem, p.at_q.at(n + 8))
    dve.tensor_tensor(t1, t1, p.at_s.rearrange("p w t d -> p w (t d)"), ALU.add).then_inc(p.at_q.sem, 1)
    dve.wait_ge(p.at_q.sem, p.at_q.at(n + 9))
    dve.wait_ge(p.at_q2p.sem, p.at_q2p.at(NB2 * b))
    qk = p.at_t1.rearrange("p w t (h d) -> p w t h d", d=HD)
    dve.tensor_copy(p.at_sk_r.rearrange("p w t h r -> p (w t h) r")[:, :, 0:HD],
                    p.at_t1.rearrange("p w t (h d) -> p (w t h) d", d=HD)).then_inc(p.at_q.sem, 1)
    dve.wait_ge(p.at_q.sem, p.at_q.at(n + 10))
    for which, c in ((0, 2 * HD), (1, HD)):
        dve.tensor_tensor(p.at_sk_r[:, which, :, :, c:c + HD], qk[:, which], p.at_sk[:, which, :, :, 0:HD],
                          ALU.subtract).then_inc(p.at_q.sem, 1)


def at_dve_element(dve, p, b, par, last, more):
    if not last:
        ln_apply(dve, p, b + 1, p.xn, P - 1, NB2)
    for f in range(NH):
        t, pair = divmod(f, NH // 2)
        dve.wait_ge(p.at_s1.sem, p.at_s1.at(NH * b + f + 1))
        q = 2 * (pair // HQ)
        dve.tensor_reduce(p.at_m[:, t, :].rearrange("p (q r) -> p q r", r=HQ)[:, q:q + 2, pair % HQ], p.bk[3 + f % 4][:].rearrange("p (h k) -> p h k", h=2),
                          AX.X, ALU.max, negate=True).then_inc(p.at_mx.sem, 1)
    dve.wait_ge(p.at_mx.sem, p.at_mx.at(NH * b + NH))
    dve.tensor_copy(p.at_sk_r[:, 0, :, :, NPROD], p.at_m[:]).then_inc(p.at_nm.sem, 1)
    dve.wait_ge(p.at_nm.sem, p.at_nm.at(2 * b + 1))
    dve.tensor_tensor(p.at_sk_r[:, 0, :, :, NPROD + 1], p.at_m[:], p.at_sk[:, 0, :, :, NPROD], ALU.subtract)\
       .then_inc(p.at_nm.sem, 1)
    if not last:
        at_project_dve(dve, p, b + 1, 1 - par)
    for half in range(2):
        dve.wait_ge(p.at_av.sem, p.at_av.at(NH * b + 8 * half + 8))
        dve.tensor_copy(p.at_o[:, 2 * half:2 * half + 2, :], p.bk[7][:].rearrange("p (q s) -> p q s", q=2))\
           .then_inc(p.at_op.sem, 1)
    x = p.X[:, bass.ds(b * NB2, NB2), :]
    dve.tensor_tensor(x, x, p.at_bo[:].unsqueeze(1).to_broadcast([P, NB2, D]), ALU.add).then_inc(p.at_x1.sem, 1)
    if more:
        ln_stats(dve, p, b + 2, NB2)
    dve.wait_ge(p.at_otp.sem, p.at_otp.at(b + 1))
    for t in range(NB2):
        o = p.bk[3 + t][:].rearrange("p (h r) -> p h r", r=HR)
        dve.reciprocal(p.at_rc[:, t, :], o[:, :, HD]).then_inc(p.at_on.sem, 1)
    dve.wait_ge(p.at_on.sem, p.at_on.at(4 * b + 2))
    for t in range(NB2):
        o = p.bk[3 + t][:].rearrange("p (h r) -> p h r", r=HR)
        dve.tensor_tensor(p.at_n[:, t, :].rearrange("p (h d) -> p h d", d=HD), o[:, :, 0:HD],
                          p.at_rc[:, t, :].unsqueeze(2).to_broadcast([P, NH, HD]), ALU.mult).then_inc(p.at_on.sem, 1)
    dve.wait_ge(p.at_wp.sem, p.at_wp.at(b + 1))
    dve.wait_ge(p.at_x1.sem, p.at_x1.at(b + 1))
    dve.tensor_tensor(x, x, p.bk[6][:, 0:S].rearrange("p (t d) -> p t d", t=NB2), ALU.add).then_inc(p.at_x.sem, 1)


def at_dve(dve, p):
    dve.wait_ge(p.at_init.sem, p.at_init.at(5))
    ln_stats(dve, p, 0, NB2)
    ln_apply(dve, p, 0, p.xn, P - 1, NB2)
    ln_stats(dve, p, 1, NB2)
    at_project_dve(dve, p, 0, 0)
    with dve.Fori(0, B // 2 - 1) as i:
        at_dve_element(dve, p, 2 * i, 0, False, True)
        at_dve_element(dve, p, 2 * i + 1, 1, False, True)
    at_dve_element(dve, p, B - 2, 0, False, False)
    at_dve_element(dve, p, B - 1, 1, True, False)


def at_pool(pool, p):
    pool.memset(p.at_sk[:], 0.0).then_inc(p.at_init.sem, 1)
    pool.memset(p.at_v[:], 0.0).then_inc(p.at_init.sem, 1)
    pool.wait_ge(p.at_init.sem, p.at_init.at(2))
    pool.memset(p.at_sk[:, 1, :, :, NPROD:NPROD + 2], 1.0).then_inc(p.at_init.sem, 1)
    for par in range(2):
        pool.memset(p.at_v[:, par, :, :, HD], 1.0).then_inc(p.at_init.sem, 1)
    with pool.Fori(0, B) as b:
        ln_scale(pool, p, b, NB2)


def at_weights_dve(dve, p):
    dve.wait_ge(p.dma_at.sem, p.dma_at.at(p.nat))
    dve.scalar_tensor_tensor(out=p.at_w[:], in0=p.at_last[:], scalar=p.neg_but_last[:, 0:1], in1=p.at_w[:],
                             op0=ALU.mult, op1=ALU.add).then_inc(p.atw.sem, 1)


ENGINES = 4
_PREP = dict(ln_free=NG, ln_stat=2 * NT, ln_rs=2 * NG, xt=NG, xhd=NG, xld=NG, lg=NG, rt1=10 * NG, rt2=7 * NG, rte=NG)
_UN = NG * E
USES = {
    "moe": dict(_PREP, act_r=4 * _UN, act_t=4 * _UN, hid=4 * _UN, hidT=4 * _UN, outl=4 * _UN, dve_a=NA * _UN,
                dve_b=NB * _UN, dve_c=NC * _UN, pl_r=NR * _UN, pl_g=NGT * _UN, pl_u=NU * _UN, gtT=NG, gts=NG,
                shf=NG, res=NG, fin=NG, gcp=2 * NG),
    "gau": dict(ln_free=B, ln_stat=2 * NT, ln_rs=6 * B, xt=B, ln_both=B, ga_xc=B, ga_qk=B, ga_qkp=B, ga_vg=2 * B,
                ga_vgp=2 * B, ga_hd=2 * B, ga_sw=B, ga_rp=3 * B, ga_lk=B, ga_lkp=B, ga_scp=B, ga_at=2 * B, ga_kv=B,
                ga_kvp=B, ga_o=B, ga_op=B, ga_ot=B, ga_otp=B, ga_y=5 * B, ga_wop=B, ga_rs=2 * B, ga_yn=B, ga_px=3 * B),
    "mla": dict(ln_free=B, ln_stat=2 * NT, ln_rs=2 * B, xt=B, at_xc=B, at_ctp=B, at_ct=B, at_krp=B, at_kr=B,
                at_prp=2 * B, at_q=NS1 * B, at_hc=2 * B, at_ktp=2 * B, at_kt=2 * B, at_qtp=2 * B, at_qt=2 * B,
                at_s1=NH * B, at_mx=NH * B, at_nm=2 * B, at_q2p=2 * B, at_q2=2 * B, at_s2=NH * B, at_ex=NH * B,
                at_av=NH * B, at_op=2 * B, at_otp=B, at_on=4 * B, at_tp=B, at_ot=B, at_wp=B, at_x1=B, at_x=B,
                at_init=5),
    "swiglu": dict(_PREP, gt_rows=NCH * NG, up_rows=NCH * NG, silu_d=NCH * NG, hid_d=NCH * NG, exp_d=E1 * NG,
                   exp_add=TG * E1 * NG, rtg=NG, rt3=2 * NG),
}


PHASES = ["moe", "gau", "moe", "swiglu", "mla", "swiglu"]
LOADS = ["xload", "dma_w1", "dma_w2", "dma_small", "dma_sw", "dma_ga", "dma_at"]
ONCE = ["const", "wts", "wpe", "wsw", "gab", "gaw", "atw", "phase_end", "stored",
        "pe_passed", "dve_passed", "pool_passed"]
NW = NQ + 2 * H

TENSORS = {
    "X": ([P, NT, D], F32),
    "w1h": ([P, E * F], F32R), "w1l": ([P, E * F], F32R), "w2c": ([P, E * F], F32),
    "sa": ([P, E * F], F32), "sb_": ([P, E * F], F32), "sc": ([P, E * F], F32),
    "wr_f": ([P, E], F32), "wr_last": ([P, E], F32), "wrh": ([P, E], F32R), "wrl": ([P, E], F32R),
    "g1": ([P, E * FC], F32), "be1": ([P, E * FC], F32), "c2b": ([P, E * D], F32), "g2b": ([P, E * D], F32),
    "be2p": ([TG * E, TG, D], F32),
    "neg_but_last": ([P, 1], F32), "ident": ([P, P], F32), "iota8": ([P, E], F32), "ones_f": ([P, P], F32),
    "neg_half": ([P, 8], F32), "eps8": ([P, 8], F32),
    "ln_st": ([P, TG, 6], F32), "ln_mv": ([P, TG, 2], F32), "ln_ve": ([P, TG], F32), "ln_r": ([P, TG], F32),
    "ln_r2": ([P, TG], F32), "xn": ([P, TG, D], F32), "xf": ([P, TG, D], F32),
    "xh": ([P, 2, W], F32R), "xl": ([P, 2, W], F32R),
    "rt_l": ([P, TG, NL], F32), "rt_m": ([P, TG, 8], F32), "rt_i": ([P, TG, 8], U32), "rt_d": ([P, TG, E], F32),
    "rt_e": ([P, TG, E], F32), "rt_s0": ([P, TG, E], F32), "rt_s1": ([P, TG, E], F32), "rt_z": ([P, TG], F32),
    "rt_r": ([P, TG], F32), "rt_g": ([P, TG], F32),
    "gate": ([P, 2, TG * E], F32), "gate_e": ([P, 2, E, TG], F32), "gT": ([TG * E, P], F32),
    "gate1": ([P, 2, TG, E1], F32),
    "st1": ([P, 2, TG, 6], F32), "mv1": ([P, 2, TG, 2], F32), "rs1": ([P, 2, TG], F32), "ve1": ([P, 2, TG], F32),
    "st2": ([P, TG, 6], F32), "mv2": ([P, 2, TG, 2], F32), "ve2": ([P, TG], F32), "rs2": ([P, TG], F32),
    "ga": ([P, 2, TG], F32),
    "wgh": ([P, ROWS], F32R), "wgl": ([P, ROWS], F32R), "wuh": ([P, ROWS], F32R), "wul": ([P, ROWS], F32R),
    "wd": ([P, len(PIECES) * D], F32), "wr1_f": ([P, NL], F32), "wr1h": ([P, NL], F32R), "wr1l": ([P, NL], F32R),
    "ga_w": ([P, NW], F32), "ga_last": ([P, NW], F32), "ga_ln_w": ([P, 2], F32), "ga_ln_b": ([P, P], F32),
    "ga_brow": ([1, NW], F32), "e_last": ([1, P], F32), "ga_gb": ([NQ, 4], F32), "ga_cos": ([NQ, S], F32),
    "ga_sin": ([NQ, S], F32), "ga_perm": ([NQ, NQ], F32), "ga_wo": ([P, 2 * D], F32), "ga_bo": ([P, D], F32),
    "ga_w2": ([P, D], F32), "ga_b2": ([P, D], F32), "ga_dist": ([P, P], F32), "ga_bias": ([P, P], F32),
    "ga_bt": ([P, P], F32), "ga_pos": ([P, MAXREL + 1], F32),
    "at_w": ([P, 2 * P], F32), "at_last": ([P, 2 * P], F32), "at_u": ([P, 2 * D], F32), "at_b": ([P, 4 * D], F32),
    "at_wo": ([P, D], F32), "at_bo": ([P, D], F32), "at_cos": ([P, S], F32), "at_sin": ([P, 2, S // 2], F32),
    "at_qT": ([P, NHQ, S], F32R), "at_qT2": ([P, NHQ, S], F32R),
}


def named(what, **parts):
    return namedtuple(what, parts)(**parts)


def work_space(t):
    w = {"gate4": t.gate[:].rearrange("p x (j e) -> p x j e", e=E)}
    at = Space(t.sb_)
    w.update(r=at.take(P, TG, F), rT=at.take(P, 2, F), y=at.take(P, 2, TG, D))
    at = Space(t.sc)
    w.update(gy=at.take(P, TG, D), acc=at.take(P, TG, D))

    w.update(hT=Space(t.sc).take(P, HRING, W), sg=Space(t.sb_).take(P, 2, W))

    at = Space(t.sb_)
    w.update(ga_xa=at.take(P, S), ga_q=at.take(NQ, S), ga_h=at.take(NQ, 2, S), ga_r1=at.take(NQ, 2, S),
             ga_r2=at.take(NQ, 2, S), ga_r=at.take(NQ, 2, 2, S), ga_k=at.take(P, P), ga_s=at.take(NQ, H))
    at = Space(t.sc)
    w.update(ga_v=at.take(P, 2, NB2, 2 * H), ga_a1=at.take(P, NB2, P), ga_a=at.take(P, NB2, P),
             ga_g=at.take(P, NB2, H), ga_t=at.take(P, 4 * P))
    at = Space(t.sa, 2 * ROWS)
    w.update(ga_yy=at.take(P, NB2, D), ga_z=at.take(P, NB2, D), ga_st=at.take(P, NB2, 6), ga_mv=at.take(P, NB2, 2),
             ga_ve=at.take(P, NB2), ga_sc=at.take(P, NB2))

    at = Space(t.sa)
    w.update(at_sk=at.take(P, 2, NB2, NH, HR), at_e=at.take(P, 4, NB2 * S))
    w.update(at_sk_r=w["at_sk"].bitcast(F32R))
    at = Space(t.sb_)
    w.update(at_v=at.take(P, 2, NB2, NH, HR), at_xa=at.take(P, S), at_c=at.take(P, S), at_r=at.take(P, 2, NB2, D),
             at_s=at.take(P, 2, NB2, D), at_t1=at.take(P, 2, NB2, D))
    at = Space(t.sc)
    w.update(at_t2=at.take(P, 2, NB2, D), at_o=at.take(P, NHQ, S), at_n=at.take(P, NB2, D), at_t=at.take(P, S),
             at_m=at.take(P, NB2, NH), at_rc=at.take(P, NB2, NH))
    w.update(at_kT=[x[:].rearrange("p a (b s) -> p (a b) s", s=S) for x in (t.xh, t.xl)])
    return w


def load(sp, dst, src, sem):
    shape = list(dst.shape)
    sp.dma_start(dst, src if src.shape[0] == shape[0] else src.to_broadcast(shape)).then_inc(sem, 16)


def build(nc, io, phases=PHASES):
    with ExitStack() as ctx:
        tally = {n: Tally(ctx.enter_context(nc.semaphore(n)))
                 for n in LOADS + ONCE + sorted({n for uses in USES.values() for n in uses})}
        tensors = {n: ctx.enter_context(nc.sbuf_tensor("sb_" + n, shape, dt)) for n, (shape, dt) in TENSORS.items()}
        t = named("Tensors", **tensors)
        small = [(t.ident, "ident"), (t.iota8, "iota8"), (t.be1, "be1"), (t.c2b, "b2"), (t.g2b, "g2"),
                 (t.be2p, "be2p")]
        ga_loads = [(t.ga_w[:], "ga_raw"), (t.ga_last[:], "ga_last"), (t.ga_ln_w[:, 0:1], "ga_ln_w"),
                    (t.ga_ln_w[:, 1:2], "ga_ln_w_last"), (t.ga_ln_b[:], "ga_ln_b"), (t.ga_brow[:], "ga_brow"),
                    (t.e_last[:], "e_last"), (t.ga_gb[:], "ga_gb"), (t.ga_cos[:], "ga_cos"), (t.ga_sin[:], "ga_sin"),
                    (t.ga_perm[:], "ga_perm"), (t.ga_wo[:], "ga_wo"), (t.ga_bo[:], "ga_bo"), (t.ga_w2[:], "ga_w2"),
                    (t.ga_b2[:], "ga_b2"), (t.ga_dist[:], "ga_dist"), (t.ga_bias[:], "ga_mask"), (t.ga_pos[:], "ga_pos")]
        at_loads = [(t.at_w[:], "at_w"), (t.at_last[:], "at_last"), (t.at_u[:], "at_u"), (t.at_b[:], "at_b"),
                    (t.at_wo[:], "at_wo"), (t.at_bo[:], "at_bo"), (t.at_cos[:], "at_cos"), (t.at_sin[:], "at_sin")]
        p = named("Program", phases=phases, tally=tally, nsmall=16 * len(small), nga=16 * len(ga_loads),
                  nat=16 * len(at_loads), bk=[ctx.enter_context(nc.psum_tensor(f"bk{i}", [P, 512], F32)) for i in range(8)],
                  **tally, **tensors, **work_space(t))

        block = ctx.enter_context(nc.Block())

        @block.sync
        def _(sp):
            xs = io["x"].rearrange("(t p) d -> p t d", p=P)
            sp.dma_start(p.X[:, 0:TG, :], xs[:, 0:TG, :]).then_inc(p.xload.sem, 16)
            for dst, n in small:
                load(sp, dst[:], io[n], p.dma_small.sem)
            sp.dma_start(p.X[:, TG:NT, :], xs[:, TG:NT, :]).then_inc(p.xload.sem, 16)
            for dst, n in ga_loads:
                load(sp, dst, io[n], p.dma_ga.sem)
            for dst, n in at_loads:
                load(sp, dst, io[n], p.dma_at.sem)
            sp.wait_ge(p.wts.sem, p.wts.at(18))
            sp.dma_start(p.sa[:, 0:2 * ROWS], io["w_gu"]).then_inc(p.dma_sw.sem, 16)
            sp.dma_start(p.wr1_f[:], io["w_r1"]).then_inc(p.dma_sw.sem, 16)
            sp.dma_start(p.wd[:], io["w_d"]).then_inc(p.dma_sw.sem, 16)
            sp.wait_ge(p.phase_end.sem, p.phase_end.at(ENGINES * len(p.phases)))
            out = io["out"].rearrange("(t p) d -> p t d", p=P)
            sp.dma_start(out, p.X[:]).then_inc(p.stored.sem, 16)
            sp.wait_ge(p.stored.sem, p.stored.at(16))

        @block.gpsimd
        def _(pool):
            pool.memset(p.neg_half[:], -0.5).then_inc(p.const.sem, 1)
            pool.memset(p.ones_f[:], 1.0 / F).then_inc(p.const.sem, 1)
            pool.memset(p.xn[:], 1.0).then_inc(p.const.sem, 1)
            pool.memset(p.eps8[:], EPS).then_inc(p.const.sem, 1)
            pool.wait_ge(p.const.sem, p.const.at(NCONST))
            ga_bias_pool(pool, p)
            for n, phase in enumerate(p.phases):
                begin(pool, p, n)
                if phase == "moe":
                    moe_pool(pool, p)
                elif phase == "gau":
                    ga_pool(pool, p)
                elif phase == "swiglu":
                    sw_pool(pool, p)
                elif phase == "mla":
                    at_pool(pool, p)
                end(pool, p)

        @block.scalar
        def _(act):
            act.dma_start(p.sa[:], io["w1"]).then_inc(p.dma_w1.sem, 16)
            act.dma_start(p.sb_[:], io["w1_last"].to_broadcast([P, E * F])).then_inc(p.dma_w1.sem, 16)
            act.dma_start(p.neg_but_last[:], io["neg_but_last"]).then_inc(p.dma_w1.sem, 16)
            act.dma_start(p.wr_f[:], io["wr"]).then_inc(p.dma_w1.sem, 16)
            act.dma_start(p.wr_last[:], io["wr_last"].to_broadcast([P, E])).then_inc(p.dma_w1.sem, 16)
            act.dma_start(p.sc[:], io["w2"]).then_inc(p.dma_w2.sem, 16)
            act.dma_start(p.g1[:], io["g1"]).then_inc(p.dma_w2.sem, 16)
            for n, phase in enumerate(p.phases):
                begin(act, p, n)
                if phase == "moe":
                    moe_act(act, p)
                elif phase == "gau":
                    ga_act(act, p)
                elif phase == "swiglu":
                    sw_act(act, p)
                elif phase == "mla":
                    at_act(act, p)
                end(act, p)

        @block.vector
        def _(dve):
            dve.wait_ge(p.const.sem, p.const.at(NCONST))
            dve.wait_ge(p.xload.sem, p.xload.at(32))
            moe_weights_dve(dve, p)
            for n, phase in enumerate(p.phases):
                begin(dve, p, n)
                if phase == "swiglu" and phase not in p.phases[:n]:
                    sw_weights_dve(dve, p)
                if phase == "gau":
                    ga_weights_dve(dve, p)
                if phase == "mla":
                    at_weights_dve(dve, p)
                if phase == "moe":
                    moe_dve(dve, p)
                elif phase == "gau":
                    ga_dve(dve, p)
                elif phase == "swiglu":
                    sw_dve(dve, p)
                elif phase == "mla":
                    at_dve(dve, p)
                end(dve, p)

        @block.tensor
        def _(pe):
            pe.wait_ge(p.dma_small.sem, p.dma_small.at(p.nsmall))
            pe.wait_ge(p.const.sem, p.const.at(NCONST))
            moe_weights_pe(pe, p)
            for n, phase in enumerate(p.phases):
                begin(pe, p, n)
                if phase == "swiglu" and phase not in p.phases[:n]:
                    pe.wait_ge(p.wsw.sem, p.wsw.at(6))
                if phase == "gau":
                    ga_weights_pe(pe, p)
                if phase == "mla":
                    pe.wait_ge(p.atw.sem, p.atw.at(1))
                if phase == "moe":
                    moe_pe(pe, p)
                elif phase == "gau":
                    ga_pe(pe, p)
                elif phase == "swiglu":
                    sw_pe(pe, p)
                elif phase == "mla":
                    at_pe(pe, p)
                end(pe, p)


def first_mixture_layout(inp):
    w1 = inp["L0_ffn_W1"].transpose(1, 0, 2).reshape(D, E * F)
    neg = -np.ones((P, 1), np.float32)
    neg[P - 1] = 0
    shifts = np.zeros((TG, E, TG, D), np.float32)
    for j in range(TG):
        shifts[j, :, j] = inp["L0_ffn_be2"]
    return dict(
        w1=np.concatenate([w1[:P - 1], inp["L0_ffn_b1"].reshape(1, E * F)], 0), w1_last=w1[P - 1:P],
        wr=np.concatenate([inp["L0_ffn_Wr"][:P - 1], inp["L0_ffn_br"][None]], 0), wr_last=inp["L0_ffn_Wr"][P - 1:P],
        w2=inp["L0_ffn_W2"].reshape(E, FC, P, D).transpose(2, 0, 1, 3).reshape(P, E * F),
        g1=inp["L0_ffn_g1"].reshape(E * FC, P).T, be1=inp["L0_ffn_be1"].reshape(E * FC, P).T,
        b2=inp["L0_ffn_b2"].reshape(1, E * D), g2=inp["L0_ffn_g2"].reshape(1, E * D),
        be2p=shifts.reshape(TG * E, TG, D), neg_but_last=neg, ident=np.eye(P, dtype=np.float32),
        iota8=np.broadcast_to(np.arange(E, dtype=np.float32), (P, E)))


def second_mixture_layout(inp):
    eg, h = inp["L1_ffn_experts_gate_up"], E * I1
    gate = np.concatenate([eg[:, :I1].reshape(h, D), inp["L1_ffn_shared_gate_w"]], 0).T
    up = np.concatenate([eg[:, I1:].reshape(h, D), inp["L1_ffn_shared_up_w"]], 0).T
    down = np.concatenate([inp["L1_ffn_experts_down"].transpose(0, 2, 1).reshape(h, D), inp["L1_ffn_shared_down_w"].T], 0)
    router = np.zeros((P, NL), np.float32)
    router[:, :E] = inp["L1_ffn_gate_w"].T
    router[:, E] = inp["L1_ffn_shared_expert_gate_w"][0]
    pieces = np.zeros((P, len(PIECES), D), np.float32)
    for q, (c, e) in enumerate(PIECES):
        a, z = max(c * P, e * I1), min(c * P + P, e * I1 + I1 if e < E else ROWS)
        pieces[a - c * P:z - c * P, q] = down[a:z]
    return dict(w_gu=np.concatenate([gate, up], 1), w_r1=router, w_d=pieces.reshape(P, -1))


def gated_unit_layout(inp):
    f = {n[8:]: a for n, a in inp.items() if n.startswith("L0_attn_")}
    qk = f["Wqk"].T
    w = np.concatenate([qk, qk, f["Wv"].T, f["Wg"].T], 1)
    ln_b = np.zeros((P, P), np.float32)
    ln_b[:, P - 1] = f["ln1_b"]
    e_last = np.zeros((1, P), np.float32)
    e_last[0, P - 1] = 1
    ga, be = f["gamma"], f["beta"]
    half = QK // 2
    freq = (10000.0 ** (-np.arange(half, dtype=np.float32) / half)).astype(np.float32)
    angle = np.arange(S, dtype=np.float32)[:, None] * freq[None]
    sin, cos = np.sin(angle).T.astype(np.float32), np.cos(angle).T.astype(np.float32)
    perm = np.zeros((NQ, NQ), np.float32)
    for i in range(NQ):
        perm[i // QK * QK + (i + half) % QK, i] = 1
    i = np.arange(P)
    dist, same = np.minimum(np.abs(i[:, None] - i[None]), MAXREL), (i[:, None] // GROUP) == (i[None] // GROUP)
    return dict(
        ga_raw=w, ga_last=w[P - 1:P], ga_ln_w=f["ln1_w"].reshape(P, 1), ga_ln_w_last=f["ln1_w"].reshape(P, 1)[P - 1:P],
        ga_ln_b=ln_b, ga_brow=np.concatenate([f["bqk"], f["bqk"], f["bv"], f["bg"]])[None], e_last=e_last,
        ga_gb=np.stack([np.concatenate([ga[0], ga[1]]), np.concatenate([be[0], be[1]]),
                        np.concatenate([ga[2], ga[3]]), np.concatenate([be[2], be[3]])], 1),
        ga_cos=np.concatenate([cos] * 4, 0), ga_sin=np.concatenate([-sin, sin] * 2, 0), ga_perm=perm,
        ga_wo=f["Wo"].T.reshape(2, P, D).transpose(1, 0, 2).reshape(P, 2 * D), ga_bo=f["bo"][None],
        ga_w2=f["ln2_w"][None], ga_b2=f["ln2_b"][None], ga_pos=f["pos_emb"][None, :MAXREL + 1],
        ga_dist=np.where(same, dist, MAXREL + 1).astype(np.float32), ga_mask=np.where(same, 0, -1e30).astype(np.float32))


def latent_attention_layout(inp):
    f = {n[8:]: a for n, a in inp.items() if n.startswith("L1_attn_")}
    w = np.concatenate([f["Wd_q_w"], f["Wd_kv_w"], f["Wk_r_w"]], 1)
    b = np.concatenate([f["Wd_q_b"], f["Wd_kv_b"], f["Wk_r_b"]])
    half = D // 2
    theta = (np.float32(10000.0) ** (-2.0 * np.arange(half, dtype=np.float32)) / half).astype(np.float32)
    angle = np.arange(S, dtype=np.float32)[:, None] * theta[None]
    cos, sin = np.cos(angle).astype(np.float32), np.sin(angle).astype(np.float32)
    sin = sin.reshape(NB2, P, half).transpose(1, 0, 2).reshape(P, NB2 * half)
    return dict(
        at_w=np.concatenate([w[:P - 1], b[None]], 0), at_last=w[P - 1:P],
        at_u=np.concatenate([np.concatenate([f["Wq_r_w"], f["Wu_q_w"]], 1),
                             np.concatenate([f["Wu_k_w"], f["Wu_v_w"]], 1)], 0),
        at_b=np.concatenate([f["Wq_r_b"], f["Wu_q_b"], f["Wu_k_b"], f["Wu_v_b"]])[None],
        at_wo=f["Wo_w"], at_bo=f["Wo_b"][None], at_sin=np.stack([-sin, sin], 1),
        at_cos=np.repeat(cos, 2, 1).reshape(NB2, P, D).transpose(1, 0, 2).reshape(P, NB2 * D))


def layout(inputs):
    inp = {n: np.asarray(a) for n, a in inputs.items()}
    out = {"x": inp["L0_attn_x"].reshape(B * S, D)}
    for part in (first_mixture_layout, second_mixture_layout, gated_unit_layout, latent_attention_layout):
        out.update(part(inp))
    return {n: np.ascontiguousarray(a) for n, a in out.items()}


def kernel(**inputs):
    import concourse.bacc as bacc
    from concourse.bass_utils import run_bass_kernel_spmd

    arrays = layout(inputs)
    nc = bacc.Bacc("TRN2", target_bir_lowering=False, num_devices=1)
    io = {n: nc.dram_tensor(n, a.shape, mybir.dt.from_np(a.dtype), kind="ExternalInput").ap() for n, a in arrays.items()}
    io["out"] = nc.dram_tensor("out", (B * S, D), F32, kind="ExternalOutput").ap()
    build(nc, io)
    r = run_bass_kernel_spmd(nc, [arrays], core_ids=[0])
    return r.results[0]["out"].reshape(B, S, D)
```

```python
from collections import namedtuple
from contextlib import ExitStack

import numpy as np

import concourse.bass as bass
from concourse import mybir

F32 = mybir.dt.float32
F32R = mybir.dt.float32r
U32 = mybir.dt.uint32
I32 = mybir.dt.int32
ALU = mybir.AluOpType
ACT = mybir.ActivationFunctionType
AX = mybir.AxisListType

P = 128
B, S, D = 16, 256, 128
NT = B * S // P
TG = 4
NG = NT // TG
W = TG * P
E = 8
F = 512
FC = F // P
EPS = 1e-5
NCONST = 7


def f32(ap):
    return ap.bitcast(F32)


class Tally:

    def __init__(self, sem):
        self.sem, self.base = sem, 0

    def at(self, n):
        return n + self.base


def uses_of(p, phase):
    behind_mixture = phase and p.phases[phase - 1] == "moe"
    return {n: u for n, u in USES[p.phases[phase]].items() if behind_mixture or n not in _COMB}


def begin(eng, p, phase):
    for uses in USES.values():
        for n in uses:
            p.tally[n].base = sum(uses_of(p, q).get(n, 0) for q in range(phase))
    if phase:
        eng.wait_ge(p.phase_end.sem, ENGINES * phase)


def end(eng, p):
    eng.drain().then_inc(p.phase_end.sem, 1)


class Space:

    def __init__(self, tensor, at=0):
        self.tensor, self.at = tensor, at

    def take(self, parts, *shape):
        n = int(np.prod(shape))
        ap = self.tensor[0:parts, self.at:self.at + n]
        self.at += n
        assert self.at <= self.tensor.shape[1]
        names = "abcd"[:len(shape)]
        if len(shape) > 1:
            ap = ap.rearrange(f"p ({' '.join(names)}) -> p {' '.join(names)}", **dict(zip(names, shape)))
        return ap


def tiles(p, g):
    return p.X[:, bass.ds(g * TG, TG), :]


def flat(ap):
    return ap.rearrange("p a b -> p (a b)")


def per_tile(ap):
    return ap.unsqueeze(2).to_broadcast([P, TG, D])


def ln_stats(dve, p, g, n=TG):
    dve.wait_ge(p.ln_free.sem, p.ln_free.at(g))
    dve.sem_inc(p.dve_passed.sem, 1)
    for j in range(n):
        dve.bn_stats(p.ln_st[:, j, :], p.X[:, g * n + j, :]).then_inc(p.ln_stat.sem, 1)
    dve.wait_ge(p.ln_stat.sem, p.ln_stat.at(2 * n * g + n))
    dve.sem_inc(p.dve_passed.sem, 1)
    for j in range(n):
        dve.bn_aggr(p.ln_mv[:, j, :], p.ln_st[:, j, :]).then_inc(p.ln_stat.sem, 1)


def ln_scale(pool, p, g, n=TG, twice=False):
    per = 6 if twice else 2
    pool.wait_ge(p.ln_stat.sem, p.ln_stat.at(2 * n * (g + 1)))
    r, ve, var = p.ln_r[:, 0:n], p.ln_ve[:, 0:n], p.ln_mv[:, 0:n, 1]
    pool.tensor_tensor(ve, var, p.eps8[:, 0:n], ALU.add).then_inc(p.ln_rs.sem, 1)
    pool.wait_ge(p.ln_rs.sem, p.ln_rs.at(per * g + 1))
    pool.tensor_tensor(r, ve, p.neg_half[:, 0:n], ALU.pow).then_inc(p.ln_rs.sem, 1)
    if twice:
        pool.wait_ge(p.ln_rs.sem, p.ln_rs.at(per * g + 2))
        pool.tensor_tensor(ve, r, r, ALU.mult).then_inc(p.ln_rs.sem, 1)
        pool.wait_ge(p.ln_rs.sem, p.ln_rs.at(per * g + 3))
        pool.tensor_tensor(ve, ve, var, ALU.mult).then_inc(p.ln_rs.sem, 1)
        pool.wait_ge(p.ln_rs.sem, p.ln_rs.at(per * g + 4))
        pool.tensor_tensor(ve, ve, p.eps8[:, 0:n], ALU.add).then_inc(p.ln_rs.sem, 1)
        pool.wait_ge(p.ln_rs.sem, p.ln_rs.at(per * g + 5))
        pool.tensor_tensor(ve, ve, p.neg_half[:, 0:n], ALU.pow).then_inc(p.ln_rs.sem, 1)


def ln_apply(dve, p, g, xn, width, n=TG, twice=False):
    dve.wait_ge(p.ln_rs.sem, p.ln_rs.at((6 if twice else 2) * (g + 1)))
    dve.wait_ge(p.xt.sem, p.xt.at(g))
    if twice:
        dve.tensor_tensor(p.ln_r2[:, 0:n], p.ln_r[:, 0:n], p.ln_ve[:, 0:n], ALU.mult).then_inc(p.ln_both.sem, 1)
        dve.wait_ge(p.ln_both.sem, p.ln_both.at(g + 1))
    for j in range(n):
        r = p.ln_r2 if twice else p.ln_r
        ins = dve.tensor_scalar(xn[:, j, 0:width], p.X[:, g * n + j, 0:width], p.ln_mv[:, j, 0:1],
                                r[:, j:j + 1], ALU.subtract, ALU.mult)
    ins.then_inc(p.ln_free.sem, 1)


def x_transpose(pe, p, g, xn, bank, n=TG):
    pe.wait_ge(p.ln_free.sem, p.ln_free.at(g + 1))
    for j in range(n):
        ins = pe.transpose(bank[:, j * P:(j + 1) * P], xn[:, j, :], p.ident)
    ins.then_inc(p.xt.sem, 1)


def x_high(act, p, g, par, bank):
    act.wait_ge(p.xt.sem, p.xt.at(g + 1))
    act.activation(p.xh[:, par, :], bank[:], ACT.Copy).then_inc(p.xhd.sem, 1)


def x_low(dve, p, g, par, bank):
    dve.wait_ge(p.xhd.sem, p.xhd.at(g + 1))
    dve.tensor_tensor(p.xl[:, par, :], bank[:], f32(p.xh[:, par, :]), ALU.subtract).then_inc(p.xld.sem, 1)


NL = 10


def router_logits(pe, p, g, par, bank, wh, wl, n):
    pe.wait_ge(p.xld.sem, p.xld.at(g + 1))
    for j in range(TG):
        c = slice(j * P, (j + 1) * P)
        out = bank[:, j * NL:j * NL + n]
        pe.matmul(out, p.xh[:, par, c], wh, start=True, stop=False)
        pe.matmul(out, p.xh[:, par, c], wl, start=False, stop=False)
        ins = pe.matmul(out, p.xl[:, par, c], wh, start=False, stop=True)
    ins.then_inc(p.lg.sem, 1)


def router_exp(act, p, g):
    act.wait_ge(p.rt1.sem, p.rt1.at(10 * g + 6))
    act.activation(p.rt_e[:], p.rt_d[:], ACT.Exp).then_inc(p.rte.sem, 1)


def router_top(dve, p, g, bank, n):
    dve.wait_ge(p.lg.sem, p.lg.at(g + 1))
    dve.wait_ge(p.rt2.sem, p.rt2.at(7 * g))
    lg = p.rt_l
    dve.tensor_copy(lg[:, :, 0:n], bank[:, 0:TG * NL].rearrange("p (j n) -> p j n", n=NL)[:, :, 0:n])\
       .then_inc(p.rt1.sem, 1)
    dve.wait_ge(p.rt1.sem, p.rt1.at(10 * g + 1))
    dve.sem_inc(p.dve_passed.sem, 1)
    for j in range(TG):
        dve.max(p.rt_m[:, j, :], lg[:, j, 0:E]).then_inc(p.rt1.sem, 1)
    dve.wait_ge(p.rt1.sem, p.rt1.at(10 * g + 5))
    dve.tensor_tensor(p.rt_d[:], lg[:, :, 0:E], p.rt_m[:, :, 0:1].to_broadcast([P, TG, E]), ALU.subtract)\
       .then_inc(p.rt1.sem, 1)
    for j in range(TG):
        dve.max_index(p.rt_i[:, j, :], p.rt_m[:, j, :], lg[:, j, 0:E]).then_inc(p.rt1.sem, 1)
    dve.wait_ge(p.rt1.sem, p.rt1.at(10 * g + 10))
    for k, sel in ((0, p.rt_s0), (1, p.rt_s1)):
        dve.tensor_tensor(sel[:], p.iota8.unsqueeze(1).to_broadcast([P, TG, E]),
                          p.rt_i[:, :, k:k + 1].to_broadcast([P, TG, E]), ALU.is_equal).then_inc(p.rt2.sem, 1)
    dve.wait_ge(p.rt2.sem, p.rt2.at(7 * g + 2))
    dve.tensor_tensor(p.rt_s0[:], p.rt_s0[:], p.rt_s1[:], ALU.add).then_inc(p.rt2.sem, 1)


def router_gate(dve, p, g, gate, top_only):
    dve.wait_ge(p.rte.sem, p.rte.at(g + 1))
    dve.wait_ge(p.rt2.sem, p.rt2.at(7 * g + 3))
    dve.tensor_tensor(p.rt_s1[:], p.rt_e[:], p.rt_s0[:], ALU.mult).then_inc(p.rt2.sem, 1)
    dve.wait_ge(p.rt2.sem, p.rt2.at(7 * g + 4))
    dve.tensor_reduce(p.rt_z[:], p.rt_s1[:] if top_only else p.rt_e[:], AX.X, ALU.add).then_inc(p.rt2.sem, 1)
    dve.wait_ge(p.rt2.sem, p.rt2.at(7 * g + 5))
    dve.reciprocal(p.rt_r[:], p.rt_z[:]).then_inc(p.rt2.sem, 1)
    dve.wait_ge(p.rt2.sem, p.rt2.at(7 * g + 6))
    dve.scalar_tensor_tensor(out=gate[:, :, 0:E], in0=p.rt_s1[:], scalar=0.5,
                             in1=p.rt_r[:].unsqueeze(2).to_broadcast([P, TG, E]),
                             op0=ALU.mult, op1=ALU.mult).then_inc(p.rt2.sem, 1)


TOP = 2
REGION = B * S + P
SLOT_TILES = TOP * NT + E
UNITS = SLOT_TILES // TG
XS_ROWS = E * REGION + E * P
NFIN = 21
BITS = 3


def route_x_pe(pe, p, g, par, xn, n_log):
    pe.wait_ge(p.ln_free.sem, p.ln_free.at(g + 1))
    pe.wait_ge(p.route_xc.sem, p.route_xc.at(g))
    for j in range(TG):
        ins = pe.transpose(p.bk[6][:, j * P:(j + 1) * P], xn[:, par, j, :], p.ident)
    ins.then_inc(p.route_xt.sem, 1)
    pe.wait_ge(p.route_xc.sem, p.route_xc.at(g + 1))
    for j in range(TG):
        ins = pe.matmul(p.bk[4][:, j * NL:j * NL + n_log], p.xT[:, j * P:(j + 1) * P], p.wr_f[:, 0:n_log],
                        start=True, stop=True)
    ins.then_inc(p.route_lg.sem, 1)


def route_rank_pe(pe, p, g):
    pe.wait_ge(p.route_sel.sem, p.route_sel.at(3 * g + 3))
    pe.wait_ge(p.route_cnt.sem, p.route_cnt.at(2 * g))
    out, m = p.bk[5][:, 0:TG * E], flat(p.chosen[:])
    pe.matmul(out, p.before, m, start=True, stop=False)
    for d in range(1, TG):
        pe.matmul(out[:, d * E:], p.ones_1[:], m[:, 0:(TG - d) * E], start=False, stop=False)
    pe.matmul(out, p.ones_1[:], p.counts[:].unsqueeze(1).to_broadcast([P, TG, E]), start=False, stop=True)\
      .then_inc(p.route_pos.sem, 1)


def route_x_act(act, p, g):
    act.wait_ge(p.route_xt.sem, p.route_xt.at(g + 1))
    act.wait_ge(p.route_lg.sem, p.route_lg.at(g))
    act.activation(p.xT, p.bk[6][:], ACT.Copy).then_inc(p.route_xc.sem, 1)


def route_exp_act(act, p, g):
    act.wait_ge(p.route_top.sem, p.route_top.at(10 * g + 6))
    act.activation(p.rt_e[:], p.rt_d[:], ACT.Exp).then_inc(p.route_e.sem, 1)


def route_stats_dve(dve, p, g, par, first=False):
    if not first:
        dve.wait_ge(p.ln_free.sem, p.ln_free.at(g - 1))
    dve.sem_inc(p.dve_passed.sem, 1)
    for j in range(TG):
        dve.bn_stats(p.route_st[:, par, j, :], p.X[:, g * TG + j, :]).then_inc(p.ln_stat.sem, 1)
    dve.wait_ge(p.ln_stat.sem, p.ln_stat.at(2 * TG * g + TG))
    dve.sem_inc(p.dve_passed.sem, 1)
    for j in range(TG):
        dve.bn_aggr(p.route_mv[:, par, j, :], p.route_st[:, par, j, :]).then_inc(p.ln_stat.sem, 1)


def route_scale_pool(pool, p, g, par):
    pool.wait_ge(p.ln_stat.sem, p.ln_stat.at(2 * TG * (g + 1)))
    pool.tensor_tensor(p.route_ve[:, par], p.route_mv[:, par, :, 1], p.eps8[:, 0:TG], ALU.add).then_inc(p.ln_rs.sem, 1)
    pool.wait_ge(p.ln_rs.sem, p.ln_rs.at(2 * g + 1))
    pool.tensor_tensor(p.route_r[:, par], p.route_ve[:, par], p.neg_half[:, 0:TG], ALU.pow).then_inc(p.ln_rs.sem, 1)


def route_apply_dve(dve, p, g, par, xn, width, first=False):
    if not first:
        dve.wait_ge(p.sent[par].sem, p.sent[par].at(8 * TG * TOP * (g - par)))
    dve.wait_ge(p.ln_rs.sem, p.ln_rs.at(2 * (g + 1)))
    for j in range(TG):
        ins = dve.tensor_scalar(xn[:, par, j, 0:width], p.X[:, g * TG + j, 0:width], p.route_mv[:, par, j, 0:1],
                                p.route_r[:, par, j:j + 1], ALU.subtract, ALU.mult)
    ins.then_inc(p.ln_free.sem, 1)


def route_top_dve(dve, p, g, n_log):
    dve.wait_ge(p.route_lg.sem, p.route_lg.at(g + 1))
    dve.wait_ge(p.route_w.sem, p.route_w.at(3 * g))
    dve.tensor_copy(p.rt_l[:, :, 0:n_log], p.bk[4][:, 0:TG * NL].rearrange("p (j n) -> p j n", n=NL)[:, :, 0:n_log])\
       .then_inc(p.route_top.sem, 1)
    dve.wait_ge(p.route_top.sem, p.route_top.at(10 * g + 1))
    dve.sem_inc(p.dve_passed.sem, 1)
    for j in range(TG):
        dve.max(p.rt_m[:, j, :], p.rt_l[:, j, 0:E]).then_inc(p.route_top.sem, 1)
    dve.wait_ge(p.route_top.sem, p.route_top.at(10 * g + 5))
    dve.tensor_tensor(p.rt_d[:], p.rt_m[:], p.rt_m[:, :, 0:1].to_broadcast([P, TG, E]), ALU.subtract)\
       .then_inc(p.route_top.sem, 1)
    for j in range(TG):
        dve.max_index(p.rt_i[:, j, :], p.rt_m[:, j, :], p.rt_l[:, j, 0:E]).then_inc(p.route_top.sem, 1)
    dve.wait_ge(p.route_top.sem, p.route_top.at(10 * g + 10))
    tiles_g = bass.ds(g * TG, TG)
    for k in range(TOP):
        dve.tensor_tensor(p.sel[:, k, tiles_g, :], p.iota8.unsqueeze(1).to_broadcast([P, TG, E]),
                          p.rt_i[:, :, k:k + 1].to_broadcast([P, TG, E]), ALU.is_equal).then_inc(p.route_sel.sem, 1)
    dve.wait_ge(p.route_sel.sem, p.route_sel.at(3 * g + 2))
    dve.tensor_tensor(p.chosen[:], p.sel[:, 0, tiles_g, :], p.sel[:, 1, tiles_g, :], ALU.add)\
       .then_inc(p.route_sel.sem, 1)


def route_weights_dve(dve, p, g, over):
    dve.wait_ge(p.route_e.sem, p.route_e.at(g + 1))
    dve.tensor_reduce(p.rt_z[:], p.rt_e[:, :, 0:over], AX.X, ALU.add).then_inc(p.route_w.sem, 1)
    dve.wait_ge(p.route_w.sem, p.route_w.at(3 * g + 1))
    dve.reciprocal(p.rt_r[:], p.rt_z[:]).then_inc(p.route_w.sem, 1)
    dve.wait_ge(p.route_w.sem, p.route_w.at(3 * g + 2))
    dve.scalar_tensor_tensor(out=p.weight[:, bass.ds(g * TG, TG), :], in0=p.rt_e[:, :, 0:TOP], scalar=0.5,
                             in1=p.rt_r[:].unsqueeze(2).to_broadcast([P, TG, TOP]),
                             op0=ALU.mult, op1=ALU.mult).then_inc(p.route_w.sem, 1)


def route_rows_dve(dve, p, g, par):
    tiles_g = bass.ds(g * TG, TG)
    dve.wait_ge(p.route_pos.sem, p.route_pos.at(g + 1))
    dve.tensor_tensor(p.rt_q[:], p.bk[5][:, 0:TG * E].rearrange("p (j e) -> p j e", e=E),
                      p.region0.unsqueeze(1).to_broadcast([P, TG, E]), ALU.add).then_inc(p.route_row.sem, 1)
    dve.tensor_reduce(p.rt_c[:], p.chosen[:].rearrange("p j e -> p e j"), AX.X, ALU.add).then_inc(p.route_cnt.sem, 1)
    dve.wait_ge(p.route_row.sem, p.route_row.at(4 * g + 1))
    dve.tensor_tensor(p.rt_t[:], p.sel[:, :, tiles_g, :], p.rt_q[:].unsqueeze(1).to_broadcast([P, TOP, TG, E]),
                      ALU.mult).then_inc(p.route_row.sem, 1)
    dve.wait_ge(p.route_row.sem, p.route_row.at(4 * g + 2))
    dve.tensor_reduce(p.row[:, :, tiles_g], p.rt_t[:], AX.X, ALU.add).then_inc(p.route_row.sem, 1)
    dve.wait_ge(p.route_row.sem, p.route_row.at(4 * g + 3))
    dve.sem_inc(p.dve_passed.sem, 1)
    dve.tensor_copy(p.send_row[:, par], p.row[:, :, tiles_g]).then_inc(p.route_row.sem, 1)
    dve.wait_ge(p.route_cnt.sem, p.route_cnt.at(2 * g + 1))
    dve.tensor_tensor(p.counts[:], p.counts[:], p.rt_c[:], ALU.add).then_inc(p.route_cnt.sem, 1)


def route_send_pool(pool, p, g, par, xn):
    pool.wait_ge(p.route_row.sem, p.route_row.at(4 * g + 4))
    pool.sem_inc(p.pool_passed.sem, 1)
    for k in range(TOP):
        for j in range(TG):
            pool.indirect_dma_start(p.xs, bass.IndirectOffsetOnAxis(ap=p.send_row[:, par, k, j:j + 1], axis=0),
                                    xn[:, par, j, :], None).then_inc(p.sent[par].sem, 16)


def route_end_pe(pe, p):
    pe.wait_ge(p.route_cnt.sem, p.route_cnt.at(2 * NG))
    pe.matmul(p.bk[4][:, 0:E], p.ones_1[:], p.counts[:], start=True, stop=True).then_inc(p.route_n.sem, 1)


def route_end_dve(dve, p):
    f, n = p.fin, [0]

    def done(ins):
        n[0] += 1
        ins.then_inc(f.sem, 1)

    def by_tile(a):
        return a.unsqueeze(1).to_broadcast([P, SLOT_TILES, E])

    dve.wait_ge(p.route_n.sem, p.route_n.at(1))
    done(dve.tensor_copy(p.en[:], p.bk[4][:, 0:E]))
    dve.wait_ge(f.sem, f.at(n[0]))
    done(dve.tensor_tensor(p.e_gt[:], p.en[:].unsqueeze(2).to_broadcast([P, E, NT]),
                           p.tile0[:, 0:NT].unsqueeze(1).to_broadcast([P, E, NT]), ALU.is_gt))
    done(dve.tensor_tensor(p.e_zero[:], p.en[:], p.region0, ALU.add))
    dve.wait_ge(f.sem, f.at(n[0]))
    done(dve.tensor_copy(p.zero_row[:], p.e_zero[:]))
    done(dve.tensor_reduce(p.e_nt[:], p.e_gt[:], AX.X, ALU.add))
    dve.wait_ge(f.sem, f.at(n[0]))
    done(dve.tensor_tensor(p.e_upto[:], p.upto8.rearrange("p (a b) -> p a b", b=E),
                           p.e_nt[:].unsqueeze(1).to_broadcast([P, E, E]), ALU.mult))
    done(dve.tensor_scalar(p.e_skip[:], p.e_nt[:], float(-P), float(REGION), ALU.mult, ALU.add))
    dve.wait_ge(f.sem, f.at(n[0]))
    done(dve.tensor_reduce(p.e_cum[:], p.e_upto[:], AX.X, ALU.add))
    dve.wait_ge(f.sem, f.at(n[0]))
    done(dve.tensor_tensor(p.t_ge, p.iota72.unsqueeze(2).to_broadcast([P, SLOT_TILES, E]),
                           by_tile(p.e_cum[:]), ALU.is_ge))
    done(dve.tensor_tensor(p.e_first[:], p.e_cum[:], p.e_nt[:], ALU.subtract))
    dve.wait_ge(f.sem, f.at(n[0]))
    done(dve.tensor_reduce(p.t_ex[:], p.t_ge, AX.X, ALU.add))
    done(dve.tensor_tensor(p.t_skip, p.t_ge, by_tile(p.e_skip[:]), ALU.mult))
    done(dve.scalar_tensor_tensor(out=p.e_move[:], in0=p.e_first[:], scalar=float(P), in1=p.region0,
                                  op0=ALU.mult, op1=ALU.subtract))
    dve.wait_ge(f.sem, f.at(n[0]))
    done(dve.tensor_scalar(p.t_exw[:, 1:1 + SLOT_TILES], p.t_ex[:], float(E - 1), None, ALU.min))
    done(dve.tensor_reduce(p.t_row[:], p.t_skip, AX.X, ALU.add))
    dve.wait_ge(f.sem, f.at(n[0]))
    done(dve.scalar_tensor_tensor(out=p.tile_row[:], in0=p.iota72, scalar=float(P), in1=p.t_row[:],
                                  op0=ALU.mult, op1=ALU.add))
    four = "p (u j) -> p u j"
    for a in range(2):
        done(dve.tensor_tensor(p.t_pack[:, a], p.t_exw[:, a * TG:a * TG + SLOT_TILES].rearrange(four, j=TG),
                               p.places[:, a * TG:(a + 1) * TG].unsqueeze(1).to_broadcast([P, UNITS, TG]), ALU.mult))
    dve.wait_ge(f.sem, f.at(n[0]))
    for a in range(2):
        done(dve.tensor_reduce(p.t_word[:, a], p.t_pack[:, a], AX.X, ALU.add))
    dve.wait_ge(f.sem, f.at(n[0]))
    done(dve.tensor_tensor(p.word[:], p.t_word[:, 0], p.t_word[:, 1], ALU.add))
    assert n[0] == NFIN


def combine_rows_dve(dve, p):
    c = p.comb_row
    dve.wait_ge(p.fin.sem, p.fin.at(NFIN))
    dve.tensor_tensor(p.c_move, p.sel[:].rearrange("p k t e -> p (k t) e"),
                      p.e_move[:].unsqueeze(1).to_broadcast([P, TOP * NT, E]), ALU.mult).then_inc(c.sem, 1)
    dve.wait_ge(c.sem, c.at(1))
    dve.tensor_reduce(p.c_row[:], p.c_move, AX.X, ALU.add).then_inc(c.sem, 1)
    dve.wait_ge(c.sem, c.at(2))
    dve.tensor_tensor(p.out_row[:].rearrange("p k t -> p (k t)"), p.row[:].rearrange("p k t -> p (k t)"), p.c_row[:],
                      ALU.add).then_inc(c.sem, 1)


def combine_rows_pool(pool, p, g):
    pool.wait_ge(p.comb.sem, p.comb.at(TOP * TG * g))
    pool.sem_inc(p.pool_passed.sem, 1)
    pool.tensor_copy(p.take_row[:], p.out_row[:, :, bass.ds(g * TG, TG)]).then_inc(p.comb_idx.sem, 1)


def combine_pool(pool, p, g, taken, k):
    pool.wait_ge(p.comb_idx.sem, p.comb_idx.at(g + 1))
    pool.sem_inc(p.pool_passed.sem, 1)
    for j in range(TG):
        pool.indirect_dma_start(taken[k][:, j * D:(j + 1) * D], None, p.ys,
                                bass.IndirectOffsetOnAxis(ap=p.take_row[:, k, j:j + 1], axis=0)).then_inc(p.got.sem, 16)


def combine_group_pool(pool, p, g, taken):
    combine_rows_pool(pool, p, g)
    for k in range(TOP):
        combine_pool(pool, p, g, taken, k)


def combine_begin_pool(pool, p, taken):
    for par in range(2):
        pool.wait_ge(p.ystored[par].sem, p.ystored[par].at(0))
    combine_group_pool(pool, p, 0, taken)


def combine_dve(dve, p, g, taken):
    dve.wait_ge(p.got.sem, p.got.at(16 * TOP * TG * (g + 1)))
    for k in range(TOP):
        dve.wait_ge(p.comb.sem, p.comb.at(TG * (TOP * g + k)))
        for j in range(TG):
            x = p.X[:, g * TG + j, :]
            dve.scalar_tensor_tensor(out=x, in0=taken[k][:, j * D:(j + 1) * D], scalar=p.weight[:, bass.ds(g * TG + j, 1), k],
                                     in1=x, op0=ALU.mult, op1=ALU.add).then_inc(p.comb.sem, 1)


def zero_rows_sp(sp, p):
    sp.wait_ge(p.fin.sem, p.fin.at(4))
    for par in range(2):
        sp.wait_ge(p.sent[par].sem, p.sent[par].at(8 * TOP * NT))
    for e in range(E):
        row = sp.value_load(p.zero_row[0:1, e:e + 1], min_val=0, max_val=E * REGION)
        sp.dma_start(p.xs[bass.ds(row, P), :], p.zeros[:]).then_inc(p.zeroed.sem, 16)


def tiles_load_sp(sp, p, k, par, first=False):
    if not first:
        sp.wait_ge(p.xt.sem, p.xt.at(k - 1))
    for j in range(TG):
        row = sp.value_load(p.tile_row[0:1, bass.ds(k * TG + j, 1)], min_val=0, max_val=XS_ROWS - P)
        sp.dma_start(p.slots[:, par, j, :], p.xs[bass.ds(row, P), :]).then_inc(p.loaded[par].sem, 16)


def tiles_store_sp(sp, p, k, par):
    sp.wait_ge(p.pl_u.sem, p.pl_u.at(NU * (k + 1)))
    sp.dma_start(p.ys.rearrange("(t p) d -> p t d", p=P)[:, bass.ds(k * TG, TG), :], p.yo[:, par])\
      .then_inc(p.ystored[par].sem, 16)


STORE_LAG = 6


def moe_sp(sp, p):
    zero_rows_sp(sp, p)
    sp.wait_ge(p.fin.sem, p.fin.at(NFIN))
    sp.wait_ge(p.zeroed.sem, p.zeroed.at(16 * E))
    for k in range(STORE_LAG):
        tiles_load_sp(sp, p, k, k % 2, k < 2)
    with sp.Fori(STORE_LAG // 2, UNITS // 2) as i:
        for m in range(2):
            tiles_load_sp(sp, p, 2 * i + m, m)
            tiles_store_sp(sp, p, 2 * i + m - STORE_LAG, m)
    for k in range(UNITS - STORE_LAG, UNITS):
        tiles_store_sp(sp, p, k, k % 2)


NA, NB, NC = 8, 13, 4
NR, NGT, NU = 2, 2, 2 * TG


def expert_of(word, n):
    return (word >> (BITS * n)) & (E - 1)


def unit_word(eng, p, k):
    return eng.value_load(p.word[0:1, bass.ds(k, 1)], min_val=0, max_val=2 ** (BITS * (TG + 3)) - 1)


def unit_x_pe(pe, p, k, par):
    pe.wait_ge(p.loaded[par].sem, p.loaded[par].at(8 * TG * (k - par + 2)))
    pe.wait_ge(p.xld.sem, p.xld.at(k))
    for j in range(TG):
        ins = pe.transpose(p.bk[6][:, j * P:(j + 1) * P], p.slots[:, par, j, :], p.ident)
    ins.then_inc(p.xt.sem, 1)


def moe_t1(pe, p, k, par, e, j):
    if j == 0:
        pe.wait_ge(p.xld.sem, p.xld.at(k + 1))
    c = slice(j * P, (j + 1) * P)
    out = p.bk[j % 2][:]
    w = bass.ds(e * F, F)
    pe.matmul(out, p.xh[:, par, c], p.w1h[:, w], start=True, stop=False)
    pe.matmul(out, p.xh[:, par, c], p.w1l[:, w], start=False, stop=False)
    pe.matmul(out, p.xl[:, par, c], p.w1h[:, w], start=False, stop=True).then_inc(p.hid.sem, 1)


def moe_t2(pe, p, k, j, first):
    pe.wait_ge(p.act_r.sem, p.act_r.at(4 * k + j + 1))
    if not first or j >= 2:
        pe.wait_ge(p.act_t.sem, p.act_t.at(4 * k + j - 1))
    for c in range(FC):
        ins = pe.transpose(p.bk[2 + j % 2][:, c * P:(c + 1) * P], p.r[:, j, c * P:(c + 1) * P], p.ident)
    ins.then_inc(p.hidT.sem, 1)


def moe_t3(pe, p, k, e, par, j):
    pe.wait_ge(p.act_t.sem, p.act_t.at(4 * k + j + 1))
    for c in range(FC):
        ins = pe.matmul(p.bk[4 + par][:, j * P:(j + 1) * P], p.rT[:, j % 2, c * P:(c + 1) * P],
                        p.w2c[:, bass.ds((e * FC + c) * D, D)], start=(c == 0), stop=(c == FC - 1))
    ins.then_inc(p.outl.sem, 1)


def moe_pe_unit(pe, p, k, par, first=False, ahead=True, last=False):
    word = unit_word(pe, p, k)
    for j in range(TG):
        moe_t2(pe, p, k, j, first and par == 0)
        if j == 0 and not (first and par == 0):
            moe_t3(pe, p, k - 1, expert_of(word, 0), 1 - par, TG - 1)
        if j == 1 and not first:
            pe.wait_ge(p.dve_b.sem, p.dve_b.at(NB * (k - 2) + 4))
        if j >= 1:
            moe_t3(pe, p, k, expert_of(word, j), par, j - 1)
        if j < 2:
            moe_t1(pe, p, k, par, expert_of(word, j + 3), j + 2)
        elif not last:
            moe_t1(pe, p, k + 1, 1 - par, expert_of(word, j + 3), j - 2)
        if j == 0 and ahead:
            unit_x_pe(pe, p, k + 2, par)
    if last:
        moe_t3(pe, p, k, expert_of(word, TG), par, TG - 1)


def moe_experts_pe(pe, p):
    unit_x_pe(pe, p, 0, 0)
    unit_x_pe(pe, p, 1, 1)
    pe.wait_ge(p.fin.sem, p.fin.at(NFIN))
    word = unit_word(pe, p, 0)
    for j in range(2):
        moe_t1(pe, p, 0, 0, expert_of(word, j + 1), j)
    for k in range(2):
        moe_pe_unit(pe, p, k, k, first=True)
    with pe.Fori(1, UNITS // 2 - 1) as i:
        moe_pe_unit(pe, p, 2 * i, 0)
        moe_pe_unit(pe, p, 2 * i + 1, 1)
    moe_pe_unit(pe, p, UNITS - 2, 0, ahead=False)
    moe_pe_unit(pe, p, UNITS - 1, 1, ahead=False, last=True)


def unit_x_high(act, p, k, par):
    act.wait_ge(p.xt.sem, p.xt.at(k + 1))
    act.activation(p.xh[:, par, :], p.bk[6][:], ACT.Copy).then_inc(p.xhd.sem, 1)


def moe_relu(act, p, k, j):
    act.wait_ge(p.hid.sem, p.hid.at(4 * k + j + 1))
    act.activation(p.r[:, j, :], p.bk[j % 2][:], ACT.Relu).then_inc(p.act_r.sem, 1)


def moe_act_unit(act, p, k, par, ahead=True, last=False):
    for j in range(TG):
        act.wait_ge(p.hidT.sem, p.hidT.at(4 * k + j + 1))
        act.activation(p.rT[:, j % 2, :], p.bk[2 + j % 2][:], ACT.Copy).then_inc(p.act_t.sem, 1)
        if j < 2:
            act.wait_ge(p.dve_a.sem, p.dve_a.at(NA * k))
            moe_relu(act, p, k, j + 2)
            if j == 1 and ahead:
                unit_x_high(act, p, k + 2, par)
        elif not last:
            act.wait_ge(p.dve_a.sem, p.dve_a.at(NA * k + j - 1))
            moe_relu(act, p, k + 1, j - 2)


def moe_experts_act(act, p):
    for k in range(2):
        unit_x_high(act, p, k, k)
    for j in range(2):
        moe_relu(act, p, 0, j)
    with act.Fori(0, UNITS // 2 - 1) as i:
        moe_act_unit(act, p, 2 * i, 0)
        moe_act_unit(act, p, 2 * i + 1, 1)
    moe_act_unit(act, p, UNITS - 2, 0, ahead=False)
    moe_act_unit(act, p, UNITS - 1, 1, ahead=False, last=True)


def unit_x_low(dve, p, k, par):
    dve.wait_ge(p.xhd.sem, p.xhd.at(k + 1))
    dve.tensor_tensor(p.xl[:, par, :], p.bk[6][:], f32(p.xh[:, par, :]), ALU.subtract).then_inc(p.xld.sem, 1)


def moe_a(dve, p, k, par):
    for j in range(TG):
        dve.wait_ge(p.act_r.sem, p.act_r.at(4 * k + j + 1))
        dve.bn_stats(p.st1[:, par, j, :], p.r[:, j, :]).then_inc(p.dve_a.sem, 1)
    dve.wait_ge(p.dve_a.sem, p.dve_a.at(NA * k + 4))
    dve.sem_inc(p.dve_passed.sem, 1)
    for j in range(TG):
        dve.bn_aggr(p.mv1[:, par, j, :], p.st1[:, par, j, :]).then_inc(p.dve_a.sem, 1)


def moe_b(dve, p, k, par, first=False):
    word = unit_word(dve, p, k)
    dve.wait_ge(p.outl.sem, p.outl.at(4 * k + 4))
    dve.wait_ge(p.pl_r.sem, p.pl_r.at(NR * k + 2))
    if not first:
        dve.wait_ge(p.pl_u.sem, p.pl_u.at(NU * (k - 1)))
    y = p.y[:, par]
    for j in range(TG):
        dve.scalar_tensor_tensor(out=y[:, j, :], in0=p.bk[4 + par][:, j * P:(j + 1) * P],
                                 scalar=p.rs1[:, par, j:j + 1], in1=p.c2b[:, bass.ds(expert_of(word, j + 1) * D, D)],
                                 op0=ALU.mult, op1=ALU.add).then_inc(p.dve_b.sem, 1)
    dve.wait_ge(p.dve_b.sem, p.dve_b.at(NB * k + 4))
    dve.tensor_scalar(flat(y), flat(y), 0.0, None, ALU.max).then_inc(p.dve_b.sem, 1)
    dve.wait_ge(p.dve_b.sem, p.dve_b.at(NB * k + 5))
    for j in range(TG):
        dve.bn_stats(p.st2[:, j, :], y[:, j, :]).then_inc(p.dve_b.sem, 1)
    dve.wait_ge(p.dve_b.sem, p.dve_b.at(NB * k + 9))
    dve.sem_inc(p.dve_passed.sem, 1)
    for j in range(TG):
        dve.bn_aggr(p.mv2[:, par, j, :], p.st2[:, j, :]).then_inc(p.dve_b.sem, 1)


def moe_c(dve, p, k, par):
    dve.wait_ge(p.pl_g.sem, p.pl_g.at(NGT * k + 2))
    y = p.y[:, par]
    for j in range(TG):
        dve.tensor_scalar(y[:, j, :], y[:, j, :], p.mv2[:, par, j, 0:1], p.rs2[:, par, j:j + 1],
                          ALU.subtract, ALU.mult).then_inc(p.dve_c.sem, 1)


def moe_dve_unit(dve, p, k, par, ahead=True):
    moe_a(dve, p, k, par)
    if ahead:
        unit_x_low(dve, p, k + 2, par)
    moe_b(dve, p, k - 1, 1 - par)
    moe_c(dve, p, k - 2, par)


def moe_experts_dve(dve, p):
    for k in range(2):
        unit_x_low(dve, p, k, k)
    combine_rows_dve(dve, p)
    moe_a(dve, p, 0, 0)
    unit_x_low(dve, p, 2, 0)
    moe_a(dve, p, 1, 1)
    unit_x_low(dve, p, 3, 1)
    moe_b(dve, p, 0, 0, first=True)
    moe_a(dve, p, 2, 0)
    unit_x_low(dve, p, 4, 0)
    moe_b(dve, p, 1, 1, first=True)
    moe_c(dve, p, 0, 0)
    moe_dve_unit(dve, p, 3, 1)
    with dve.Fori(2, UNITS // 2 - 1) as i:
        moe_dve_unit(dve, p, 2 * i, 0)
        moe_dve_unit(dve, p, 2 * i + 1, 1)
    moe_dve_unit(dve, p, UNITS - 2, 0, ahead=False)
    moe_dve_unit(dve, p, UNITS - 1, 1, ahead=False)
    moe_b(dve, p, UNITS - 1, 1)
    moe_c(dve, p, UNITS - 2, 0)
    moe_c(dve, p, UNITS - 1, 1)


def moe_r(pool, p, k, par):
    pool.wait_ge(p.dve_a.sem, p.dve_a.at(NA * k + NA))
    pool.tensor_tensor(p.ve1[:, par, :], p.mv1[:, par, :, 1], p.eps8[:, 0:TG], ALU.add).then_inc(p.pl_r.sem, 1)
    pool.wait_ge(p.pl_r.sem, p.pl_r.at(NR * k + 1))
    pool.tensor_tensor(p.rs1[:, par, :], p.ve1[:, par, :], p.neg_half[:, 0:TG], ALU.pow).then_inc(p.pl_r.sem, 1)


def moe_g(pool, p, k, par):
    pool.wait_ge(p.dve_b.sem, p.dve_b.at(NB * k + NB))
    pool.tensor_tensor(p.ve2[:], p.mv2[:, par, :, 1], p.eps8[:, 0:TG], ALU.add).then_inc(p.pl_g.sem, 1)
    pool.wait_ge(p.pl_g.sem, p.pl_g.at(NGT * k + 1))
    pool.tensor_tensor(p.rs2[:, par, :], p.ve2[:], p.neg_half[:, 0:TG], ALU.pow).then_inc(p.pl_g.sem, 1)


def moe_u(pool, p, k, par, first=False):
    word = unit_word(pool, p, k)
    pool.wait_ge(p.dve_c.sem, p.dve_c.at(NC * k + NC))
    if not first:
        pool.wait_ge(p.ystored[par].sem, p.ystored[par].at(8 * (k - par)))
    for n, table in enumerate((p.g2b, p.be2b)):
        if n:
            pool.wait_ge(p.pl_u.sem, p.pl_u.at(NU * k + TG))
        pool.sem_inc(p.pool_passed.sem, 1)
        for j in range(TG):
            pool.tensor_tensor(p.yo[:, par, j, :], (p.yo if n else p.y)[:, par, j, :],
                               table[:, bass.ds(expert_of(word, j + 1) * D, D)], ALU.add if n else ALU.mult)\
                .then_inc(p.pl_u.sem, 1)


def moe_pool_unit(pool, p, k, par, first=False):
    moe_r(pool, p, k, par)
    moe_g(pool, p, k - 1, 1 - par)
    moe_u(pool, p, k - 2, par, first)


def moe_experts_pool(pool, p):
    moe_r(pool, p, 0, 0)
    moe_r(pool, p, 1, 1)
    moe_g(pool, p, 0, 0)
    for k in range(2, 4):
        moe_pool_unit(pool, p, k, k % 2, first=True)
    with pool.Fori(2, UNITS // 2) as i:
        moe_pool_unit(pool, p, 2 * i, 0)
        moe_pool_unit(pool, p, 2 * i + 1, 1)
    moe_g(pool, p, UNITS - 1, 1)
    moe_u(pool, p, UNITS - 2, 0)
    moe_u(pool, p, UNITS - 1, 1)


def moe_pe_group(pe, p, g, par, weights, last=False):
    route_rank_pe(pe, p, g)
    if not last:
        route_x_pe(pe, p, g + 1, 1 - par, p.xn, E)
    if weights:
        moe_last_row_pe(pe, p, g)
        moe_weights_pe(pe, p, g)


def moe_pe(pe, p, weights):
    route_x_pe(pe, p, 0, 0, p.xn, E)
    with pe.Fori(0, NG // 2 - 1) as i:
        moe_pe_group(pe, p, 2 * i, 0, weights)
        moe_pe_group(pe, p, 2 * i + 1, 1, weights)
    moe_pe_group(pe, p, NG - 2, 0, weights)
    moe_pe_group(pe, p, NG - 1, 1, weights, last=True)
    route_end_pe(pe, p)
    if weights:
        pe.wait_ge(p.wts.sem, p.wts.at(NWT * E))
    moe_experts_pe(pe, p)


def moe_act_group(act, p, g, weights, last=False):
    route_exp_act(act, p, g)
    if not last:
        route_x_act(act, p, g + 1)
    if weights:
        moe_weights_act(act, p, g)


def moe_act(act, p, weights):
    route_x_act(act, p, 0)
    moe_act_group(act, p, 0, weights)
    with act.Fori(1, NG - 1) as g:
        moe_act_group(act, p, g, weights)
    moe_act_group(act, p, NG - 1, weights, last=True)
    moe_experts_act(act, p)


def moe_dve_group(dve, p, g, par, weights, first=False, ahead=2):
    route_top_dve(dve, p, g, E)
    if ahead >= 1:
        route_apply_dve(dve, p, g + 1, 1 - par, p.xn, P - 1, first)
    route_rows_dve(dve, p, g, par)
    if ahead >= 2:
        route_stats_dve(dve, p, g + 2, par)
    route_weights_dve(dve, p, g, TOP)
    if weights:
        moe_weights_dve(dve, p, g)


def moe_dve(dve, p, weights):
    dve.memset(p.counts[:], 0.0).then_inc(p.route_init.sem, 1)
    dve.wait_ge(p.route_init.sem, p.route_init.at(1))
    route_stats_dve(dve, p, 0, 0, True)
    if weights:
        moe_router_weights_dve(dve, p)
        dve.wait_ge(p.xload.sem, p.xload.at(16))
    route_stats_dve(dve, p, 1, 1, True)
    route_apply_dve(dve, p, 0, 0, p.xn, P - 1, True)
    moe_dve_group(dve, p, 0, 0, weights, first=True)
    moe_dve_group(dve, p, 1, 1, weights)
    with dve.Fori(1, NG // 2 - 1) as i:
        moe_dve_group(dve, p, 2 * i, 0, weights)
        moe_dve_group(dve, p, 2 * i + 1, 1, weights)
    moe_dve_group(dve, p, NG - 2, 0, weights, ahead=1)
    moe_dve_group(dve, p, NG - 1, 1, weights, ahead=0)
    if weights:
        c2b = p.c2b[:].rearrange("p (e d) -> p e d", d=D)
        dve.wait_ge(p.wcopy.sem, p.wcopy.at(3 * E))
        dve.tensor_tensor(c2b, c2b, p.c2s, ALU.add).then_inc(p.wshift.sem, 1)
        dve.wait_ge(p.wshift.sem, p.wshift.at(1))
    route_end_dve(dve, p)
    moe_experts_dve(dve, p)


def moe_pool_group(pool, p, g, par, ahead=True):
    route_send_pool(pool, p, g, par, p.xn)
    if ahead:
        route_scale_pool(pool, p, g + 2, par)


def moe_pool(pool, p):
    for g in range(2):
        route_scale_pool(pool, p, g, g)
    with pool.Fori(0, NG // 2 - 1) as i:
        moe_pool_group(pool, p, 2 * i, 0)
        moe_pool_group(pool, p, 2 * i + 1, 1)
    moe_pool_group(pool, p, NG - 2, 0, ahead=False)
    moe_pool_group(pool, p, NG - 1, 1, ahead=False)
    pool.wait_ge(p.dma_norm.sem, p.dma_norm.at(32))
    moe_experts_pool(pool, p)


NWT = 4


def moe_router_weights_dve(dve, p):
    dve.scalar_tensor_tensor(out=p.wr_f, in0=p.wr_last, scalar=p.neg_but_last, in1=p.wr_f,
                             op0=ALU.mult, op1=ALU.add).then_inc(p.wrouter.sem, 1)


def moe_weights_dve(dve, p, e):
    s = p.wts
    f = bass.ds(e * F, F)
    chunks = "p (c d) -> p c d"
    if isinstance(e, int) and e == 0:
        dve.wait_ge(p.dma_first.sem, p.dma_first.at(16 * 2))
    elif isinstance(e, int) and e == 1:
        dve.wait_ge(p.dma_rest.sem, p.dma_rest.at(16 * 3))
    w = p.w2c[:, f].rearrange(chunks, d=D)
    dve.tensor_tensor(w, p.sc[:, f].rearrange(chunks, d=D),
                      p.g1[:, bass.ds(e * FC, FC)].unsqueeze(2).to_broadcast([P, FC, D]), ALU.mult).then_inc(s.sem, 1)
    dve.wait_ge(p.wlast.sem, p.wlast.at(e + 1))
    dve.scalar_tensor_tensor(out=p.sa[:, f], in0=p.bk[1][:], scalar=p.neg_but_last, in1=p.sa[:, f],
                             op0=ALU.mult, op1=ALU.add).then_inc(s.sem, 1)
    dve.wait_ge(s.sem, s.at(NWT * e + 1))
    dve.wait_ge(p.wpe.sem, p.wpe.at(2 * e + 1))
    dve.tensor_tensor(w, w, p.bk[0][:, 0:D].unsqueeze(1).to_broadcast([P, FC, D]), ALU.subtract).then_inc(s.sem, 1)
    dve.wait_ge(p.wcopy.sem, p.wcopy.at(3 * e + 2))
    dve.tensor_tensor(p.w1l[:, f], p.sa[:, f], f32(p.w1h[:, f]), ALU.subtract).then_inc(s.sem, 1)


def moe_weights_act(act, p, e):
    s, f = p.wcopy, bass.ds(e * F, F)
    if isinstance(e, int) and e == 0:
        act.wait_ge(p.dma_tables.sem, p.dma_tables.at(32))
    act.wait_ge(p.wpe.sem, p.wpe.at(2 * e))
    act.activation(p.be1s.rearrange("p (c d) -> p c d", d=D),
                   p.be1[:, bass.ds(e * FC, FC)].unsqueeze(2).to_broadcast([P, FC, D]), ACT.Copy).then_inc(s.sem, 1)
    act.wait_ge(p.wts.sem, p.wts.at(NWT * e + 2))
    act.activation(p.w1h[:, f], p.sa[:, f], ACT.Copy).then_inc(s.sem, 1)
    act.wait_ge(p.wpe.sem, p.wpe.at(2 * e + 2))
    act.activation(p.sc[:, bass.ds(e * F, D)], p.bk[2][:, 0:D], ACT.Copy).then_inc(s.sem, 1)


def moe_last_row_pe(pe, p, e):
    pe.wait_ge(p.wts.sem, p.wts.at(NWT * e))
    pe.matmul(p.bk[1][:], p.ones_1[0:1, :], p.w1_last[:, bass.ds(e * F, F)], start=True, stop=True)\
      .then_inc(p.wlast.sem, 1)


def moe_weights_pe(pe, p, e):
    pe.wait_ge(p.wts.sem, p.wts.at(NWT * e + 1))
    for c in range(FC):
        ins = pe.matmul(p.bk[0][:, 0:D], p.ones_f[:], p.w2c[:, bass.ds((e * FC + c) * D, D)],
                        start=(c == 0), stop=(c == FC - 1))
    ins.then_inc(p.wpe.sem, 1)
    pe.wait_ge(p.wcopy.sem, p.wcopy.at(3 * e + 1))
    for c in range(FC):
        ins = pe.matmul(p.bk[2][:, 0:D], p.be1s[:, c * P:(c + 1) * P], p.sc[:, bass.ds((e * FC + c) * D, D)],
                        start=(c == 0), stop=(c == FC - 1))
    ins.then_inc(p.wpe.sem, 1)


I1, SI = 176, 352
ROWS = E * I1 + SI
NCH = -(-ROWS // P)
HRING = 7
E1 = E + 1
PIECES = [(c, e) for c in range(NCH) for e in range(E1)
          if e * I1 < (c + 1) * P and c * P < (e * I1 + I1 if e < E else ROWS)]
FIRST = {e: min(c for c, x in PIECES if x == e) for e in range(E1)}
LAST = {e: max(c for c, x in PIECES if x == e) for e in range(E1)}
DBANK = [4, 5, 7]


def rows_of(c):
    return slice(c * P, min((c + 1) * P, ROWS))


def sw_gu(pe, p, g, c, par):
    n, rows = NCH * g + c, rows_of(c)
    m = rows.stop - rows.start
    for w_h, w_l, bank, done, freed in ((p.wgh, p.wgl, p.bk[c % 2], p.gt_rows, p.silu_d),
                                        (p.wuh, p.wul, p.bk[2 + c % 2], p.up_rows, p.hid_d)):
        if not isinstance(n, int) or n >= 2:
            pe.wait_ge(freed.sem, freed.at(n - 1))
        pe.matmul(bank[0:m, :], w_h[:, rows], p.xh[:, par, :], start=True, stop=False)
        pe.matmul(bank[0:m, :], w_l[:, rows], p.xh[:, par, :], start=False, stop=False)
        pe.matmul(bank[0:m, :], w_h[:, rows], p.xl[:, par, :], start=False, stop=True).then_inc(done.sem, 1)


def sw_down(pe, p, g, c):
    n, m = NCH * g + c, rows_of(c).stop - c * P
    pe.wait_ge(p.hid_d.sem, p.hid_d.at(n + 1))
    for q, (cc, e) in enumerate(PIECES):
        if cc != c:
            continue
        bank = p.bk[DBANK[e % 3]]
        if c == FIRST[e]:
            pe.wait_ge(p.exp_add.sem, p.exp_add.at(TG * (E1 * g + e - 2) if e >= 2 else TG * E1 * g))
        for j in range(TG):
            ins = pe.matmul(bank[:, j * P:(j + 1) * P], p.hT[0:m, c % HRING, j * P:(j + 1) * P],
                            p.wd[0:m, q * D:(q + 1) * D], start=(c == FIRST[e] and j == 0),
                            stop=(c == LAST[e]), skip_group_check=True)
        if c == LAST[e]:
            ins.then_inc(p.exp_d.sem, 1)


def sw_pe_group(pe, p, g, par, last):
    for c in range(2, NCH):
        sw_gu(pe, p, g, c, par)
        sw_down(pe, p, g, c - 2)
        if c == 3 and not last:
            pe.wait_ge(p.rt2.sem, p.rt2.at(7 * g + 7))
            x_transpose(pe, p, g + 1, p.xf, p.bk[6])
        if c == 7 and not last:
            router_logits(pe, p, g + 1, 1 - par, p.bk[6], p.wr1h[:], p.wr1l[:], NL)
    for c in range(2):
        if not last:
            sw_gu(pe, p, g + 1, c, 1 - par)
        sw_down(pe, p, g, NCH - 2 + c)


def sw_pe(pe, p):
    x_transpose(pe, p, 0, p.xf, p.bk[6])
    router_logits(pe, p, 0, 0, p.bk[6], p.wr1h[:], p.wr1l[:], NL)
    for c in range(2):
        sw_gu(pe, p, 0, c, 0)
    with pe.Fori(0, NG // 2 - 1) as i:
        sw_pe_group(pe, p, 2 * i, 0, False)
        sw_pe_group(pe, p, 2 * i + 1, 1, False)
    sw_pe_group(pe, p, NG - 2, 0, False)
    sw_pe_group(pe, p, NG - 1, 1, True)


def sw_silu(act, p, g, c):
    n, m = NCH * g + c, rows_of(c).stop - c * P
    act.wait_ge(p.gt_rows.sem, p.gt_rows.at(n + 1))
    if not isinstance(n, int) or n >= 2:
        act.wait_ge(p.hid_d.sem, p.hid_d.at(n - 1))
    act.activation(p.sg[0:m, c % 2, :], p.bk[c % 2][0:m, :], ACT.Silu).then_inc(p.silu_d.sem, 1)


def router_shared_exp(act, p, g):
    act.activation(p.rt_g[:], p.rt_l[:, :, E], ACT.Exp, scale=-1.0).then_inc(p.rtg.sem, 1)


def sw_act_group(act, p, g, par, last):
    for c in range(2, NCH):
        sw_silu(act, p, g, c)
        if c == 5 and not last:
            x_high(act, p, g + 1, 1 - par, p.bk[6])
        if c == 10 and not last:
            router_exp(act, p, g + 1)
            router_shared_exp(act, p, g + 1)
    if not last:
        for c in range(2):
            sw_silu(act, p, g + 1, c)


def sw_act(act, p):
    x_high(act, p, 0, 0, p.bk[6])
    router_exp(act, p, 0)
    router_shared_exp(act, p, 0)
    for c in range(2):
        sw_silu(act, p, 0, c)
    with act.Fori(0, NG // 2 - 1) as i:
        sw_act_group(act, p, 2 * i, 0, False)
        sw_act_group(act, p, 2 * i + 1, 1, False)
    sw_act_group(act, p, NG - 2, 0, False)
    sw_act_group(act, p, NG - 1, 1, True)


def router_shared_gate(dve, p, g, gate):
    dve.wait_ge(p.rtg.sem, p.rtg.at(g + 1))
    dve.tensor_scalar(p.rt_g[:], p.rt_g[:], 2.0, 2.0, ALU.mult, ALU.add).then_inc(p.rt3.sem, 1)
    dve.wait_ge(p.rt3.sem, p.rt3.at(2 * g + 1))
    dve.reciprocal(gate[:, :, E], p.rt_g[:]).then_inc(p.rt3.sem, 1)


def sw_product(dve, p, g, c):
    n, m = NCH * g + c, rows_of(c).stop - c * P
    dve.wait_ge(p.silu_d.sem, p.silu_d.at(n + 1))
    dve.wait_ge(p.up_rows.sem, p.up_rows.at(n + 1))
    dve.tensor_tensor(p.hT[0:m, c % HRING, :], p.sg[0:m, c % 2, :], p.bk[2 + c % 2][0:m, :], ALU.mult)\
       .then_inc(p.hid_d.sem, 1)


def sw_add(dve, p, g, e, par):
    n = E1 * g + e
    dve.wait_ge(p.exp_d.sem, p.exp_d.at(n + 1))
    dve.wait_ge(p.exp_add.sem, p.exp_add.at(TG * n))
    if e == 0:
        dve.wait_ge(p.rt2.sem, p.rt2.at(7 * g + 7))
        dve.wait_ge(p.rt3.sem, p.rt3.at(2 * g + 2))
    for j in range(TG):
        x = p.X[:, g * TG + j, :]
        dve.scalar_tensor_tensor(out=x, in0=p.bk[DBANK[e % 3]][:, j * P:(j + 1) * P],
                                 scalar=p.gate1[:, par, j, e:e + 1], in1=x, op0=ALU.mult, op1=ALU.add)\
           .then_inc(p.exp_add.sem, 1)


def sw_router(dve, p, g, par):
    router_top(dve, p, g, p.bk[6], NL)
    router_gate(dve, p, g, p.gate1[:, par], False)
    router_shared_gate(dve, p, g, p.gate1[:, par])


def sw_dve_group(dve, p, g, par, last, after):
    if not last and after:
        combine_dve(dve, p, g + 1, p.sw_taken)
        dve.wait_ge(p.comb.sem, p.comb.at(TOP * TG * (g + 2)))
    if not last:
        ln_stats(dve, p, g + 1)
    for c in range(2, NCH):
        sw_product(dve, p, g, c)
        if c == 2 and not last:
            ln_apply(dve, p, g + 1, p.xf, P)
        if c == 6 and not last:
            x_low(dve, p, g + 1, 1 - par, p.bk[6])
        if c == 10 and not last:
            sw_router(dve, p, g + 1, 1 - par)
        for e in range(E1):
            if LAST[e] == c - 3:
                sw_add(dve, p, g, e, par)
    for c in range(2):
        if not last:
            sw_product(dve, p, g + 1, c)
        for e in range(E1):
            if LAST[e] == NCH - 3 + c:
                sw_add(dve, p, g, e, par)
    sw_add(dve, p, g, E, par)


def sw_dve(dve, p, after):
    if after:
        combine_dve(dve, p, 0, p.sw_taken)
        dve.wait_ge(p.comb.sem, p.comb.at(TOP * TG))
    ln_stats(dve, p, 0)
    ln_apply(dve, p, 0, p.xf, P)
    x_low(dve, p, 0, 0, p.bk[6])
    sw_router(dve, p, 0, 0)
    for c in range(2):
        sw_product(dve, p, 0, c)
    with dve.Fori(0, NG // 2 - 1) as i:
        sw_dve_group(dve, p, 2 * i, 0, False, after)
        sw_dve_group(dve, p, 2 * i + 1, 1, False, after)
    sw_dve_group(dve, p, NG - 2, 0, False, after)
    sw_dve_group(dve, p, NG - 1, 1, True, after)


def sw_pool(pool, p, after):
    if after:
        combine_begin_pool(pool, p, p.sw_taken)
        with pool.Fori(0, NG - 1) as g:
            combine_group_pool(pool, p, g + 1, p.sw_taken)
            ln_scale(pool, p, g)
        ln_scale(pool, p, NG - 1)
    else:
        with pool.Fori(0, NG) as g:
            ln_scale(pool, p, g)


def sw_weights_dve(dve, p):
    dve.wait_ge(p.dma_sw.sem, p.dma_sw.at(48))
    s = p.wsw
    for w, h, l in ((p.sa[:, 0:ROWS], p.wgh, p.wgl), (p.sa[:, ROWS:2 * ROWS], p.wuh, p.wul),
                    (p.wr1_f[:], p.wr1h, p.wr1l)):
        dve.tensor_copy(h[:], w).then_inc(s.sem, 1)
    dve.wait_ge(s.sem, s.at(3))
    for w, h, l in ((p.sa[:, 0:ROWS], p.wgh, p.wgl), (p.sa[:, ROWS:2 * ROWS], p.wuh, p.wul),
                    (p.wr1_f[:], p.wr1h, p.wr1l)):
        dve.tensor_tensor(l[:], w, f32(h[:]), ALU.subtract).then_inc(s.sem, 1)


QK, H, GROUP, MAXREL = 32, 256, 64, 32
NB2 = 2
NQ = 2 * QK


def ga_project_pe(pe, p, b):
    pe.wait_ge(p.ga_xc.sem, p.ga_xc.at(b + 1))
    pe.wait_ge(p.ga_qk.sem, p.ga_qk.at(b))
    pe.matmul(p.bk[0][0:NQ, S:2 * S], p.ga_w[:, 0:NQ], p.ga_xa[:], start=True, stop=True).then_inc(p.ga_qkp.sem, 1)
    pe.wait_ge(p.ga_vg.sem, p.ga_vg.at(NB2 * b))
    for t in range(NB2):
        pe.matmul(p.bk[1 + t][:], p.ga_xa[:, t * P:(t + 1) * P], p.ga_w[:, NQ:], start=True, stop=True)\
          .then_inc(p.ga_vgp.sem, 1)


def ga_swap_pe(pe, p, b):
    pe.wait_ge(p.ga_hd.sem, p.ga_hd.at(2 * b + 2))
    pe.sem_inc(p.pe_passed.sem, 1)
    pe.matmul(p.bk[3][0:NQ, :], p.ga_perm[:], flat(p.ga_h[:]), start=True, stop=True).then_inc(p.ga_sw.sem, 1)


def ga_x_pe(pe, p, b):
    pe.wait_ge(p.ga_xc.sem, p.ga_xc.at(b))
    x_transpose(pe, p, b, p.xn[:, 0], p.bk[0], NB2)


def ga_pe_element(pe, p, b, par, last):
    rp, vg = p.ga_r[:, par], p.ga_v[:, par]
    pe.wait_ge(p.ga_rp.sem, p.ga_rp.at(3 * b + 3))
    pe.wait_ge(p.ga_at.sem, p.ga_at.at(2 * b))
    for t in range(NB2):
        c = slice(t * P, (t + 1) * P)
        ins = pe.matmul(p.bk[5][:, c], rp[0:QK, 1, c], rp[0:QK, 0, c], start=True, stop=True)
    ins.then_inc(p.ga_scp.sem, 1)
    for t in range(NB2):
        ins = pe.transpose(p.bk[6][:, t * NQ:(t + 1) * NQ], rp[:, 1, t * P:(t + 1) * P], p.ident[0:NQ, 0:NQ])
    ins.then_inc(p.ga_lkp.sem, 1)
    if not last:
        ga_x_pe(pe, p, b + 1)
    pe.wait_ge(p.ga_lk.sem, p.ga_lk.at(b + 1))
    pe.wait_ge(p.ga_y.sem, p.ga_y.at(5 * b))
    pe.wait_ge(p.ga_vg.sem, p.ga_vg.at(NB2 * b + NB2))
    for t in range(NB2):
        ins = pe.matmul(p.bk[4][0:NQ, 0:H], p.ga_k[:, t * NQ:(t + 1) * NQ], vg[:, t, 0:H],
                        start=(t == 0), stop=(t == NB2 - 1))
    ins.then_inc(p.ga_kvp.sem, 1)
    if not last:
        ga_project_pe(pe, p, b + 1)
    pe.wait_ge(p.ga_at.sem, p.ga_at.at(2 * b + 2))
    pe.wait_ge(p.ga_kv.sem, p.ga_kv.at(b + 1))
    pe.wait_ge(p.ga_o.sem, p.ga_o.at(b))
    for t in range(NB2):
        o, c = p.bk[6][:, t * H:(t + 1) * H], slice(t * P, (t + 1) * P)
        pe.matmul(o, p.ga_a[:, t, :], vg[:, t, 0:H], start=True, stop=False)
        ins = pe.matmul(o, rp[QK:NQ, 0, c], p.ga_s[QK:NQ, :], start=False, stop=True)
    ins.then_inc(p.ga_op.sem, 1)
    if not last:
        ga_swap_pe(pe, p, b + 1)
    pe.wait_ge(p.ga_o.sem, p.ga_o.at(b + 1))
    pe.wait_ge(p.ga_ot.sem, p.ga_ot.at(b))
    for q in range(NB2 * 2):
        ins = pe.transpose(p.bk[7][:, q * P:(q + 1) * P], p.ga_g[:, q // 2, (q % 2) * P:(q % 2 + 1) * P], p.ident)
    ins.then_inc(p.ga_otp.sem, 1)
    pe.wait_ge(p.ga_ot.sem, p.ga_ot.at(b + 1))
    for t in range(NB2):
        for c in range(2):
            q = t * 2 + c
            ins = pe.matmul(p.bk[4][:, P + t * P:P + (t + 1) * P], p.ga_t[:, q * P:(q + 1) * P],
                            p.ga_wo[:, c * P:(c + 1) * P], start=(c == 0), stop=(c == 1))
    ins.then_inc(p.ga_wop.sem, 1)


def ga_pe(pe, p):
    ga_x_pe(pe, p, 0)
    ga_project_pe(pe, p, 0)
    ga_swap_pe(pe, p, 0)
    with pe.Fori(0, B // 2 - 1) as i:
        ga_pe_element(pe, p, 2 * i, 0, False)
        ga_pe_element(pe, p, 2 * i + 1, 1, False)
    ga_pe_element(pe, p, B - 2, 0, False)
    ga_pe_element(pe, p, B - 1, 1, True)


def ga_x_act(act, p, b):
    act.wait_ge(p.xt.sem, p.xt.at(b + 1))
    act.wait_ge(p.ga_vgp.sem, p.ga_vgp.at(NB2 * b))
    act.activation(p.ga_xa[:], p.bk[0][:, 0:S], ACT.Copy).then_inc(p.ga_xc.sem, 1)


def ga_silu_act(act, p, b, par):
    act.wait_ge(p.ga_qkp.sem, p.ga_qkp.at(b + 1))
    act.wait_ge(p.ga_hd.sem, p.ga_hd.at(2 * b))
    act.activation(p.ga_q[:], p.bk[0][0:NQ, S:2 * S], ACT.Silu).then_inc(p.ga_qk.sem, 1)
    if not isinstance(b, int) or b >= 1:
        act.wait_ge(p.ga_o.sem, p.ga_o.at(b - 1))
    for t in range(NB2):
        act.wait_ge(p.ga_vgp.sem, p.ga_vgp.at(NB2 * b + t + 1))
        act.activation(p.ga_v[:, par, t, :], p.bk[1 + t][:], ACT.Silu).then_inc(p.ga_vg.sem, 1)


def ga_act_element(act, p, b, par, last):
    act.wait_ge(p.ga_lkp.sem, p.ga_lkp.at(b + 1))
    act.activation(p.ga_k[:], p.bk[6][:, 0:P], ACT.Copy).then_inc(p.ga_lk.sem, 1)
    if not last:
        ga_x_act(act, p, b + 1)
    act.wait_ge(p.ga_kvp.sem, p.ga_kvp.at(b + 1))
    act.activation(p.ga_s[:], p.bk[4][0:NQ, 0:H], ACT.Copy, scale=1.0 / S).then_inc(p.ga_kv.sem, 1)
    if not last:
        ga_silu_act(act, p, b + 1, 1 - par)
    act.wait_ge(p.ga_otp.sem, p.ga_otp.at(b + 1))
    act.activation(p.ga_t[:], p.bk[7][:], ACT.Copy).then_inc(p.ga_ot.sem, 1)


def ga_act(act, p):
    ga_x_act(act, p, 0)
    ga_silu_act(act, p, 0, 0)
    with act.Fori(0, B // 2 - 1) as i:
        ga_act_element(act, p, 2 * i, 0, False)
        ga_act_element(act, p, 2 * i + 1, 1, False)
    ga_act_element(act, p, B - 2, 0, False)
    ga_act_element(act, p, B - 1, 1, True)


def ga_heads_dve(dve, p, b):
    dve.wait_ge(p.ga_qk.sem, p.ga_qk.at(b + 1))
    dve.wait_ge(p.ga_sw.sem, p.ga_sw.at(b))
    for n in range(2):
        dve.tensor_scalar(p.ga_h[:, n, :], p.ga_q[:], p.ga_gb[:, 2 * n:2 * n + 1], p.ga_gb[:, 2 * n + 1:2 * n + 2],
                          ALU.mult, ALU.add).then_inc(p.ga_hd.sem, 1)


def ga_rope_dve(dve, p, b, par):
    def table(t):
        return t[:].unsqueeze(1).to_broadcast([NQ, 2, S])
    dve.wait_ge(p.ga_hd.sem, p.ga_hd.at(2 * b + 2))
    dve.tensor_tensor(p.ga_r1[:], p.ga_h[:], table(p.ga_cos), ALU.mult).then_inc(p.ga_rp.sem, 1)
    dve.wait_ge(p.ga_sw.sem, p.ga_sw.at(b + 1))
    dve.tensor_tensor(p.ga_r2[:], p.bk[3][0:NQ, :].rearrange("p (a s) -> p a s", a=2), table(p.ga_sin), ALU.mult)\
       .then_inc(p.ga_rp.sem, 1)
    dve.wait_ge(p.ga_rp.sem, p.ga_rp.at(3 * b + 2))
    dve.tensor_tensor(p.ga_r[:, par], p.ga_r1[:], p.ga_r2[:], ALU.add).then_inc(p.ga_rp.sem, 1)


def ga_dve_pair(dve, p, i, last=False):
    if not last:
        combine_dve(dve, p, i + 1, p.ga_taken)
        dve.wait_ge(p.comb.sem, p.comb.at(TOP * TG * (i + 2)))
    ga_dve_element(dve, p, 2 * i, 0, False, not last)
    ga_dve_element(dve, p, 2 * i + 1, 1, last, not last)


def ga_dve_element(dve, p, b, par, last, more):
    if not last:
        ln_apply(dve, p, b + 1, p.xn[:, 0], P - 1, NB2, True)
    dve.wait_ge(p.ga_scp.sem, p.ga_scp.at(b + 1))
    dve.scalar_tensor_tensor(out=p.ga_a1[:], in0=p.bk[5][:, 0:S].rearrange("p (t k) -> p t k", t=NB2),
                             scalar=1.0 / GROUP, in1=p.ga_bias[:].unsqueeze(1).to_broadcast([P, NB2, P]),
                             op0=ALU.mult, op1=ALU.add).then_inc(p.ga_at.sem, 1)
    dve.wait_ge(p.ga_at.sem, p.ga_at.at(2 * b + 1))
    dve.scalar_tensor_tensor(out=p.ga_a[:], in0=p.ga_a1[:], scalar=0.0, in1=p.ga_a1[:],
                             op0=ALU.max, op1=ALU.mult).then_inc(p.ga_at.sem, 1)
    if not last:
        ga_heads_dve(dve, p, b + 1)
    dve.wait_ge(p.ga_op.sem, p.ga_op.at(b + 1))
    dve.wait_ge(p.ga_otp.sem, p.ga_otp.at(b))
    dve.tensor_tensor(p.ga_g[:], p.bk[6][:].rearrange("p (t h) -> p t h", t=NB2), p.ga_v[:, par, :, H:], ALU.mult)\
       .then_inc(p.ga_o.sem, 1)
    if not last:
        ga_rope_dve(dve, p, b + 1, 1 - par)
    dve.wait_ge(p.ga_wop.sem, p.ga_wop.at(b + 1))
    dve.wait_ge(p.ga_px.sem, p.ga_px.at(3 * b))
    dve.tensor_tensor(p.ga_yy[:], p.bk[4][:, P:3 * P].rearrange("p (t d) -> p t d", t=NB2),
                      p.ga_bo[:].unsqueeze(1).to_broadcast([P, NB2, D]), ALU.add).then_inc(p.ga_y.sem, 1)
    dve.wait_ge(p.ga_y.sem, p.ga_y.at(5 * b + 1))
    for t in range(NB2):
        dve.bn_stats(p.ga_st[:, t, :], p.ga_yy[:, t, :]).then_inc(p.ga_y.sem, 1)
    dve.wait_ge(p.ga_y.sem, p.ga_y.at(5 * b + 3))
    dve.sem_inc(p.dve_passed.sem, 1)
    for t in range(NB2):
        dve.bn_aggr(p.ga_mv[:, t, :], p.ga_st[:, t, :]).then_inc(p.ga_y.sem, 1)
    if more:
        ln_stats(dve, p, b + 2, NB2)
    dve.wait_ge(p.ga_rs.sem, p.ga_rs.at(2 * b + 2))
    for t in range(NB2):
        ins = dve.tensor_scalar(p.ga_yy[:, t, :], p.ga_yy[:, t, :], p.ga_mv[:, t, 0:1], p.ga_sc[:, t:t + 1],
                                ALU.subtract, ALU.mult)
    ins.then_inc(p.ga_yn.sem, 1)


def ga_dve(dve, p):
    combine_dve(dve, p, 0, p.ga_taken)
    dve.wait_ge(p.comb.sem, p.comb.at(TOP * TG))
    ln_stats(dve, p, 0, NB2)
    ln_apply(dve, p, 0, p.xn[:, 0], P - 1, NB2, True)
    ln_stats(dve, p, 1, NB2)
    ga_heads_dve(dve, p, 0)
    ga_rope_dve(dve, p, 0, 0)
    with dve.Fori(0, B // 2 - 1) as i:
        ga_dve_pair(dve, p, i)
    ga_dve_pair(dve, p, B // 2 - 1, last=True)


def ga_pool_element(pool, p, b, more):
    pool.wait_ge(p.ga_y.sem, p.ga_y.at(5 * b + 5))
    pool.tensor_tensor(p.ga_ve[:], p.ga_mv[:, :, 1], p.eps8[:, 0:NB2], ALU.add).then_inc(p.ga_rs.sem, 1)
    pool.wait_ge(p.ga_rs.sem, p.ga_rs.at(2 * b + 1))
    pool.tensor_tensor(p.ga_sc[:], p.ga_ve[:], p.neg_half[:, 0:NB2], ALU.pow).then_inc(p.ga_rs.sem, 1)
    if more:
        ln_scale(pool, p, b + 2, NB2, True)
    x = p.X[:, bass.ds(b * NB2, NB2), :]
    pool.wait_ge(p.ga_yn.sem, p.ga_yn.at(b + 1))
    pool.tensor_tensor(p.ga_z[:], p.ga_yy[:], p.ga_w2[:].unsqueeze(1).to_broadcast([P, NB2, D]), ALU.mult)\
        .then_inc(p.ga_px.sem, 1)
    pool.tensor_tensor(x, x, p.ga_b2[:].unsqueeze(1).to_broadcast([P, NB2, D]), ALU.add).then_inc(p.ga_px.sem, 1)
    pool.wait_ge(p.ga_px.sem, p.ga_px.at(3 * b + 2))
    pool.sem_inc(p.pool_passed.sem, 1)
    pool.tensor_tensor(x, x, p.ga_z[:], ALU.add).then_inc(p.ga_px.sem, 1)


def ga_pool_pair(pool, p, i, ahead=True, more=True):
    if ahead:
        combine_rows_pool(pool, p, i + 2)
    for k in range(TOP):
        if ahead:
            combine_pool(pool, p, i + 2, p.ga_taken, k)
        ga_pool_element(pool, p, 2 * i + k, more)


def ga_pool(pool, p):
    combine_begin_pool(pool, p, p.ga_taken)
    combine_group_pool(pool, p, 1, p.ga_taken)
    ln_scale(pool, p, 0, NB2, True)
    ln_scale(pool, p, 1, NB2, True)
    with pool.Fori(0, NG - 2) as i:
        ga_pool_pair(pool, p, i)
    ga_pool_pair(pool, p, NG - 2, ahead=False)
    ga_pool_pair(pool, p, NG - 1, ahead=False, more=False)


def ga_bias_pool(pool, p):
    pool.wait_ge(p.dma_ga.sem, p.dma_ga.at(p.nga))
    pool.tensor_tensor(p.ga_bias[:], p.ga_bias[:], p.ga_mask[:], ALU.add).then_inc(p.gab.sem, 1)


def ga_weights_pe(pe, p):
    pe.wait_ge(p.dma_ga.sem, p.dma_ga.at(p.nga))
    for n, c in enumerate((slice(0, NQ), slice(NQ, NQ + 2 * H))):
        out = p.bk[n][:, 0:c.stop - c.start]
        pe.matmul(out, p.ga_ln_b[:], p.ga_w[:, c], start=True, stop=False)
        ins = pe.matmul(out, p.e_last[:], p.ga_brow[:, c], start=False, stop=True)
    ins.then_inc(p.gaw.sem, 1)
    pe.wait_ge(p.gaw.sem, p.gaw.at(6))


def ga_weights_dve(dve, p):
    dve.wait_ge(p.dma_ga.sem, p.dma_ga.at(p.nga))
    dve.wait_ge(p.gaw.sem, p.gaw.at(1))
    dve.tensor_scalar(p.ga_w[:], p.ga_w[:], p.ga_ln_w[:, 0:1], None, ALU.mult).then_inc(p.gaw.sem, 1)
    dve.tensor_scalar(p.ga_last[:], p.ga_last[:], p.ga_ln_w[:, 1:2], None, ALU.mult).then_inc(p.gaw.sem, 1)
    dve.wait_ge(p.gaw.sem, p.gaw.at(3))
    dve.tensor_tensor(p.ga_w[:], p.ga_w[:], p.ga_last[:], ALU.subtract).then_inc(p.gaw.sem, 1)
    dve.wait_ge(p.gaw.sem, p.gaw.at(4))
    dve.tensor_tensor(p.ga_w[:, 0:NQ], p.ga_w[:, 0:NQ], p.bk[0][:, 0:NQ], ALU.add).then_inc(p.gaw.sem, 1)
    dve.tensor_tensor(p.ga_w[:, NQ:], p.ga_w[:, NQ:], p.bk[1][:], ALU.add).then_inc(p.gaw.sem, 1)


NH, HD = 16, 8
HR = 32
HQ = P // HR
NHQ = NH // HQ
NPROD = 3 * HD
LATENT = 64
ATT_SCALE = 1.0 / float(np.sqrt(NH + 2 * LATENT))
NS1 = 12


def at_x_pe(pe, p, b):
    pe.wait_ge(p.at_kr.sem, p.at_kr.at(b))
    x_transpose(pe, p, b, p.xn[:, 0], p.bk[0], NB2)


def at_latent_pe(pe, p, b):
    pe.wait_ge(p.at_xc.sem, p.at_xc.at(b + 1))
    pe.matmul(p.bk[0][:, S:2 * S], p.at_w[:, 0:P], p.at_xa[:], start=True, stop=True).then_inc(p.at_ctp.sem, 1)


def at_project_pe(pe, p, b):
    pe.wait_ge(p.at_ct.sem, p.at_ct.at(b + 1))
    for t in range(NB2):
        c = slice(t * P, (t + 1) * P)
        ins = pe.matmul(p.bk[0][:, c], p.at_xa[:, c], p.at_w[:, P:2 * P], start=True, stop=True)
    ins.then_inc(p.at_krp.sem, 1)
    pe.wait_ge(p.at_qt.sem, p.at_qt.at(NB2 * b))
    for n in range(2):
        r = slice(n * LATENT, (n + 1) * LATENT)
        for t in range(NB2):
            ins = pe.matmul(p.bk[1 + n][:, 2 * t * D:2 * (t + 1) * D], p.at_c[r, t * P:(t + 1) * P], p.at_u[r, :],
                            start=True, stop=True)
        ins.then_inc(p.at_prp.sem, 1)


def at_turn_pe(pe, p, t, which, bank):
    for q in range(NHQ):
        src = p.at_sk[:, which, t, q * HQ:(q + 1) * HQ, :].rearrange("p h r -> p (h r)")
        ins = pe.transpose(bank[:, q * P:(q + 1) * P], src, p.ident)
    return ins


def at_keys_pe(pe, p, b):
    pe.wait_ge(p.at_q.sem, p.at_q.at(NS1 * b + NS1))
    pe.wait_ge(p.at_hc.sem, p.at_hc.at(2 * b + 2))
    for t in range(NB2):
        at_turn_pe(pe, p, t, 1, p.bk[1 + t]).then_inc(p.at_ktp.sem, 1)


def at_queries_pe(pe, p, b):
    for t in range(NB2):
        pe.wait_ge(p.at_kt.sem, p.at_kt.at(NB2 * b + t + 1))
        at_turn_pe(pe, p, t, 0, p.bk[1 + t]).then_inc(p.at_qtp.sem, 1)


def head_rows(h, n):
    return slice(HR * (h % HQ), HR * (h % HQ) + n)


def at_pe_element(pe, p, b, par, last):
    pe.wait_ge(p.at_qt.sem, p.at_qt.at(NB2 * b + NB2))
    pe.wait_ge(p.at_x.sem, p.at_x.at(b))
    for f in range(NH):
        t, pair = divmod(f, NH // 2)
        if f >= 4:
            pe.wait_ge(p.at_mx.sem, p.at_mx.at(NH * b + f - 3))
        for n in range(2):
            h = pair % HQ + HQ * (2 * (pair // HQ) + n)
            r = head_rows(h, NPROD)
            ins = pe.matmul(p.bk[3 + f % 4][:, n * S:(n + 1) * S], p.at_qT[r, h // HQ, t * P:(t + 1) * P],
                            p.at_kT[par][r, h // HQ, :], start=True, stop=True)
        ins.then_inc(p.at_s1.sem, 1)
        if f == 8 and not last:
            at_x_pe(pe, p, b + 1)
    pe.wait_ge(p.at_nm.sem, p.at_nm.at(2 * b + 2))
    for t in range(NB2):
        at_turn_pe(pe, p, t, 0, p.bk[3 + t]).then_inc(p.at_q2p.sem, 1)
    if not last:
        at_latent_pe(pe, p, b + 1)
    pe.wait_ge(p.at_q2.sem, p.at_q2.at(NB2 * b + NB2))
    for h in range(NH + 2):
        if h < NH:
            if h >= 4:
                pe.wait_ge(p.at_ex.sem, p.at_ex.at(NH * b + h - 3))
            r = head_rows(h, NPROD + 2)
            for t in range(NB2):
                ins = pe.matmul(p.bk[3 + (h + 2) % 4][:, t * S:(t + 1) * S],
                                p.at_kT[par][r, h // HQ, t * P:(t + 1) * P], p.at_qT2[r, h // HQ, :],
                                start=True, stop=True)
            ins.then_inc(p.at_s2.sem, 1)
        if h >= 2:
            a = h - 2
            pe.wait_ge(p.at_ex.sem, p.at_ex.at(NH * b + a + 1))
            if a % 8 == 0:
                pe.wait_ge(p.at_op.sem, p.at_op.at(2 * b + a // 8))
            o = p.bk[7][HR * (a % HQ):HR * (a % HQ + 1), (a // HQ) % 2 * S:((a // HQ) % 2 + 1) * S]
            for t in range(NB2):
                ins = pe.matmul(o, p.at_v[:, par, t, a, :], p.at_e[:, a % 4, t * S:(t + 1) * S],
                                start=(t == 0), stop=(t == NB2 - 1))
            ins.then_inc(p.at_av.sem, 1)
        if not last:
            if h == 2:
                at_project_pe(pe, p, b + 1)
            if h == 12:
                at_keys_pe(pe, p, b + 1)
            if h == 15:
                at_queries_pe(pe, p, b + 1)
    pe.wait_ge(p.at_op.sem, p.at_op.at(2 * b + 2))
    for t in range(NB2):
        for q in range(NHQ):
            ins = pe.transpose(p.bk[3 + t][:, q * P:(q + 1) * P], p.at_o[:, q, t * P:(t + 1) * P], p.ident)
    ins.then_inc(p.at_otp.sem, 1)
    pe.wait_ge(p.at_on.sem, p.at_on.at(4 * b + 4))
    for t in range(NB2):
        ins = pe.transpose(p.bk[5][:, t * P:(t + 1) * P], p.at_n[:, t, :], p.ident)
    ins.then_inc(p.at_tp.sem, 1)
    pe.wait_ge(p.at_ot.sem, p.at_ot.at(b + 1))
    for t in range(NB2):
        c = slice(t * P, (t + 1) * P)
        ins = pe.matmul(p.bk[6][:, c], p.at_t[:, c], p.at_wo, start=True, stop=True)
    ins.then_inc(p.at_wp.sem, 1)


def at_pe(pe, p):
    pe.wait_ge(p.at_init.sem, p.at_init.at(5))
    at_x_pe(pe, p, 0)
    at_latent_pe(pe, p, 0)
    at_project_pe(pe, p, 0)
    at_keys_pe(pe, p, 0)
    at_queries_pe(pe, p, 0)
    with pe.Fori(0, B // 2 - 1) as i:
        at_pe_element(pe, p, 2 * i, 0, False)
        at_pe_element(pe, p, 2 * i + 1, 1, False)
    at_pe_element(pe, p, B - 2, 0, False)
    at_pe_element(pe, p, B - 1, 1, True)


def at_x_act(act, p, b):
    act.wait_ge(p.xt.sem, p.xt.at(b + 1))
    act.wait_ge(p.at_prp.sem, p.at_prp.at(NB2 * b))
    act.activation(p.at_xa[:], p.bk[0][:, 0:S], ACT.Copy).then_inc(p.at_xc.sem, 1)


def at_latent_act(act, p, b):
    act.wait_ge(p.at_ctp.sem, p.at_ctp.at(b + 1))
    act.activation(p.at_c[:], p.bk[0][:, S:2 * S], ACT.Copy).then_inc(p.at_ct.sem, 1)


def at_kr_act(act, p, b):
    act.wait_ge(p.at_krp.sem, p.at_krp.at(b + 1))
    act.wait_ge(p.at_q.sem, p.at_q.at(NS1 * b))
    act.activation(p.at_r[:, 1], p.bk[0][:, 0:S].rearrange("p (t d) -> p t d", t=NB2), ACT.Copy)\
       .then_inc(p.at_kr.sem, 1)


def at_parts_act(act, p, b):
    act.wait_ge(p.at_q.sem, p.at_q.at(NS1 * b + 10))
    for which, c in ((0, HD), (1, 2 * HD)):
        act.activation(p.at_sk_r[:, which, :, :, c:c + HD], p.at_sk[:, which, :, :, 0:HD], ACT.Copy)\
           .then_inc(p.at_hc.sem, 1)


def at_turned_act(act, src, dst, t):
    return act.activation(dst[:, :, t * P:(t + 1) * P], src[:].rearrange("p (q t) -> p q t", q=NHQ), ACT.Copy)


def at_keys_act(act, p, b, par):
    for t in range(NB2):
        act.wait_ge(p.at_ktp.sem, p.at_ktp.at(NB2 * b + t + 1))
        at_turned_act(act, p.bk[1 + t], p.at_kT[par], t).then_inc(p.at_kt.sem, 1)


def at_queries_act(act, p, b):
    for t in range(NB2):
        act.wait_ge(p.at_qtp.sem, p.at_qtp.at(NB2 * b + t + 1))
        at_turned_act(act, p.bk[1 + t], p.at_qT, t).then_inc(p.at_qt.sem, 1)


def at_act_element(act, p, b, par, last):
    if not last:
        at_x_act(act, p, b + 1)
    for t in range(NB2):
        act.wait_ge(p.at_q2p.sem, p.at_q2p.at(NB2 * b + t + 1))
        at_turned_act(act, p.bk[3 + t], p.at_qT2, t).then_inc(p.at_q2.sem, 1)
    if not last:
        at_latent_act(act, p, b + 1)
    for h in range(NH):
        act.wait_ge(p.at_s2.sem, p.at_s2.at(NH * b + h + 1))
        if h >= 4:
            act.wait_ge(p.at_av.sem, p.at_av.at(NH * b + h - 3))
        act.activation(p.at_e[:, h % 4, :], p.bk[3 + (h + 2) % 4][:], ACT.Exp, scale=ATT_SCALE)\
           .then_inc(p.at_ex.sem, 1)
        if not last:
            if h == 3:
                at_kr_act(act, p, b + 1)
            if h == 10:
                at_parts_act(act, p, b + 1)
            if h == 13:
                at_keys_act(act, p, b + 1, 1 - par)
    if not last:
        at_queries_act(act, p, b + 1)
    act.wait_ge(p.at_tp.sem, p.at_tp.at(b + 1))
    act.activation(p.at_t[:], p.bk[5][:, 0:S], ACT.Copy).then_inc(p.at_ot.sem, 1)


def at_act(act, p):
    act.wait_ge(p.at_init.sem, p.at_init.at(5))
    at_x_act(act, p, 0)
    at_latent_act(act, p, 0)
    at_kr_act(act, p, 0)
    at_parts_act(act, p, 0)
    at_keys_act(act, p, 0, 0)
    at_queries_act(act, p, 0)
    with act.Fori(0, B // 2 - 1) as i:
        at_act_element(act, p, 2 * i, 0, False)
        at_act_element(act, p, 2 * i + 1, 1, False)
    at_act_element(act, p, B - 2, 0, False)
    at_act_element(act, p, B - 1, 1, True)


def at_project_dve(dve, p, b, par):
    n = NS1 * b
    heads = "p t (h d) -> p t h d"
    for m, dst in ((0, p.at_r[:, 0]), (1, p.at_s[:, 0]), (2, p.at_s[:, 1]), (3, p.at_v[:, par, :, :, 0:HD])):
        dve.wait_ge(p.at_prp.sem, p.at_prp.at(2 * b + m // 2 + 1))
        src = p.bk[1 + m // 2][:].rearrange("p (t d) -> p t d", t=NB2)[:, :, (m % 2) * D:(m % 2 + 1) * D]
        bias = p.at_b[:, m * D:(m + 1) * D].unsqueeze(1).to_broadcast([P, NB2, D])
        if m == 3:
            src, bias = src.rearrange(heads, d=HD), bias.rearrange(heads, d=HD)
        dve.tensor_tensor(dst, src, bias, ALU.add).then_inc(p.at_q.sem, 1)
    dve.wait_ge(p.at_kr.sem, p.at_kr.at(b + 1))
    dve.wait_ge(p.at_q.sem, p.at_q.at(n + 4))
    r, t1, t2 = (x.rearrange("p w t d -> p w (t d)") for x in (p.at_r, p.at_t1, p.at_t2))
    pairs = "p w (i two) -> p w i two"
    rp, tp = r.rearrange(pairs, two=2), t2.rearrange(pairs, two=2)
    dve.tensor_tensor(t1, r, p.at_cos.unsqueeze(1).to_broadcast([P, 2, S]), ALU.mult).then_inc(p.at_q.sem, 1)
    for k in range(2):
        sin = p.at_sin[:, k, :].unsqueeze(1).to_broadcast([P, 2, S // 2])
        dve.tensor_tensor(tp[:, :, :, k], rp[:, :, :, 1 - k], sin, ALU.mult).then_inc(p.at_q.sem, 1)
    dve.wait_ge(p.at_q.sem, p.at_q.at(n + 7))
    dve.tensor_tensor(t1, t1, t2, ALU.add).then_inc(p.at_q.sem, 1)
    dve.wait_ge(p.at_q.sem, p.at_q.at(n + 8))
    dve.tensor_tensor(t1, t1, p.at_s.rearrange("p w t d -> p w (t d)"), ALU.add).then_inc(p.at_q.sem, 1)
    dve.wait_ge(p.at_q.sem, p.at_q.at(n + 9))
    dve.wait_ge(p.at_q2p.sem, p.at_q2p.at(NB2 * b))
    qk = p.at_t1.rearrange("p w t (h d) -> p w t h d", d=HD)
    dve.tensor_copy(p.at_sk_r.rearrange("p w t h r -> p (w t h) r")[:, :, 0:HD],
                    p.at_t1.rearrange("p w t (h d) -> p (w t h) d", d=HD)).then_inc(p.at_q.sem, 1)
    dve.wait_ge(p.at_q.sem, p.at_q.at(n + 10))
    for which, c in ((0, 2 * HD), (1, HD)):
        dve.tensor_tensor(p.at_sk_r[:, which, :, :, c:c + HD], qk[:, which], p.at_sk[:, which, :, :, 0:HD],
                          ALU.subtract).then_inc(p.at_q.sem, 1)


def at_dve_element(dve, p, b, par, last, more):
    if not last:
        ln_apply(dve, p, b + 1, p.xn[:, 0], P - 1, NB2)
    for f in range(NH):
        t, pair = divmod(f, NH // 2)
        dve.wait_ge(p.at_s1.sem, p.at_s1.at(NH * b + f + 1))
        q = 2 * (pair // HQ)
        dve.tensor_reduce(p.at_m[:, t, :].rearrange("p (q r) -> p q r", r=HQ)[:, q:q + 2, pair % HQ], p.bk[3 + f % 4][:].rearrange("p (h k) -> p h k", h=2),
                          AX.X, ALU.max, negate=True).then_inc(p.at_mx.sem, 1)
    dve.wait_ge(p.at_mx.sem, p.at_mx.at(NH * b + NH))
    dve.tensor_copy(p.at_sk_r[:, 0, :, :, NPROD], p.at_m[:]).then_inc(p.at_nm.sem, 1)
    dve.wait_ge(p.at_nm.sem, p.at_nm.at(2 * b + 1))
    dve.tensor_tensor(p.at_sk_r[:, 0, :, :, NPROD + 1], p.at_m[:], p.at_sk[:, 0, :, :, NPROD], ALU.subtract)\
       .then_inc(p.at_nm.sem, 1)
    if not last:
        at_project_dve(dve, p, b + 1, 1 - par)
    for half in range(2):
        dve.wait_ge(p.at_av.sem, p.at_av.at(NH * b + 8 * half + 8))
        dve.tensor_copy(p.at_o[:, 2 * half:2 * half + 2, :], p.bk[7][:].rearrange("p (q s) -> p q s", q=2))\
           .then_inc(p.at_op.sem, 1)
    x = p.X[:, bass.ds(b * NB2, NB2), :]
    dve.tensor_tensor(x, x, p.at_bo.unsqueeze(1).to_broadcast([P, NB2, D]), ALU.add).then_inc(p.at_x1.sem, 1)
    if more:
        ln_stats(dve, p, b + 2, NB2)
    dve.wait_ge(p.at_otp.sem, p.at_otp.at(b + 1))
    for t in range(NB2):
        o = p.bk[3 + t][:].rearrange("p (h r) -> p h r", r=HR)
        dve.reciprocal(p.at_rc[:, t, :], o[:, :, HD]).then_inc(p.at_on.sem, 1)
    dve.wait_ge(p.at_on.sem, p.at_on.at(4 * b + 2))
    for t in range(NB2):
        o = p.bk[3 + t][:].rearrange("p (h r) -> p h r", r=HR)
        dve.tensor_tensor(p.at_n[:, t, :].rearrange("p (h d) -> p h d", d=HD), o[:, :, 0:HD],
                          p.at_rc[:, t, :].unsqueeze(2).to_broadcast([P, NH, HD]), ALU.mult).then_inc(p.at_on.sem, 1)
    dve.wait_ge(p.at_wp.sem, p.at_wp.at(b + 1))
    dve.wait_ge(p.at_x1.sem, p.at_x1.at(b + 1))
    dve.tensor_tensor(x, x, p.bk[6][:, 0:S].rearrange("p (t d) -> p t d", t=NB2), ALU.add).then_inc(p.at_x.sem, 1)


def at_dve(dve, p):
    dve.wait_ge(p.at_init.sem, p.at_init.at(5))
    ln_stats(dve, p, 0, NB2)
    ln_apply(dve, p, 0, p.xn[:, 0], P - 1, NB2)
    ln_stats(dve, p, 1, NB2)
    at_project_dve(dve, p, 0, 0)
    with dve.Fori(0, B // 2 - 1) as i:
        at_dve_element(dve, p, 2 * i, 0, False, True)
        at_dve_element(dve, p, 2 * i + 1, 1, False, True)
    at_dve_element(dve, p, B - 2, 0, False, False)
    at_dve_element(dve, p, B - 1, 1, True, False)


def at_pool(pool, p):
    pool.memset(p.at_sk[:], 0.0).then_inc(p.at_init.sem, 1)
    pool.memset(p.at_v[:], 0.0).then_inc(p.at_init.sem, 1)
    pool.wait_ge(p.at_init.sem, p.at_init.at(2))
    pool.memset(p.at_sk[:, 1, :, :, NPROD:NPROD + 2], 1.0).then_inc(p.at_init.sem, 1)
    for par in range(2):
        pool.memset(p.at_v[:, par, :, :, HD], 1.0).then_inc(p.at_init.sem, 1)
    with pool.Fori(0, B) as b:
        ln_scale(pool, p, b, NB2)


def at_weights_dve(dve, p):
    dve.wait_ge(p.dma_at.sem, p.dma_at.at(p.nat))
    dve.scalar_tensor_tensor(out=p.at_w, in0=p.at_last, scalar=p.neg_but_last, in1=p.at_w,
                             op0=ALU.mult, op1=ALU.add).then_inc(p.atw.sem, 1)


ENGINES = 4
_PREP = dict(ln_free=NG, ln_stat=2 * NT, ln_rs=2 * NG, xt=NG, xhd=NG, xld=NG, lg=NG, rt1=10 * NG, rt2=7 * NG, rte=NG)
_ROUTE = dict(ln_free=NG, ln_stat=2 * NT, ln_rs=2 * NG, route_init=1, route_xt=NG, route_xc=NG, route_lg=NG,
              route_top=10 * NG, route_e=NG, route_sel=3 * NG, route_pos=NG, route_cnt=2 * NG, route_row=4 * NG,
              route_w=3 * NG, sent_even=8 * TOP * NT, sent_odd=8 * TOP * NT, route_n=1, fin=NFIN, zeroed=16 * E,
              loaded_even=8 * SLOT_TILES, loaded_odd=8 * SLOT_TILES, ystored_even=8 * UNITS, ystored_odd=8 * UNITS,
              comb_row=3,
              xt=UNITS, xhd=UNITS, xld=UNITS)
_COMB = dict(comb_idx=NG, got=16 * TOP * NT, comb=TOP * NT)
USES = {
    "moe": dict(_ROUTE, act_r=4 * UNITS, act_t=4 * UNITS, hid=4 * UNITS, hidT=4 * UNITS, outl=4 * UNITS,
                dve_a=NA * UNITS, dve_b=NB * UNITS, dve_c=NC * UNITS, pl_r=NR * UNITS, pl_g=NGT * UNITS,
                pl_u=NU * UNITS),
    "gau": dict(_COMB, ln_free=B, ln_stat=2 * NT, ln_rs=6 * B, xt=B, ln_both=B, ga_xc=B, ga_qk=B, ga_qkp=B, ga_vg=2 * B,
                ga_vgp=2 * B, ga_hd=2 * B, ga_sw=B, ga_rp=3 * B, ga_lk=B, ga_lkp=B, ga_scp=B, ga_at=2 * B, ga_kv=B,
                ga_kvp=B, ga_o=B, ga_op=B, ga_ot=B, ga_otp=B, ga_y=5 * B, ga_wop=B, ga_rs=2 * B, ga_yn=B, ga_px=3 * B),
    "mla": dict(ln_free=B, ln_stat=2 * NT, ln_rs=2 * B, xt=B, at_xc=B, at_ctp=B, at_ct=B, at_krp=B, at_kr=B,
                at_prp=2 * B, at_q=NS1 * B, at_hc=2 * B, at_ktp=2 * B, at_kt=2 * B, at_qtp=2 * B, at_qt=2 * B,
                at_s1=NH * B, at_mx=NH * B, at_nm=2 * B, at_q2p=2 * B, at_q2=2 * B, at_s2=NH * B, at_ex=NH * B,
                at_av=NH * B, at_op=2 * B, at_otp=B, at_on=4 * B, at_tp=B, at_ot=B, at_wp=B, at_x1=B, at_x=B,
                at_init=5),
    "swiglu": dict(_PREP, **_COMB, gt_rows=NCH * NG, up_rows=NCH * NG, silu_d=NCH * NG, hid_d=NCH * NG, exp_d=E1 * NG,
                   exp_add=TG * E1 * NG, rtg=NG, rt3=2 * NG),
}


PHASES = ["moe", "gau", "moe", "swiglu", "mla", "swiglu"]
LOADS = ["xload0", "xload", "dma_tables", "dma_first", "dma_rest", "dma_norm", "dma_sw", "dma_ga", "dma_at"]
ONCE = ["const", "tail0", "wrouter", "wts", "wcopy", "wlast", "wshift", "wpe", "wsw", "gab", "gaw", "atw", "phase_end", "stored",
        "pe_passed", "dve_passed", "pool_passed"]
NW = NQ + 2 * H

TABLES = dict(ident=P, before=P, iota8=E, region0=E, tile0=NT, upto8=E * E, iota72=SLOT_TILES, places=2 * TG,
              neg_but_last=1, wr_f=E, wr_last=E, g1=E * FC, be1=E * FC)

TENSORS = {
    "X": ([P, NT, D], F32),
    "w1h": ([P, E * F], F32R), "w1l": ([P, E * F], F32R), "w2c": ([P, E * F], F32),
    "sa": ([P, E * F], F32), "sb_": ([P, E * F], F32), "sc": ([P, E * F], F32),
    "c2b": ([P, E * D], F32), "g2b": ([P, E * D], F32),
    "be2b": ([P, E * D], F32),
    "tables": ([P, sum(TABLES.values())], F32), "ones_f": ([P, P], F32), "ones_1": ([P, P], F32),
    "neg_half": ([P, 8], F32), "eps8": ([P, 8], F32), "zeros": ([P, D], F32),
    "ln_st": ([P, TG, 6], F32), "ln_mv": ([P, TG, 2], F32), "ln_ve": ([P, TG], F32), "ln_r": ([P, TG], F32),
    "ln_r2": ([P, TG], F32), "route_st": ([P, 2, TG, 6], F32),
    "route_mv": ([P, 2, TG, 2], F32), "route_ve": ([P, 2, TG], F32), "route_r": ([P, 2, TG], F32), "xn": ([P, 2, TG, D], F32), "xf": ([P, TG, D], F32),
    "xh": ([P, 2, W], F32R), "xl": ([P, 2, W], F32R),
    "rt_l": ([P, TG, NL], F32), "rt_m": ([P, TG, 8], F32), "rt_i": ([P, TG, 8], U32), "rt_d": ([P, TG, E], F32),
    "rt_e": ([P, TG, E], F32), "rt_s0": ([P, TG, E], F32), "rt_s1": ([P, TG, E], F32), "rt_z": ([P, TG], F32),
    "rt_r": ([P, TG], F32), "rt_g": ([P, TG], F32),
    "rt_q": ([P, TG, E], F32), "rt_c": ([P, E], F32), "rt_t": ([P, TOP, TG, E], F32), "chosen": ([P, TG, E], F32),
    "counts": ([P, E], F32), "sel": ([P, TOP, NT, E], F32), "row": ([P, TOP, NT], F32), "weight": ([P, NT, TOP], F32),
    "send_row": ([P, 2, TOP, TG], U32), "take_row": ([P, TOP, TG], U32), "out_row": ([P, TOP, NT], U32),
    "en": ([P, E], F32), "e_gt": ([P, E, NT], F32), "e_zero": ([P, E], F32), "e_nt": ([P, E], F32),
    "e_upto": ([P, E, E], F32), "e_skip": ([P, E], F32), "e_cum": ([P, E], F32), "e_first": ([P, E], F32),
    "e_move": ([P, E], F32), "zero_row": ([P, E], I32),
    "t_ex": ([P, SLOT_TILES], F32), "t_exw": ([P, SLOT_TILES + 2 * TG], F32),
    "t_row": ([P, SLOT_TILES], F32), "tile_row": ([P, SLOT_TILES], I32), "t_pack": ([P, 2, UNITS, TG], F32),
    "t_word": ([P, 2, UNITS], F32), "word": ([P, UNITS], I32),
    "c_row": ([P, TOP * NT], F32),
    "gate1": ([P, 2, TG, E1], F32),
    "st1": ([P, 2, TG, 6], F32), "mv1": ([P, 2, TG, 2], F32), "rs1": ([P, 2, TG], F32), "ve1": ([P, 2, TG], F32),
    "st2": ([P, TG, 6], F32), "mv2": ([P, 2, TG, 2], F32), "ve2": ([P, TG], F32), "rs2": ([P, 2, TG], F32),
    "wgh": ([P, ROWS], F32R), "wgl": ([P, ROWS], F32R), "wuh": ([P, ROWS], F32R), "wul": ([P, ROWS], F32R),
    "wd": ([P, len(PIECES) * D], F32), "wr1_f": ([P, NL], F32), "wr1h": ([P, NL], F32R), "wr1l": ([P, NL], F32R),
    "ga_w": ([P, NW], F32), "ga_last": ([P, NW], F32), "ga_ln_w": ([P, 2], F32), "ga_ln_b": ([P, P], F32),
    "ga_brow": ([1, NW], F32), "e_last": ([1, P], F32), "ga_gb": ([NQ, 4], F32), "ga_cos": ([NQ, S], F32),
    "ga_sin": ([NQ, S], F32), "ga_perm": ([NQ, NQ], F32), "ga_wo": ([P, 2 * D], F32), "ga_bo": ([P, D], F32),
    "ga_w2": ([P, D], F32), "ga_b2": ([P, D], F32), "ga_bias": ([P, P], F32), "ga_mask": ([P, P], F32),
}


def named(what, **parts):
    return namedtuple(what, parts)(**parts)


def work_space(t):
    at = Space(t.tables)
    w = {n: at.take(P, cols) for n, cols in TABLES.items()}
    at = Space(t.sb_)
    w.update(r=at.take(P, TG, F), rT=at.take(P, 2, F), y=at.take(P, 2, TG, D))
    at = Space(t.sc)
    w.update(yo=at.take(P, 2, TG, D), slots=at.take(P, 2, TG, D), t_ge=at.take(P, SLOT_TILES, E),
             t_skip=at.take(P, SLOT_TILES, E), c_move=at.take(P, TOP * NT, E), xT=flat(t.xf[:]), be1s=t.wd[:, 0:F], w1_last=t.sb_[0:1, :],
             c2s=t.sc[:].rearrange("p (e f) -> p e f", f=F)[:, :, 0:D],
             ga_taken=(flat(t.xf[:]), t.sel[:].rearrange("p k t e -> p (k t e)")))
    at = Space(t.sb_, 2 * W)
    w.update(sw_taken=(at.take(P, W), at.take(P, W)))

    w.update(hT=Space(t.sc).take(P, HRING, W), sg=Space(t.sb_).take(P, 2, W))

    at = Space(t.sb_)
    w.update(ga_xa=at.take(P, S), ga_q=at.take(NQ, S), ga_h=at.take(NQ, 2, S), ga_r1=at.take(NQ, 2, S),
             ga_r2=at.take(NQ, 2, S), ga_r=at.take(NQ, 2, 2, S), ga_k=at.take(P, P), ga_s=at.take(NQ, H))
    at = Space(t.sc)
    w.update(ga_v=at.take(P, 2, NB2, 2 * H), ga_a1=at.take(P, NB2, P), ga_a=at.take(P, NB2, P),
             ga_g=at.take(P, NB2, H), ga_t=at.take(P, 4 * P))
    at = Space(t.sa, 2 * ROWS)
    w.update(ga_yy=at.take(P, NB2, D), ga_z=at.take(P, NB2, D), ga_st=at.take(P, NB2, 6), ga_mv=at.take(P, NB2, 2),
             ga_ve=at.take(P, NB2), ga_sc=at.take(P, NB2))

    at = Space(t.w2c)
    w.update(at_w=at.take(P, 2 * P), at_last=at.take(P, 2 * P), at_u=at.take(P, 2 * D), at_b=at.take(P, 4 * D),
             at_wo=at.take(P, D), at_bo=at.take(P, D), at_cos=at.take(P, S), at_sin=at.take(P, 2, S // 2))
    at = Space(t.w1h)
    w.update(at_qT=at.take(P, NHQ, S), at_qT2=at.take(P, NHQ, S))
    at = Space(t.sa)
    w.update(at_sk=at.take(P, 2, NB2, NH, HR), at_e=at.take(P, 4, NB2 * S))
    w.update(at_sk_r=w["at_sk"].bitcast(F32R))
    at = Space(t.sb_)
    w.update(at_v=at.take(P, 2, NB2, NH, HR), at_xa=at.take(P, S), at_c=at.take(P, S), at_r=at.take(P, 2, NB2, D),
             at_s=at.take(P, 2, NB2, D), at_t1=at.take(P, 2, NB2, D))
    at = Space(t.sc)
    w.update(at_t2=at.take(P, 2, NB2, D), at_o=at.take(P, NHQ, S), at_n=at.take(P, NB2, D), at_t=at.take(P, S),
             at_m=at.take(P, NB2, NH), at_rc=at.take(P, NB2, NH))
    w.update(at_kT=[x[:].rearrange("p a (b s) -> p (a b) s", s=S) for x in (t.xh, t.xl)])
    return w


def load(sp, dst, src, sem):
    shape = list(dst.shape)
    sp.dma_start(dst, src if src.shape[0] == shape[0] else src.to_broadcast(shape)).then_inc(sem, 16)


def build(nc, io, phases=PHASES):
    with ExitStack() as ctx:
        tally = {n: Tally(ctx.enter_context(nc.semaphore(n)))
                 for n in LOADS + ONCE + sorted({n for uses in USES.values() for n in uses})}
        tensors = {n: ctx.enter_context(nc.sbuf_tensor("sb_" + n, shape, dt)) for n, (shape, dt) in TENSORS.items()}
        t = named("Tensors", **tensors)
        w = work_space(t)
        ga_loads = [(t.ga_w[:], "ga_raw"), (t.ga_last[:], "ga_last"), (t.ga_ln_w[:, 0:1], "ga_ln_w"),
                    (t.ga_ln_w[:, 1:2], "ga_ln_w_last"), (t.ga_ln_b[:], "ga_ln_b"), (t.ga_brow[:], "ga_brow"),
                    (t.e_last[:], "e_last"), (t.ga_gb[:], "ga_gb"), (t.ga_cos[:], "ga_cos"), (t.ga_sin[:], "ga_sin"),
                    (t.ga_perm[:], "ga_perm"), (t.ga_wo[:], "ga_wo"), (t.ga_bo[:], "ga_bo"), (t.ga_w2[:], "ga_w2"),
                    (t.ga_b2[:], "ga_b2"), (t.ga_bias[:], "ga_bias"), (t.ga_mask[:], "ga_mask")]
        at_loads = [(w["at_w"], "at_w"), (w["at_last"], "at_last"), (w["at_u"], "at_u"), (w["at_b"], "at_b"),
                    (w["at_wo"], "at_wo"), (w["at_bo"], "at_bo"), (w["at_cos"], "at_cos"), (w["at_sin"], "at_sin")]
        scratch = {"xs": nc.dram_tensor("xs", (XS_ROWS, D), F32).ap(), "ys": nc.dram_tensor("ys", (SLOT_TILES * P, D), F32).ap()}
        pairs = {n: (tally[n + "_even"], tally[n + "_odd"]) for n in ("sent", "loaded", "ystored")}
        p = named("Program", phases=phases, tally=tally, nga=16 * len(ga_loads),
                  nat=16 * len(at_loads), bk=[ctx.enter_context(nc.psum_tensor(f"bk{i}", [P, 512], F32)) for i in range(8)],
                  **tally, **tensors, **scratch, **pairs, **w)

        block = ctx.enter_context(nc.Block())

        @block.sync
        def _(sp):
            sp.dma_start(p.tables[:], io["tables"]).then_inc(p.dma_tables.sem, 16)
            sp.dma_start(p.w1_last, io["w1_last"]).then_inc(p.dma_tables.sem, 16)
            first, rest = slice(0, F), slice(F, E * F)
            for c, sem in ((first, p.dma_first), (rest, p.dma_rest)):
                sp.dma_start(p.sa[:, c], io["w1"][:, c]).then_inc(sem.sem, 16)
                sp.dma_start(p.sc[:, c], io["w2"][:, c]).then_inc(sem.sem, 16)
            load(sp, p.c2b[:], io["b2"], p.dma_rest.sem)
            load(sp, p.g2b[:], io["g2"], p.dma_norm.sem)
            load(sp, p.be2b[:], io["be2"], p.dma_norm.sem)
            sp.wait_ge(p.const.sem, p.const.at(NCONST))
            for q in range(E):
                sp.dma_start(p.xs[E * REGION + q * P:E * REGION + (q + 1) * P, :], p.zeros[:]).then_inc(p.tail0.sem, 16)
            for dst, n in ga_loads:
                load(sp, dst, io[n], p.dma_ga.sem)
            sp.wait_ge(p.tail0.sem, p.tail0.at(16 * E))
            for n, phase in enumerate(p.phases):
                begin(sp, p, n)
                if "moe" not in p.phases[n:] and (n == 0 or p.phases[n - 1] == "moe"):
                    for dst, src in at_loads:
                        load(sp, dst, io[src], p.dma_at.sem)
                if phase == "moe":
                    moe_sp(sp, p)
                    if "moe" not in p.phases[:n]:
                        sp.wait_ge(p.wts.sem, p.wts.at(NWT * E))
                        sp.wait_ge(p.wcopy.sem, p.wcopy.at(3 * E))
                        sp.dma_start(p.sa[:, 0:2 * ROWS], io["w_gu"]).then_inc(p.dma_sw.sem, 16)
                        sp.dma_start(p.wr1_f[:], io["w_r1"]).then_inc(p.dma_sw.sem, 16)
                        sp.dma_start(p.wd[:], io["w_d"]).then_inc(p.dma_sw.sem, 16)
            sp.wait_ge(p.phase_end.sem, p.phase_end.at(ENGINES * len(p.phases)))
            out = io["out"].rearrange("(t p) d -> p t d", p=P)
            sp.dma_start(out, p.X[:]).then_inc(p.stored.sem, 16)
            sp.wait_ge(p.stored.sem, p.stored.at(16))

        @block.gpsimd
        def _(pool):
            pool.memset(p.neg_half[:], -0.5).then_inc(p.const.sem, 1)
            pool.memset(p.ones_f[:], 1.0 / F).then_inc(p.const.sem, 1)
            pool.memset(p.xn[:], 1.0).then_inc(p.const.sem, 1)
            pool.memset(p.eps8[:], EPS).then_inc(p.const.sem, 1)
            pool.memset(p.ones_1[:], 1.0).then_inc(p.const.sem, 1)
            pool.memset(p.zeros[:], 0.0).then_inc(p.const.sem, 1)
            pool.memset(p.t_exw[:], 0.0).then_inc(p.const.sem, 1)
            pool.wait_ge(p.const.sem, p.const.at(NCONST))
            for n, phase in enumerate(p.phases):
                begin(pool, p, n)
                if phase == "moe":
                    moe_pool(pool, p)
                elif phase == "gau":
                    ga_bias_pool(pool, p)
                    ga_pool(pool, p)
                elif phase == "swiglu":
                    sw_pool(pool, p, p.phases[n - 1] == "moe")
                elif phase == "mla":
                    at_pool(pool, p)
                end(pool, p)

        @block.scalar
        def _(act):
            xs = io["x"].rearrange("(t p) d -> p t d", p=P)
            act.dma_start(p.X[:, 0:TG, :], xs[:, 0:TG, :]).then_inc(p.xload0.sem, 16)
            act.dma_start(p.X[:, TG:NT, :], xs[:, TG:NT, :]).then_inc(p.xload.sem, 16)
            for n, phase in enumerate(p.phases):
                begin(act, p, n)
                if phase == "moe":
                    moe_act(act, p, phase not in p.phases[:n])
                elif phase == "gau":
                    ga_act(act, p)
                elif phase == "swiglu":
                    sw_act(act, p)
                elif phase == "mla":
                    at_act(act, p)
                end(act, p)

        @block.vector
        def _(dve):
            dve.wait_ge(p.const.sem, p.const.at(NCONST))
            dve.wait_ge(p.dma_tables.sem, p.dma_tables.at(32))
            dve.wait_ge(p.xload0.sem, p.xload0.at(16))
            for n, phase in enumerate(p.phases):
                begin(dve, p, n)
                if phase == "swiglu" and phase not in p.phases[:n]:
                    sw_weights_dve(dve, p)
                if phase == "gau":
                    dve.wait_ge(p.gab.sem, p.gab.at(1))
                    ga_weights_dve(dve, p)
                if phase == "mla":
                    at_weights_dve(dve, p)
                if phase == "moe":
                    moe_dve(dve, p, phase not in p.phases[:n])
                elif phase == "gau":
                    ga_dve(dve, p)
                elif phase == "swiglu":
                    sw_dve(dve, p, p.phases[n - 1] == "moe")
                elif phase == "mla":
                    at_dve(dve, p)
                end(dve, p)

        @block.tensor
        def _(pe):
            pe.wait_ge(p.dma_tables.sem, p.dma_tables.at(32))
            pe.wait_ge(p.const.sem, p.const.at(NCONST))
            for n, phase in enumerate(p.phases):
                begin(pe, p, n)
                if phase == "swiglu" and phase not in p.phases[:n]:
                    pe.wait_ge(p.wsw.sem, p.wsw.at(6))
                if phase == "gau":
                    ga_weights_pe(pe, p)
                if phase == "mla":
                    pe.wait_ge(p.atw.sem, p.atw.at(1))
                if phase == "moe":
                    if phase not in p.phases[:n]:
                        pe.wait_ge(p.wrouter.sem, p.wrouter.at(1))
                    moe_pe(pe, p, phase not in p.phases[:n])
                elif phase == "gau":
                    ga_pe(pe, p)
                elif phase == "swiglu":
                    sw_pe(pe, p)
                elif phase == "mla":
                    at_pe(pe, p)
                end(pe, p)


def first_mixture_layout(inp):
    w1 = inp["L0_ffn_W1"].transpose(1, 0, 2).reshape(D, E * F)
    neg = -np.ones((P, 1), np.float32)
    neg[P - 1] = 0
    n = np.arange(P, dtype=np.float32)
    def rows(a):
        return np.broadcast_to(a, (P, a.size))
    tables = dict(
        ident=np.eye(P, dtype=np.float32), before=(n[:, None] < n[None]).astype(np.float32), iota8=rows(n[:E]),
        region0=rows(REGION * n[:E]), tile0=rows(P * n[:NT]), iota72=rows(n[:SLOT_TILES]),
        upto8=rows((n[None, :E] <= n[:E, None]).astype(np.float32).reshape(-1)),
        places=rows(np.where(np.arange(2 * TG) < TG + 3, float(E) ** np.arange(2 * TG), 0).astype(np.float32)),
        neg_but_last=neg, wr_f=np.concatenate([inp["L0_ffn_Wr"][:P - 1], inp["L0_ffn_br"][None]], 0),
        wr_last=np.broadcast_to(inp["L0_ffn_Wr"][P - 1:P], (P, E)), g1=inp["L0_ffn_g1"].reshape(E * FC, P).T,
        be1=inp["L0_ffn_be1"].reshape(E * FC, P).T)
    return dict(
        tables=np.concatenate([tables[t] for t in TABLES], 1),
        w1=np.concatenate([w1[:P - 1], inp["L0_ffn_b1"].reshape(1, E * F)], 0), w1_last=w1[P - 1:P],
        w2=inp["L0_ffn_W2"].reshape(E, FC, P, D).transpose(2, 0, 1, 3).reshape(P, E * F),
        b2=inp["L0_ffn_b2"].reshape(1, E * D), g2=inp["L0_ffn_g2"].reshape(1, E * D),
        be2=inp["L0_ffn_be2"].reshape(1, E * D))


def second_mixture_layout(inp):
    eg, h = inp["L1_ffn_experts_gate_up"], E * I1
    gate = np.concatenate([eg[:, :I1].reshape(h, D), inp["L1_ffn_shared_gate_w"]], 0).T
    up = np.concatenate([eg[:, I1:].reshape(h, D), inp["L1_ffn_shared_up_w"]], 0).T
    down = np.concatenate([inp["L1_ffn_experts_down"].transpose(0, 2, 1).reshape(h, D), inp["L1_ffn_shared_down_w"].T], 0)
    router = np.zeros((P, NL), np.float32)
    router[:, :E] = inp["L1_ffn_gate_w"].T
    router[:, E] = inp["L1_ffn_shared_expert_gate_w"][0]
    pieces = np.zeros((P, len(PIECES), D), np.float32)
    for q, (c, e) in enumerate(PIECES):
        a, z = max(c * P, e * I1), min(c * P + P, e * I1 + I1 if e < E else ROWS)
        pieces[a - c * P:z - c * P, q] = down[a:z]
    return dict(w_gu=np.concatenate([gate, up], 1), w_r1=router, w_d=pieces.reshape(P, -1))


def gated_unit_layout(inp):
    f = {n[8:]: a for n, a in inp.items() if n.startswith("L0_attn_")}
    qk = f["Wqk"].T
    w = np.concatenate([qk, qk, f["Wv"].T, f["Wg"].T], 1)
    ln_b = np.zeros((P, P), np.float32)
    ln_b[:, P - 1] = f["ln1_b"]
    e_last = np.zeros((1, P), np.float32)
    e_last[0, P - 1] = 1
    ga, be = f["gamma"], f["beta"]
    half = QK // 2
    freq = (10000.0 ** (-np.arange(half, dtype=np.float32) / half)).astype(np.float32)
    angle = np.arange(S, dtype=np.float32)[:, None] * freq[None]
    sin, cos = np.sin(angle).T.astype(np.float32), np.cos(angle).T.astype(np.float32)
    perm = np.zeros((NQ, NQ), np.float32)
    for i in range(NQ):
        perm[i // QK * QK + (i + half) % QK, i] = 1
    i = np.arange(P)
    same = (i[:, None] // GROUP) == (i[None] // GROUP)
    pos = f["pos_emb"][:MAXREL + 1]
    far = np.broadcast_to(pos[MAXREL], P - 1 - MAXREL)
    by_distance = np.concatenate([far, pos[:0:-1], pos, far])
    return dict(
        ga_raw=w, ga_last=w[P - 1:P], ga_ln_w=f["ln1_w"].reshape(P, 1), ga_ln_w_last=f["ln1_w"].reshape(P, 1)[P - 1:P],
        ga_ln_b=ln_b, ga_brow=np.concatenate([f["bqk"], f["bqk"], f["bv"], f["bg"]])[None], e_last=e_last,
        ga_gb=np.stack([np.concatenate([ga[0], ga[1]]), np.concatenate([be[0], be[1]]),
                        np.concatenate([ga[2], ga[3]]), np.concatenate([be[2], be[3]])], 1),
        ga_cos=np.concatenate([cos] * 4, 0), ga_sin=np.concatenate([-sin, sin] * 2, 0), ga_perm=perm,
        ga_wo=f["Wo"].T.reshape(2, P, D).transpose(1, 0, 2).reshape(P, 2 * D), ga_bo=f["bo"][None],
        ga_w2=f["ln2_w"][None], ga_b2=f["ln2_b"][None], ga_bias=np.stack([by_distance[P - 1 - r:2 * P - 1 - r] for r in i]),
        ga_mask=np.where(same, 0, -1e30).astype(np.float32))


def latent_attention_layout(inp):
    f = {n[8:]: a for n, a in inp.items() if n.startswith("L1_attn_")}
    w = np.concatenate([f["Wd_q_w"], f["Wd_kv_w"], f["Wk_r_w"]], 1)
    b = np.concatenate([f["Wd_q_b"], f["Wd_kv_b"], f["Wk_r_b"]])
    half = D // 2
    theta = (np.float32(10000.0) ** (-2.0 * np.arange(half, dtype=np.float32)) / half).astype(np.float32)
    angle = np.arange(S, dtype=np.float32)[:, None] * theta[None]
    cos, sin = np.cos(angle).astype(np.float32), np.sin(angle).astype(np.float32)
    sin = sin.reshape(NB2, P, half).transpose(1, 0, 2).reshape(P, NB2 * half)
    return dict(
        at_w=np.concatenate([w[:P - 1], b[None]], 0), at_last=w[P - 1:P],
        at_u=np.concatenate([np.concatenate([f["Wq_r_w"], f["Wu_q_w"]], 1),
                             np.concatenate([f["Wu_k_w"], f["Wu_v_w"]], 1)], 0),
        at_b=np.concatenate([f["Wq_r_b"], f["Wu_q_b"], f["Wu_k_b"], f["Wu_v_b"]])[None],
        at_wo=f["Wo_w"], at_bo=f["Wo_b"][None], at_sin=np.stack([-sin, sin], 1),
        at_cos=np.repeat(cos, 2, 1).reshape(NB2, P, D).transpose(1, 0, 2).reshape(P, NB2 * D))


def layout(inputs):
    inp = {n: np.asarray(a) for n, a in inputs.items()}
    out = {"x": inp["L0_attn_x"].reshape(B * S, D)}
    for part in (first_mixture_layout, second_mixture_layout, gated_unit_layout, latent_attention_layout):
        out.update(part(inp))
    return {n: np.ascontiguousarray(a) for n, a in out.items()}


def kernel(**inputs):
    import concourse.bacc as bacc
    from concourse.bass_utils import run_bass_kernel_spmd

    arrays = layout(inputs)
    nc = bacc.Bacc("TRN2", target_bir_lowering=False, num_devices=1)
    io = {n: nc.dram_tensor(n, a.shape, mybir.dt.from_np(a.dtype), kind="ExternalInput").ap() for n, a in arrays.items()}
    io["out"] = nc.dram_tensor("out", (B * S, D), F32, kind="ExternalOutput").ap()
    build(nc, io)
    r = run_bass_kernel_spmd(nc, [arrays], core_ids=[0])
    return r.results[0]["out"].reshape(B, S, D)
```

```python
from collections import namedtuple
from contextlib import ExitStack

import numpy as np

import concourse.bass as bass
from concourse import mybir

F32 = mybir.dt.float32
F32R = mybir.dt.float32r
U32 = mybir.dt.uint32
I32 = mybir.dt.int32
ALU = mybir.AluOpType
ACT = mybir.ActivationFunctionType
AX = mybir.AxisListType

P = 128
B, S, D = 16, 256, 128
NT = B * S // P
TG = 4
NG = NT // TG
W = TG * P
E = 8
F = 512
FC = F // P
EPS = 1e-5
NCONST = 7


def f32(ap):
    return ap.bitcast(F32)


class Tally:

    def __init__(self, sem):
        self.sem, self.base = sem, 0

    def at(self, n):
        return n + self.base


def uses_of(p, phase):
    behind_mixture = phase and p.phases[phase - 1] == "moe"
    return {n: u for n, u in USES[p.phases[phase]].items() if behind_mixture or n not in _COMB}


def begin(eng, p, phase):
    for uses in USES.values():
        for n in uses:
            p.tally[n].base = sum(uses_of(p, q).get(n, 0) for q in range(phase))
    if phase:
        eng.wait_ge(p.phase_end.sem, ENGINES * phase)


def end(eng, p):
    eng.drain().then_inc(p.phase_end.sem, 1)


class Space:

    def __init__(self, tensor, at=0):
        self.tensor, self.at = tensor, at

    def take(self, parts, *shape):
        n = int(np.prod(shape))
        ap = self.tensor[0:parts, self.at:self.at + n]
        self.at += n
        assert self.at <= self.tensor.shape[1]
        names = "abcd"[:len(shape)]
        if len(shape) > 1:
            ap = ap.rearrange(f"p ({' '.join(names)}) -> p {' '.join(names)}", **dict(zip(names, shape)))
        return ap


def tiles(p, g):
    return p.X[:, bass.ds(g * TG, TG), :]


def flat(ap):
    return ap.rearrange("p a b -> p (a b)")


def ln_stats(dve, p, g, n=TG):
    dve.wait_ge(p.ln_free.sem, p.ln_free.at(g))
    dve.sem_inc(p.dve_passed.sem, 1)
    for j in range(n):
        dve.bn_stats(p.ln_st[:, j, :], p.X[:, g * n + j, :]).then_inc(p.ln_stat.sem, 1)
    dve.wait_ge(p.ln_stat.sem, p.ln_stat.at(2 * n * g + n))
    dve.sem_inc(p.dve_passed.sem, 1)
    for j in range(n):
        dve.bn_aggr(p.ln_mv[:, j, :], p.ln_st[:, j, :]).then_inc(p.ln_stat.sem, 1)


def ln_scale(pool, p, g, n=TG, twice=False):
    per = 6 if twice else 2
    pool.wait_ge(p.ln_stat.sem, p.ln_stat.at(2 * n * (g + 1)))
    r, ve, var = p.ln_r[:, 0:n], p.ln_ve[:, 0:n], p.ln_mv[:, 0:n, 1]
    pool.tensor_tensor(ve, var, p.eps8[:, 0:n], ALU.add).then_inc(p.ln_rs.sem, 1)
    pool.wait_ge(p.ln_rs.sem, p.ln_rs.at(per * g + 1))
    pool.tensor_tensor(r, ve, p.neg_half[:, 0:n], ALU.pow).then_inc(p.ln_rs.sem, 1)
    if twice:
        pool.wait_ge(p.ln_rs.sem, p.ln_rs.at(per * g + 2))
        pool.tensor_tensor(ve, r, r, ALU.mult).then_inc(p.ln_rs.sem, 1)
        pool.wait_ge(p.ln_rs.sem, p.ln_rs.at(per * g + 3))
        pool.tensor_tensor(ve, ve, var, ALU.mult).then_inc(p.ln_rs.sem, 1)
        pool.wait_ge(p.ln_rs.sem, p.ln_rs.at(per * g + 4))
        pool.tensor_tensor(ve, ve, p.eps8[:, 0:n], ALU.add).then_inc(p.ln_rs.sem, 1)
        pool.wait_ge(p.ln_rs.sem, p.ln_rs.at(per * g + 5))
        pool.tensor_tensor(ve, ve, p.neg_half[:, 0:n], ALU.pow).then_inc(p.ln_rs.sem, 1)


def ln_apply(dve, p, g, xn, width, n=TG, twice=False):
    dve.wait_ge(p.ln_rs.sem, p.ln_rs.at((6 if twice else 2) * (g + 1)))
    dve.wait_ge(p.xt.sem, p.xt.at(g))
    if twice:
        dve.tensor_tensor(p.ln_r2[:, 0:n], p.ln_r[:, 0:n], p.ln_ve[:, 0:n], ALU.mult).then_inc(p.ln_both.sem, 1)
        dve.wait_ge(p.ln_both.sem, p.ln_both.at(g + 1))
    for j in range(n):
        r = p.ln_r2 if twice else p.ln_r
        ins = dve.tensor_scalar(xn[:, j, 0:width], p.X[:, g * n + j, 0:width], p.ln_mv[:, j, 0:1],
                                r[:, j:j + 1], ALU.subtract, ALU.mult)
    ins.then_inc(p.ln_free.sem, 1)


def x_transpose(pe, p, g, xn, bank, n=TG):
    pe.wait_ge(p.ln_free.sem, p.ln_free.at(g + 1))
    for j in range(n):
        ins = pe.transpose(bank[:, j * P:(j + 1) * P], xn[:, j, :], p.ident)
    ins.then_inc(p.xt.sem, 1)


def x_high(act, p, g, par, bank):
    act.wait_ge(p.xt.sem, p.xt.at(g + 1))
    act.activation(p.xh[:, par, :], bank[:], ACT.Copy).then_inc(p.xhd.sem, 1)


def x_low(dve, p, g, par, bank):
    dve.wait_ge(p.xhd.sem, p.xhd.at(g + 1))
    dve.tensor_tensor(p.xl[:, par, :], bank[:], f32(p.xh[:, par, :]), ALU.subtract).then_inc(p.xld.sem, 1)


NL = 10


def router_logits(pe, p, g, par, bank, wh, wl, n):
    pe.wait_ge(p.xld.sem, p.xld.at(g + 1))
    for j in range(TG):
        c = slice(j * P, (j + 1) * P)
        out = bank[:, j * NL:j * NL + n]
        pe.matmul(out, p.xh[:, par, c], wh, start=True, stop=False)
        pe.matmul(out, p.xh[:, par, c], wl, start=False, stop=False)
        ins = pe.matmul(out, p.xl[:, par, c], wh, start=False, stop=True)
    ins.then_inc(p.lg.sem, 1)


def router_exp(act, p, g):
    act.wait_ge(p.rt1.sem, p.rt1.at(10 * g + 6))
    act.activation(p.rt_e[:], p.rt_d[:], ACT.Exp).then_inc(p.rte.sem, 1)


def router_top(dve, p, g, bank, n):
    dve.wait_ge(p.lg.sem, p.lg.at(g + 1))
    dve.wait_ge(p.rt2.sem, p.rt2.at(7 * g))
    lg = p.rt_l
    dve.tensor_copy(lg[:, :, 0:n], bank[:, 0:TG * NL].rearrange("p (j n) -> p j n", n=NL)[:, :, 0:n])\
       .then_inc(p.rt1.sem, 1)
    dve.wait_ge(p.rt1.sem, p.rt1.at(10 * g + 1))
    dve.sem_inc(p.dve_passed.sem, 1)
    for j in range(TG):
        dve.max(p.rt_m[:, j, :], lg[:, j, 0:E]).then_inc(p.rt1.sem, 1)
    dve.wait_ge(p.rt1.sem, p.rt1.at(10 * g + 5))
    dve.tensor_tensor(p.rt_d[:], lg[:, :, 0:E], p.rt_m[:, :, 0:1].to_broadcast([P, TG, E]), ALU.subtract)\
       .then_inc(p.rt1.sem, 1)
    for j in range(TG):
        dve.max_index(p.rt_i[:, j, :], p.rt_m[:, j, :], lg[:, j, 0:E]).then_inc(p.rt1.sem, 1)
    dve.wait_ge(p.rt1.sem, p.rt1.at(10 * g + 10))
    for k, sel in ((0, p.rt_s0), (1, p.rt_s1)):
        dve.tensor_tensor(sel[:], p.iota8.unsqueeze(1).to_broadcast([P, TG, E]),
                          p.rt_i[:, :, k:k + 1].to_broadcast([P, TG, E]), ALU.is_equal).then_inc(p.rt2.sem, 1)
    dve.wait_ge(p.rt2.sem, p.rt2.at(7 * g + 2))
    dve.tensor_tensor(p.rt_s0[:], p.rt_s0[:], p.rt_s1[:], ALU.add).then_inc(p.rt2.sem, 1)


def router_gate(dve, p, g, gate, top_only):
    dve.wait_ge(p.rte.sem, p.rte.at(g + 1))
    dve.wait_ge(p.rt2.sem, p.rt2.at(7 * g + 3))
    dve.tensor_tensor(p.rt_s1[:], p.rt_e[:], p.rt_s0[:], ALU.mult).then_inc(p.rt2.sem, 1)
    dve.wait_ge(p.rt2.sem, p.rt2.at(7 * g + 4))
    dve.tensor_reduce(p.rt_z[:], p.rt_s1[:] if top_only else p.rt_e[:], AX.X, ALU.add).then_inc(p.rt2.sem, 1)
    dve.wait_ge(p.rt2.sem, p.rt2.at(7 * g + 5))
    dve.reciprocal(p.rt_r[:], p.rt_z[:]).then_inc(p.rt2.sem, 1)
    dve.wait_ge(p.rt2.sem, p.rt2.at(7 * g + 6))
    dve.scalar_tensor_tensor(out=gate[:, :, 0:E], in0=p.rt_s1[:], scalar=0.5,
                             in1=p.rt_r[:].unsqueeze(2).to_broadcast([P, TG, E]),
                             op0=ALU.mult, op1=ALU.mult).then_inc(p.rt2.sem, 1)


TOP = 2
REGION = B * S + P
SLOT_TILES = TOP * NT + E
UNITS = SLOT_TILES // TG
XS_ROWS = E * REGION + E * P
NFIN = 21
BITS = 3


def route_x_pe(pe, p, g, par, xn, n_log):
    pe.wait_ge(p.ln_free.sem, p.ln_free.at(g + 1))
    pe.wait_ge(p.route_xc.sem, p.route_xc.at(g))
    for j in range(TG):
        ins = pe.transpose(p.bk[6][:, j * P:(j + 1) * P], xn[:, par, j, :], p.ident)
    ins.then_inc(p.route_xt.sem, 1)
    pe.wait_ge(p.route_xc.sem, p.route_xc.at(g + 1))
    for j in range(TG):
        ins = pe.matmul(p.bk[4][:, j * NL:j * NL + n_log], p.xT[:, j * P:(j + 1) * P], p.wr_f[:, 0:n_log],
                        start=True, stop=True)
    ins.then_inc(p.route_lg.sem, 1)


def route_rank_pe(pe, p, g):
    pe.wait_ge(p.route_sel.sem, p.route_sel.at(3 * g + 3))
    pe.wait_ge(p.route_cnt.sem, p.route_cnt.at(2 * g))
    out, m = p.bk[5][:, 0:TG * E], flat(p.chosen[:])
    pe.matmul(out, p.before, m, start=True, stop=False)
    for d in range(1, TG):
        pe.matmul(out[:, d * E:], p.ones_1[:], m[:, 0:(TG - d) * E], start=False, stop=False)
    pe.matmul(out, p.ones_1[:], p.counts[:].unsqueeze(1).to_broadcast([P, TG, E]), start=False, stop=True)\
      .then_inc(p.route_pos.sem, 1)


def route_x_act(act, p, g):
    act.wait_ge(p.route_xt.sem, p.route_xt.at(g + 1))
    act.wait_ge(p.route_lg.sem, p.route_lg.at(g))
    act.activation(p.xT, p.bk[6][:], ACT.Copy).then_inc(p.route_xc.sem, 1)


def route_exp_act(act, p, g):
    act.wait_ge(p.route_top.sem, p.route_top.at(10 * g + 6))
    act.activation(p.rt_e[:], p.rt_d[:], ACT.Exp).then_inc(p.route_e.sem, 1)


def route_stats_dve(dve, p, g, par, first=False):
    if not first:
        dve.wait_ge(p.ln_free.sem, p.ln_free.at(g - 1))
    dve.sem_inc(p.dve_passed.sem, 1)
    for j in range(TG):
        dve.bn_stats(p.route_st[:, par, j, :], p.X[:, g * TG + j, :]).then_inc(p.ln_stat.sem, 1)
    dve.wait_ge(p.ln_stat.sem, p.ln_stat.at(2 * TG * g + TG))
    dve.sem_inc(p.dve_passed.sem, 1)
    for j in range(TG):
        dve.bn_aggr(p.route_mv[:, par, j, :], p.route_st[:, par, j, :]).then_inc(p.ln_stat.sem, 1)


def route_scale_pool(pool, p, g, par):
    pool.wait_ge(p.ln_stat.sem, p.ln_stat.at(2 * TG * (g + 1)))
    pool.tensor_tensor(p.route_ve[:, par], p.route_mv[:, par, :, 1], p.eps8[:, 0:TG], ALU.add).then_inc(p.ln_rs.sem, 1)
    pool.wait_ge(p.ln_rs.sem, p.ln_rs.at(2 * g + 1))
    pool.tensor_tensor(p.route_r[:, par], p.route_ve[:, par], p.neg_half[:, 0:TG], ALU.pow).then_inc(p.ln_rs.sem, 1)


def route_apply_dve(dve, p, g, par, xn, width, first=False):
    if not first:
        dve.wait_ge(p.sent[par].sem, p.sent[par].at(8 * TG * TOP * (g - par)))
    dve.wait_ge(p.ln_rs.sem, p.ln_rs.at(2 * (g + 1)))
    for j in range(TG):
        ins = dve.tensor_scalar(xn[:, par, j, 0:width], p.X[:, g * TG + j, 0:width], p.route_mv[:, par, j, 0:1],
                                p.route_r[:, par, j:j + 1], ALU.subtract, ALU.mult)
    ins.then_inc(p.ln_free.sem, 1)


def route_top_dve(dve, p, g, n_log):
    dve.wait_ge(p.route_lg.sem, p.route_lg.at(g + 1))
    dve.wait_ge(p.route_w.sem, p.route_w.at(3 * g))
    dve.tensor_copy(p.rt_l[:, :, 0:n_log], p.bk[4][:, 0:TG * NL].rearrange("p (j n) -> p j n", n=NL)[:, :, 0:n_log])\
       .then_inc(p.route_top.sem, 1)
    dve.wait_ge(p.route_top.sem, p.route_top.at(10 * g + 1))
    dve.sem_inc(p.dve_passed.sem, 1)
    for j in range(TG):
        dve.max(p.rt_m[:, j, :], p.rt_l[:, j, 0:E]).then_inc(p.route_top.sem, 1)
    dve.wait_ge(p.route_top.sem, p.route_top.at(10 * g + 5))
    dve.tensor_tensor(p.rt_d[:], p.rt_m[:], p.rt_m[:, :, 0:1].to_broadcast([P, TG, E]), ALU.subtract)\
       .then_inc(p.route_top.sem, 1)
    for j in range(TG):
        dve.max_index(p.rt_i[:, j, :], p.rt_m[:, j, :], p.rt_l[:, j, 0:E]).then_inc(p.route_top.sem, 1)
    dve.wait_ge(p.route_top.sem, p.route_top.at(10 * g + 10))
    tiles_g = bass.ds(g * TG, TG)
    for k in range(TOP):
        dve.tensor_tensor(p.sel[:, k, tiles_g, :], p.iota8.unsqueeze(1).to_broadcast([P, TG, E]),
                          p.rt_i[:, :, k:k + 1].to_broadcast([P, TG, E]), ALU.is_equal).then_inc(p.route_sel.sem, 1)
    dve.wait_ge(p.route_sel.sem, p.route_sel.at(3 * g + 2))
    dve.tensor_tensor(p.chosen[:], p.sel[:, 0, tiles_g, :], p.sel[:, 1, tiles_g, :], ALU.add)\
       .then_inc(p.route_sel.sem, 1)


def route_weights_dve(dve, p, g, over):
    dve.wait_ge(p.route_e.sem, p.route_e.at(g + 1))
    dve.tensor_reduce(p.rt_z[:], p.rt_e[:, :, 0:over], AX.X, ALU.add).then_inc(p.route_w.sem, 1)
    dve.wait_ge(p.route_w.sem, p.route_w.at(3 * g + 1))
    dve.reciprocal(p.rt_r[:], p.rt_z[:]).then_inc(p.route_w.sem, 1)
    dve.wait_ge(p.route_w.sem, p.route_w.at(3 * g + 2))
    dve.scalar_tensor_tensor(out=p.weight[:, bass.ds(g * TG, TG), :], in0=p.rt_e[:, :, 0:TOP], scalar=0.5,
                             in1=p.rt_r[:].unsqueeze(2).to_broadcast([P, TG, TOP]),
                             op0=ALU.mult, op1=ALU.mult).then_inc(p.route_w.sem, 1)


def route_rows_dve(dve, p, g, par):
    tiles_g = bass.ds(g * TG, TG)
    dve.wait_ge(p.route_pos.sem, p.route_pos.at(g + 1))
    dve.tensor_tensor(p.rt_q[:], p.bk[5][:, 0:TG * E].rearrange("p (j e) -> p j e", e=E),
                      p.region0.unsqueeze(1).to_broadcast([P, TG, E]), ALU.add).then_inc(p.route_row.sem, 1)
    dve.tensor_reduce(p.rt_c[:], p.chosen[:].rearrange("p j e -> p e j"), AX.X, ALU.add).then_inc(p.route_cnt.sem, 1)
    dve.wait_ge(p.route_row.sem, p.route_row.at(4 * g + 1))
    dve.tensor_tensor(p.rt_t[:], p.sel[:, :, tiles_g, :], p.rt_q[:].unsqueeze(1).to_broadcast([P, TOP, TG, E]),
                      ALU.mult).then_inc(p.route_row.sem, 1)
    dve.wait_ge(p.route_row.sem, p.route_row.at(4 * g + 2))
    dve.tensor_reduce(p.row[:, :, tiles_g], p.rt_t[:], AX.X, ALU.add).then_inc(p.route_row.sem, 1)
    dve.wait_ge(p.route_row.sem, p.route_row.at(4 * g + 3))
    dve.sem_inc(p.dve_passed.sem, 1)
    dve.tensor_copy(p.send_row[:, par], p.row[:, :, tiles_g]).then_inc(p.route_row.sem, 1)
    dve.wait_ge(p.route_cnt.sem, p.route_cnt.at(2 * g + 1))
    dve.tensor_tensor(p.counts[:], p.counts[:], p.rt_c[:], ALU.add).then_inc(p.route_cnt.sem, 1)


def route_send_pool(pool, p, g, par, xn):
    pool.wait_ge(p.route_row.sem, p.route_row.at(4 * g + 4))
    pool.sem_inc(p.pool_passed.sem, 1)
    for k in range(TOP):
        for j in range(TG):
            pool.indirect_dma_start(p.xs, bass.IndirectOffsetOnAxis(ap=p.send_row[:, par, k, j:j + 1], axis=0),
                                    xn[:, par, j, :], None).then_inc(p.sent[par].sem, 16)


def route_end_pe(pe, p):
    pe.wait_ge(p.route_cnt.sem, p.route_cnt.at(2 * NG))
    pe.matmul(p.bk[4][:, 0:E], p.ones_1[:], p.counts[:], start=True, stop=True).then_inc(p.route_n.sem, 1)


def route_end_dve(dve, p):
    f, n = p.fin, [0]

    def done(ins):
        n[0] += 1
        ins.then_inc(f.sem, 1)

    def by_tile(a):
        return a.unsqueeze(1).to_broadcast([P, SLOT_TILES, E])

    dve.wait_ge(p.route_n.sem, p.route_n.at(1))
    done(dve.tensor_copy(p.en[:], p.bk[4][:, 0:E]))
    dve.wait_ge(f.sem, f.at(n[0]))
    done(dve.tensor_tensor(p.e_gt[:], p.en[:].unsqueeze(2).to_broadcast([P, E, NT]),
                           p.tile0[:, 0:NT].unsqueeze(1).to_broadcast([P, E, NT]), ALU.is_gt))
    done(dve.tensor_tensor(p.e_zero[:], p.en[:], p.region0, ALU.add))
    dve.wait_ge(f.sem, f.at(n[0]))
    done(dve.tensor_copy(p.zero_row[:], p.e_zero[:]))
    done(dve.tensor_reduce(p.e_nt[:], p.e_gt[:], AX.X, ALU.add))
    dve.wait_ge(f.sem, f.at(n[0]))
    done(dve.tensor_tensor(p.e_upto[:], p.upto8.rearrange("p (a b) -> p a b", b=E),
                           p.e_nt[:].unsqueeze(1).to_broadcast([P, E, E]), ALU.mult))
    done(dve.tensor_scalar(p.e_skip[:], p.e_nt[:], float(-P), float(REGION), ALU.mult, ALU.add))
    dve.wait_ge(f.sem, f.at(n[0]))
    done(dve.tensor_reduce(p.e_cum[:], p.e_upto[:], AX.X, ALU.add))
    dve.wait_ge(f.sem, f.at(n[0]))
    done(dve.tensor_tensor(p.t_ge, p.iota72.unsqueeze(2).to_broadcast([P, SLOT_TILES, E]),
                           by_tile(p.e_cum[:]), ALU.is_ge))
    done(dve.tensor_tensor(p.e_first[:], p.e_cum[:], p.e_nt[:], ALU.subtract))
    dve.wait_ge(f.sem, f.at(n[0]))
    done(dve.tensor_reduce(p.t_ex[:], p.t_ge, AX.X, ALU.add))
    done(dve.tensor_tensor(p.t_skip, p.t_ge, by_tile(p.e_skip[:]), ALU.mult))
    done(dve.scalar_tensor_tensor(out=p.e_move[:], in0=p.e_first[:], scalar=float(P), in1=p.region0,
                                  op0=ALU.mult, op1=ALU.subtract))
    dve.wait_ge(f.sem, f.at(n[0]))
    done(dve.tensor_scalar(p.t_exw[:, 1:1 + SLOT_TILES], p.t_ex[:], float(E - 1), None, ALU.min))
    done(dve.tensor_reduce(p.t_row[:], p.t_skip, AX.X, ALU.add))
    dve.wait_ge(f.sem, f.at(n[0]))
    done(dve.scalar_tensor_tensor(out=p.tile_row[:], in0=p.iota72, scalar=float(P), in1=p.t_row[:],
                                  op0=ALU.mult, op1=ALU.add))
    four = "p (u j) -> p u j"
    for a in range(2):
        done(dve.tensor_tensor(p.t_pack[:, a], p.t_exw[:, a * TG:a * TG + SLOT_TILES].rearrange(four, j=TG),
                               p.places[:, a * TG:(a + 1) * TG].unsqueeze(1).to_broadcast([P, UNITS, TG]), ALU.mult))
    dve.wait_ge(f.sem, f.at(n[0]))
    for a in range(2):
        done(dve.tensor_reduce(p.t_word[:, a], p.t_pack[:, a], AX.X, ALU.add))
    dve.wait_ge(f.sem, f.at(n[0]))
    done(dve.tensor_tensor(p.word[:], p.t_word[:, 0], p.t_word[:, 1], ALU.add))
    assert n[0] == NFIN


def combine_rows_dve(dve, p):
    c = p.comb_row
    dve.wait_ge(p.fin.sem, p.fin.at(NFIN))
    dve.tensor_tensor(p.c_move, p.sel[:].rearrange("p k t e -> p (k t) e"),
                      p.e_move[:].unsqueeze(1).to_broadcast([P, TOP * NT, E]), ALU.mult).then_inc(c.sem, 1)
    dve.wait_ge(c.sem, c.at(1))
    dve.tensor_reduce(p.c_row[:], p.c_move, AX.X, ALU.add).then_inc(c.sem, 1)
    dve.wait_ge(c.sem, c.at(2))
    dve.tensor_tensor(p.out_row[:].rearrange("p k t -> p (k t)"), p.row[:].rearrange("p k t -> p (k t)"), p.c_row[:],
                      ALU.add).then_inc(c.sem, 1)


def combine_rows_pool(pool, p, g):
    pool.wait_ge(p.comb.sem, p.comb.at(TOP * TG * g))
    pool.sem_inc(p.pool_passed.sem, 1)
    pool.tensor_copy(p.take_row[:], p.out_row[:, :, bass.ds(g * TG, TG)]).then_inc(p.comb_idx.sem, 1)


def combine_pool(pool, p, g, taken, k):
    pool.wait_ge(p.comb_idx.sem, p.comb_idx.at(g + 1))
    pool.sem_inc(p.pool_passed.sem, 1)
    for j in range(TG):
        pool.indirect_dma_start(taken[k][:, j * D:(j + 1) * D], None, p.ys,
                                bass.IndirectOffsetOnAxis(ap=p.take_row[:, k, j:j + 1], axis=0)).then_inc(p.got.sem, 16)


def combine_group_pool(pool, p, g, taken):
    combine_rows_pool(pool, p, g)
    for k in range(TOP):
        combine_pool(pool, p, g, taken, k)


def combine_begin_pool(pool, p, taken):
    for par in range(2):
        pool.wait_ge(p.ystored[par].sem, p.ystored[par].at(0))
    combine_group_pool(pool, p, 0, taken)


def combine_dve(dve, p, g, taken, ks=range(TOP)):
    dve.wait_ge(p.got.sem, p.got.at(16 * TOP * TG * (g + 1)))
    for k in ks:
        dve.wait_ge(p.comb.sem, p.comb.at(TG * (TOP * g + k)))
        for j in range(TG):
            x = p.X[:, g * TG + j, :]
            dve.scalar_tensor_tensor(out=x, in0=taken[k][:, j * D:(j + 1) * D], scalar=p.weight[:, bass.ds(g * TG + j, 1), k],
                                     in1=x, op0=ALU.mult, op1=ALU.add).then_inc(p.comb.sem, 1)


def zero_rows_sp(sp, p):
    sp.wait_ge(p.fin.sem, p.fin.at(4))
    rows = [sp.value_load(p.zero_row[0:1, e:e + 1], min_val=0, max_val=E * REGION) for e in range(E)]
    for row in rows:
        sp.dma_start(p.xs[bass.ds(row, P), :], p.zeros[:]).then_inc(p.zeroed.sem, 16)


def tiles_load_sp(sp, p, k, par, first=False):
    rows = [sp.value_load(p.tile_row[0:1, bass.ds(k * TG + j, 1)], min_val=0, max_val=XS_ROWS - P) for j in range(TG)]
    if first:
        for sent in p.sent:
            sp.wait_ge(sent.sem, sent.at(8 * TOP * NT))
        sp.wait_ge(p.zeroed.sem, p.zeroed.at(16 * E))
    else:
        sp.wait_ge(p.xt.sem, p.xt.at(k - 1))
    for j, row in enumerate(rows):
        sp.dma_start(p.slots[:, par, j, :], p.xs[bass.ds(row, P), :]).then_inc(p.loaded[par].sem, 16)


def tiles_store_sp(sp, p, k, par):
    if isinstance(k, int) and k == UNITS - 1:
        sp.wait_ge(p.dve_u.sem, p.dve_u.at(NU))
    else:
        sp.wait_ge(p.pl_u.sem, p.pl_u.at(NU * (k + 1)))
    sp.dma_start(p.ys.rearrange("(t p) d -> p t d", p=P)[:, bass.ds(k * TG, TG), :], p.yo[:, par])\
      .then_inc(p.ystored[par].sem, 16)


STORE_LAG = 6


def moe_sp(sp, p):
    zero_rows_sp(sp, p)
    sp.wait_ge(p.fin.sem, p.fin.at(NFIN))
    for k in range(STORE_LAG):
        tiles_load_sp(sp, p, k, k % 2, k < 2)
    with sp.Fori(STORE_LAG // 2, UNITS // 2) as i:
        for m in range(2):
            tiles_load_sp(sp, p, 2 * i + m, m)
            tiles_store_sp(sp, p, 2 * i + m - STORE_LAG, m)
    for k in range(UNITS - STORE_LAG, UNITS):
        tiles_store_sp(sp, p, k, k % 2)


NA, NB, NC = 8, 13, 4
NR, NGT, NU = 2, 2, 2 * TG


def expert_of(word, n):
    return (word >> (BITS * n)) & (E - 1)


def unit_word(eng, p, k):
    return eng.value_load(p.word[0:1, bass.ds(k, 1)], min_val=0, max_val=2 ** (BITS * (TG + 3)) - 1)


def unit_x_pe(pe, p, k, par):
    pe.wait_ge(p.loaded[par].sem, p.loaded[par].at(8 * TG * (k - par + 2)))
    pe.wait_ge(p.xld.sem, p.xld.at(k))
    for j in range(TG):
        ins = pe.transpose(p.bk[6][:, j * P:(j + 1) * P], p.slots[:, par, j, :], p.ident)
    ins.then_inc(p.xt.sem, 1)


def moe_t1(pe, p, k, par, e, j):
    if j == 0:
        pe.wait_ge(p.xld.sem, p.xld.at(k + 1))
    c = slice(j * P, (j + 1) * P)
    out = p.bk[j % 2][:]
    w = bass.ds(e * F, F)
    pe.matmul(out, p.xh[:, par, c], p.w1h[:, w], start=True, stop=False)
    pe.matmul(out, p.xh[:, par, c], p.w1l[:, w], start=False, stop=False)
    pe.matmul(out, p.xl[:, par, c], p.w1h[:, w], start=False, stop=True).then_inc(p.hid.sem, 1)


def moe_t2(pe, p, k, j, first):
    pe.wait_ge(p.act_r.sem, p.act_r.at(4 * k + j + 1))
    if not first or j >= 2:
        pe.wait_ge(p.act_t.sem, p.act_t.at(4 * k + j - 1))
    for c in range(FC):
        ins = pe.transpose(p.bk[2 + j % 2][:, c * P:(c + 1) * P], p.r[:, j, c * P:(c + 1) * P], p.ident)
    ins.then_inc(p.hidT.sem, 1)


def moe_t3(pe, p, k, e, par, j):
    pe.wait_ge(p.act_t.sem, p.act_t.at(4 * k + j + 1))
    for c in range(FC):
        ins = pe.matmul(p.bk[4 + par][:, j * P:(j + 1) * P], p.rT[:, j % 2, c * P:(c + 1) * P],
                        p.w2c[:, bass.ds((e * FC + c) * D, D)], start=(c == 0), stop=(c == FC - 1))
    ins.then_inc(p.outl.sem, 1)


def moe_pe_unit(pe, p, k, par, first=False, ahead=True, last=False):
    word = unit_word(pe, p, k)
    for j in range(TG):
        moe_t2(pe, p, k, j, first and par == 0)
        if j == 0 and not (first and par == 0):
            moe_t3(pe, p, k - 1, expert_of(word, 0), 1 - par, TG - 1)
        if j == 1 and not first:
            pe.wait_ge(p.dve_b.sem, p.dve_b.at(NB * (k - 2) + 4))
        if j >= 1:
            moe_t3(pe, p, k, expert_of(word, j), par, j - 1)
        if j < 2:
            moe_t1(pe, p, k, par, expert_of(word, j + 3), j + 2)
        elif not last:
            moe_t1(pe, p, k + 1, 1 - par, expert_of(word, j + 3), j - 2)
        if j == 0 and ahead:
            unit_x_pe(pe, p, k + 2, par)
    if last:
        moe_t3(pe, p, k, expert_of(word, TG), par, TG - 1)


def moe_experts_pe(pe, p):
    unit_x_pe(pe, p, 0, 0)
    unit_x_pe(pe, p, 1, 1)
    pe.wait_ge(p.fin.sem, p.fin.at(NFIN))
    word = unit_word(pe, p, 0)
    for j in range(2):
        moe_t1(pe, p, 0, 0, expert_of(word, j + 1), j)
    for k in range(2):
        moe_pe_unit(pe, p, k, k, first=True)
    with pe.Fori(1, UNITS // 2 - 1) as i:
        moe_pe_unit(pe, p, 2 * i, 0)
        moe_pe_unit(pe, p, 2 * i + 1, 1)
    moe_pe_unit(pe, p, UNITS - 2, 0, ahead=False)
    moe_pe_unit(pe, p, UNITS - 1, 1, ahead=False, last=True)


def unit_x_high(act, p, k, par):
    act.wait_ge(p.xt.sem, p.xt.at(k + 1))
    act.activation(p.xh[:, par, :], p.bk[6][:], ACT.Copy).then_inc(p.xhd.sem, 1)


def moe_relu(act, p, k, j):
    act.wait_ge(p.hid.sem, p.hid.at(4 * k + j + 1))
    act.activation(p.r[:, j, :], p.bk[j % 2][:], ACT.Relu).then_inc(p.act_r.sem, 1)


def moe_act_unit(act, p, k, par, ahead=True, last=False):
    for j in range(TG):
        act.wait_ge(p.hidT.sem, p.hidT.at(4 * k + j + 1))
        act.activation(p.rT[:, j % 2, :], p.bk[2 + j % 2][:], ACT.Copy).then_inc(p.act_t.sem, 1)
        if j < 2:
            act.wait_ge(p.dve_a.sem, p.dve_a.at(NA * k))
            moe_relu(act, p, k, j + 2)
            if j == 1 and ahead:
                unit_x_high(act, p, k + 2, par)
        elif not last:
            act.wait_ge(p.dve_a.sem, p.dve_a.at(NA * k + j - 1))
            moe_relu(act, p, k + 1, j - 2)


def moe_experts_act(act, p):
    for k in range(2):
        unit_x_high(act, p, k, k)
    for j in range(2):
        moe_relu(act, p, 0, j)
    with act.Fori(0, UNITS // 2 - 1) as i:
        moe_act_unit(act, p, 2 * i, 0)
        moe_act_unit(act, p, 2 * i + 1, 1)
    moe_act_unit(act, p, UNITS - 2, 0, ahead=False)
    moe_act_unit(act, p, UNITS - 1, 1, ahead=False, last=True)


def unit_x_low(dve, p, k, par):
    dve.wait_ge(p.xhd.sem, p.xhd.at(k + 1))
    dve.tensor_tensor(p.xl[:, par, :], p.bk[6][:], f32(p.xh[:, par, :]), ALU.subtract).then_inc(p.xld.sem, 1)


def moe_a(dve, p, k, par):
    for j in range(TG):
        dve.wait_ge(p.act_r.sem, p.act_r.at(4 * k + j + 1))
        dve.bn_stats(p.st1[:, par, j, :], p.r[:, j, :]).then_inc(p.dve_a.sem, 1)
    dve.wait_ge(p.dve_a.sem, p.dve_a.at(NA * k + 4))
    dve.sem_inc(p.dve_passed.sem, 1)
    for j in range(TG):
        dve.bn_aggr(p.mv1[:, par, j, :], p.st1[:, par, j, :]).then_inc(p.dve_a.sem, 1)


def moe_b(dve, p, k, par, first=False):
    word = unit_word(dve, p, k)
    dve.wait_ge(p.outl.sem, p.outl.at(4 * k + 4))
    dve.wait_ge(p.pl_r.sem, p.pl_r.at(NR * k + 2))
    if not first:
        dve.wait_ge(p.pl_u.sem, p.pl_u.at(NU * (k - 1)))
    y = p.y[:, par]
    for j in range(TG):
        dve.scalar_tensor_tensor(out=y[:, j, :], in0=p.bk[4 + par][:, j * P:(j + 1) * P],
                                 scalar=p.rs1[:, par, j:j + 1], in1=p.c2b[:, bass.ds(expert_of(word, j + 1) * D, D)],
                                 op0=ALU.mult, op1=ALU.add).then_inc(p.dve_b.sem, 1)
    dve.wait_ge(p.dve_b.sem, p.dve_b.at(NB * k + 4))
    dve.tensor_scalar(flat(y), flat(y), 0.0, None, ALU.max).then_inc(p.dve_b.sem, 1)
    dve.wait_ge(p.dve_b.sem, p.dve_b.at(NB * k + 5))
    for j in range(TG):
        dve.bn_stats(p.st2[:, j, :], y[:, j, :]).then_inc(p.dve_b.sem, 1)
    dve.wait_ge(p.dve_b.sem, p.dve_b.at(NB * k + 9))
    dve.sem_inc(p.dve_passed.sem, 1)
    for j in range(TG):
        dve.bn_aggr(p.mv2[:, par, j, :], p.st2[:, j, :]).then_inc(p.dve_b.sem, 1)


def moe_c(dve, p, k, par):
    dve.wait_ge(p.pl_g.sem, p.pl_g.at(NGT * k + 2))
    y = p.y[:, par]
    for j in range(TG):
        dve.tensor_scalar(y[:, j, :], y[:, j, :], p.mv2[:, par, j, 0:1], p.rs2[:, par, j:j + 1],
                          ALU.subtract, ALU.mult).then_inc(p.dve_c.sem, 1)


def moe_dve_unit(dve, p, k, par, ahead=True):
    moe_a(dve, p, k, par)
    if ahead:
        unit_x_low(dve, p, k + 2, par)
    moe_c(dve, p, k - 2, par)
    moe_b(dve, p, k - 1, 1 - par)


def moe_experts_dve(dve, p):
    for k in range(2):
        unit_x_low(dve, p, k, k)
    combine_rows_dve(dve, p)
    moe_a(dve, p, 0, 0)
    unit_x_low(dve, p, 2, 0)
    moe_a(dve, p, 1, 1)
    unit_x_low(dve, p, 3, 1)
    moe_b(dve, p, 0, 0, first=True)
    moe_a(dve, p, 2, 0)
    unit_x_low(dve, p, 4, 0)
    moe_c(dve, p, 0, 0)
    moe_b(dve, p, 1, 1, first=True)
    moe_dve_unit(dve, p, 3, 1)
    with dve.Fori(2, UNITS // 2 - 1) as i:
        moe_dve_unit(dve, p, 2 * i, 0)
        moe_dve_unit(dve, p, 2 * i + 1, 1)
    moe_dve_unit(dve, p, UNITS - 2, 0, ahead=False)
    moe_dve_unit(dve, p, UNITS - 1, 1, ahead=False)
    moe_b(dve, p, UNITS - 1, 1)
    moe_c(dve, p, UNITS - 2, 0)
    moe_c(dve, p, UNITS - 1, 1)
    moe_u(dve, p, UNITS - 1, 1, p.dve_passed, p.dve_u)


def moe_r(pool, p, k, par):
    pool.wait_ge(p.dve_a.sem, p.dve_a.at(NA * k + NA))
    pool.tensor_tensor(p.ve1[:, par, :], p.mv1[:, par, :, 1], p.eps8[:, 0:TG], ALU.add).then_inc(p.pl_r.sem, 1)
    pool.wait_ge(p.pl_r.sem, p.pl_r.at(NR * k + 1))
    pool.tensor_tensor(p.rs1[:, par, :], p.ve1[:, par, :], p.neg_half[:, 0:TG], ALU.pow).then_inc(p.pl_r.sem, 1)


def moe_g(pool, p, k, par):
    pool.wait_ge(p.dve_b.sem, p.dve_b.at(NB * k + NB))
    pool.tensor_tensor(p.ve2[:], p.mv2[:, par, :, 1], p.eps8[:, 0:TG], ALU.add).then_inc(p.pl_g.sem, 1)
    pool.wait_ge(p.pl_g.sem, p.pl_g.at(NGT * k + 1))
    pool.tensor_tensor(p.rs2[:, par, :], p.ve2[:], p.neg_half[:, 0:TG], ALU.pow).then_inc(p.pl_g.sem, 1)


def moe_u(eng, p, k, par, passed, done, first=False):
    word = unit_word(eng, p, k)
    eng.wait_ge(p.dve_c.sem, p.dve_c.at(NC * k + NC))
    if not first:
        eng.wait_ge(p.ystored[par].sem, p.ystored[par].at(8 * (k - par)))
    for n, table in enumerate((p.g2b, p.be2b)):
        if n:
            eng.wait_ge(done.sem, done.at(NU * (0 if done is p.dve_u else k) + TG))
        eng.sem_inc(passed.sem, 1)
        for j in range(TG):
            eng.tensor_tensor(p.yo[:, par, j, :], (p.yo if n else p.y)[:, par, j, :],
                               table[:, bass.ds(expert_of(word, j + 1) * D, D)], ALU.add if n else ALU.mult)\
                .then_inc(done.sem, 1)


def moe_pool_unit(pool, p, k, par, first=False):
    moe_r(pool, p, k, par)
    moe_u(pool, p, k - 2, par, p.pool_passed, p.pl_u, first)
    moe_g(pool, p, k - 1, 1 - par)


def moe_experts_pool(pool, p):
    moe_r(pool, p, 0, 0)
    moe_r(pool, p, 1, 1)
    moe_g(pool, p, 0, 0)
    for k in range(2, 4):
        moe_pool_unit(pool, p, k, k % 2, first=True)
    with pool.Fori(2, UNITS // 2) as i:
        moe_pool_unit(pool, p, 2 * i, 0)
        moe_pool_unit(pool, p, 2 * i + 1, 1)
    pool.wait_ge(p.pl_g.sem, p.pl_g.at(NGT * (UNITS - 1)))
    moe_g(pool, p, UNITS - 1, 1)
    moe_u(pool, p, UNITS - 2, 0, p.pool_passed, p.pl_u)


def moe_pe_group(pe, p, g, par, weights, last=False):
    route_rank_pe(pe, p, g)
    if not last:
        route_x_pe(pe, p, g + 1, 1 - par, p.xn, E)
    if weights:
        moe_last_row_pe(pe, p, g)
        moe_weights_pe(pe, p, g)


def moe_pe(pe, p, weights):
    route_x_pe(pe, p, 0, 0, p.xn, E)
    with pe.Fori(0, NG // 2 - 1) as i:
        moe_pe_group(pe, p, 2 * i, 0, weights)
        moe_pe_group(pe, p, 2 * i + 1, 1, weights)
    moe_pe_group(pe, p, NG - 2, 0, weights)
    moe_pe_group(pe, p, NG - 1, 1, weights, last=True)
    route_end_pe(pe, p)
    if weights:
        pe.wait_ge(p.wts.sem, p.wts.at(NWT * E))
    moe_experts_pe(pe, p)


def moe_act_group(act, p, g, weights, last=False):
    route_exp_act(act, p, g)
    if not last:
        route_x_act(act, p, g + 1)
    if weights:
        moe_weights_act(act, p, g)


def moe_act(act, p, weights):
    route_x_act(act, p, 0)
    moe_act_group(act, p, 0, weights)
    with act.Fori(1, NG - 1) as g:
        moe_act_group(act, p, g, weights)
    moe_act_group(act, p, NG - 1, weights, last=True)
    moe_experts_act(act, p)


def moe_dve_group(dve, p, g, par, weights, first=False, ahead=2):
    route_top_dve(dve, p, g, E)
    if not weights:
        route_rows_dve(dve, p, g, par)
    if ahead >= 1:
        route_apply_dve(dve, p, g + 1, 1 - par, p.xn, P - 1, first)
    if weights:
        route_rows_dve(dve, p, g, par)
    if ahead >= 2:
        route_stats_dve(dve, p, g + 2, par)
    route_weights_dve(dve, p, g, TOP)
    if weights:
        moe_weights_dve(dve, p, g)


def moe_dve(dve, p, weights, prepare):
    dve.memset(p.counts[:], 0.0).then_inc(p.route_init.sem, 1)
    dve.wait_ge(p.route_init.sem, p.route_init.at(1))
    route_stats_dve(dve, p, 0, 0, True)
    if weights:
        moe_router_weights_dve(dve, p)
        dve.wait_ge(p.xload.sem, p.xload.at(16))
    route_stats_dve(dve, p, 1, 1, True)
    route_apply_dve(dve, p, 0, 0, p.xn, P - 1, True)
    moe_dve_group(dve, p, 0, 0, weights, first=True)
    moe_dve_group(dve, p, 1, 1, weights)
    with dve.Fori(1, NG // 2 - 1) as i:
        moe_dve_group(dve, p, 2 * i, 0, weights)
        moe_dve_group(dve, p, 2 * i + 1, 1, weights)
    moe_dve_group(dve, p, NG - 2, 0, weights, ahead=1)
    moe_dve_group(dve, p, NG - 1, 1, weights, ahead=0)
    if weights:
        c2b = p.c2b[:].rearrange("p (e d) -> p e d", d=D)
        dve.wait_ge(p.wcopy.sem, p.wcopy.at(3 * E))
        dve.tensor_tensor(c2b, c2b, p.c2s, ALU.add).then_inc(p.wshift.sem, 1)
        dve.wait_ge(p.wshift.sem, p.wshift.at(1))
    route_end_dve(dve, p)
    if prepare:
        sw_weights_dve(dve, p)
    moe_experts_dve(dve, p)


def moe_pool_group(pool, p, g, par, ahead=True):
    route_send_pool(pool, p, g, par, p.xn)
    if ahead:
        route_scale_pool(pool, p, g + 2, par)


def moe_pool(pool, p):
    for g in range(2):
        route_scale_pool(pool, p, g, g)
    with pool.Fori(0, NG // 2 - 1) as i:
        moe_pool_group(pool, p, 2 * i, 0)
        moe_pool_group(pool, p, 2 * i + 1, 1)
    moe_pool_group(pool, p, NG - 2, 0, ahead=False)
    moe_pool_group(pool, p, NG - 1, 1, ahead=False)
    pool.wait_ge(p.dma_norm.sem, p.dma_norm.at(32))
    moe_experts_pool(pool, p)


NWT = 4


def moe_router_weights_dve(dve, p):
    dve.scalar_tensor_tensor(out=p.wr_f, in0=p.wr_last, scalar=p.neg_but_last, in1=p.wr_f,
                             op0=ALU.mult, op1=ALU.add).then_inc(p.wrouter.sem, 1)


def moe_weights_dve(dve, p, e):
    s = p.wts
    f = bass.ds(e * F, F)
    chunks = "p (c d) -> p c d"
    if isinstance(e, int) and e == 0:
        dve.wait_ge(p.dma_first.sem, p.dma_first.at(16 * 2))
    elif isinstance(e, int) and e == 1:
        dve.wait_ge(p.dma_rest.sem, p.dma_rest.at(16 * 3))
    w = p.w2c[:, f].rearrange(chunks, d=D)
    dve.tensor_tensor(w, p.sc[:, f].rearrange(chunks, d=D),
                      p.g1[:, bass.ds(e * FC, FC)].unsqueeze(2).to_broadcast([P, FC, D]), ALU.mult).then_inc(s.sem, 1)
    dve.wait_ge(p.wlast.sem, p.wlast.at(e + 1))
    dve.scalar_tensor_tensor(out=p.sa[:, f], in0=p.bk[1][:], scalar=p.neg_but_last, in1=p.sa[:, f],
                             op0=ALU.mult, op1=ALU.add).then_inc(s.sem, 1)
    dve.wait_ge(s.sem, s.at(NWT * e + 1))
    dve.wait_ge(p.wpe.sem, p.wpe.at(2 * e + 1))
    dve.tensor_tensor(w, w, p.bk[0][:, 0:D].unsqueeze(1).to_broadcast([P, FC, D]), ALU.subtract).then_inc(s.sem, 1)
    dve.wait_ge(p.wcopy.sem, p.wcopy.at(3 * e + 2))
    dve.tensor_tensor(p.w1l[:, f], p.sa[:, f], f32(p.w1h[:, f]), ALU.subtract).then_inc(s.sem, 1)


def moe_weights_act(act, p, e):
    s, f = p.wcopy, bass.ds(e * F, F)
    if isinstance(e, int) and e == 0:
        act.wait_ge(p.dma_tables.sem, p.dma_tables.at(32))
    act.wait_ge(p.wpe.sem, p.wpe.at(2 * e))
    act.activation(p.be1s.rearrange("p (c d) -> p c d", d=D),
                   p.be1[:, bass.ds(e * FC, FC)].unsqueeze(2).to_broadcast([P, FC, D]), ACT.Copy).then_inc(s.sem, 1)
    act.wait_ge(p.wts.sem, p.wts.at(NWT * e + 2))
    act.activation(p.w1h[:, f], p.sa[:, f], ACT.Copy).then_inc(s.sem, 1)
    act.wait_ge(p.wpe.sem, p.wpe.at(2 * e + 2))
    act.activation(p.sc[:, bass.ds(e * F, D)], p.bk[2][:, 0:D], ACT.Copy).then_inc(s.sem, 1)


def moe_last_row_pe(pe, p, e):
    pe.wait_ge(p.wts.sem, p.wts.at(NWT * e))
    pe.matmul(p.bk[1][:], p.ones_1[0:1, :], p.w1_last[:, bass.ds(e * F, F)], start=True, stop=True)\
      .then_inc(p.wlast.sem, 1)


def moe_weights_pe(pe, p, e):
    pe.wait_ge(p.wts.sem, p.wts.at(NWT * e + 1))
    for c in range(FC):
        ins = pe.matmul(p.bk[0][:, 0:D], p.ones_f[:], p.w2c[:, bass.ds((e * FC + c) * D, D)],
                        start=(c == 0), stop=(c == FC - 1))
    ins.then_inc(p.wpe.sem, 1)
    pe.wait_ge(p.wcopy.sem, p.wcopy.at(3 * e + 1))
    for c in range(FC):
        ins = pe.matmul(p.bk[2][:, 0:D], p.be1s[:, c * P:(c + 1) * P], p.sc[:, bass.ds((e * FC + c) * D, D)],
                        start=(c == 0), stop=(c == FC - 1))
    ins.then_inc(p.wpe.sem, 1)


I1, SI = 176, 352
ROWS = E * I1 + SI
NCH = -(-ROWS // P)
HRING = 7
E1 = E + 1
PIECES = [(c, e) for c in range(NCH) for e in range(E1)
          if e * I1 < (c + 1) * P and c * P < (e * I1 + I1 if e < E else ROWS)]
FIRST = {e: min(c for c, x in PIECES if x == e) for e in range(E1)}
LAST = {e: max(c for c, x in PIECES if x == e) for e in range(E1)}
DBANK = [4, 5, 7]


def rows_of(c):
    return slice(c * P, min((c + 1) * P, ROWS))


def sw_gu(pe, p, g, c, par):
    n, rows = NCH * g + c, rows_of(c)
    m = rows.stop - rows.start
    for w_h, w_l, bank, done, freed in ((p.wgh, p.wgl, p.bk[c % 2], p.gt_rows, p.silu_d),
                                        (p.wuh, p.wul, p.bk[2 + c % 2], p.up_rows, p.hid_d)):
        if not isinstance(n, int) or n >= 2:
            pe.wait_ge(freed.sem, freed.at(n - 1))
        pe.matmul(bank[0:m, :], w_h[:, rows], p.xh[:, par, :], start=True, stop=False)
        pe.matmul(bank[0:m, :], w_l[:, rows], p.xh[:, par, :], start=False, stop=False)
        pe.matmul(bank[0:m, :], w_h[:, rows], p.xl[:, par, :], start=False, stop=True).then_inc(done.sem, 1)


def sw_down(pe, p, g, c):
    n, m = NCH * g + c, rows_of(c).stop - c * P
    pe.wait_ge(p.hid_d.sem, p.hid_d.at(n + 1))
    for q, (cc, e) in enumerate(PIECES):
        if cc != c:
            continue
        bank = p.bk[DBANK[e % 3]]
        if c == FIRST[e]:
            pe.wait_ge(p.exp_add.sem, p.exp_add.at(TG * (E1 * g + e - 2) if e >= 2 else TG * E1 * g))
        for j in range(TG):
            ins = pe.matmul(bank[:, j * P:(j + 1) * P], p.hT[0:m, c % HRING, j * P:(j + 1) * P],
                            p.wd[0:m, q * D:(q + 1) * D], start=(c == FIRST[e] and j == 0),
                            stop=(c == LAST[e]), skip_group_check=True)
        if c == LAST[e]:
            ins.then_inc(p.exp_d.sem, 1)


def sw_pe_group(pe, p, g, par, last):
    for c in range(2, NCH):
        sw_gu(pe, p, g, c, par)
        sw_down(pe, p, g, c - 2)
        if c == 7 and not last:
            pe.wait_ge(p.rt2.sem, p.rt2.at(7 * g + 7))
            x_transpose(pe, p, g + 1, p.xf, p.bk[6])
        if c == 10 and not last:
            router_logits(pe, p, g + 1, 1 - par, p.bk[6], p.wr1h[:], p.wr1l[:], NL)
    for c in range(2):
        if not last:
            sw_gu(pe, p, g + 1, c, 1 - par)
        sw_down(pe, p, g, NCH - 2 + c)


def sw_pe(pe, p):
    x_transpose(pe, p, 0, p.xf, p.bk[6])
    router_logits(pe, p, 0, 0, p.bk[6], p.wr1h[:], p.wr1l[:], NL)
    for c in range(2):
        sw_gu(pe, p, 0, c, 0)
    with pe.Fori(0, NG // 2 - 1) as i:
        sw_pe_group(pe, p, 2 * i, 0, False)
        sw_pe_group(pe, p, 2 * i + 1, 1, False)
    sw_pe_group(pe, p, NG - 2, 0, False)
    sw_pe_group(pe, p, NG - 1, 1, True)


def sw_silu(act, p, g, c):
    n, m = NCH * g + c, rows_of(c).stop - c * P
    act.wait_ge(p.gt_rows.sem, p.gt_rows.at(n + 1))
    if not isinstance(n, int) or n >= 2:
        act.wait_ge(p.hid_d.sem, p.hid_d.at(n - 1))
    act.activation(p.sg[0:m, c % 2, :], p.bk[c % 2][0:m, :], ACT.Silu).then_inc(p.silu_d.sem, 1)


def router_shared_exp(act, p, g):
    act.activation(p.rt_g[:], p.rt_l[:, :, E], ACT.Exp, scale=-1.0).then_inc(p.rtg.sem, 1)


def sw_act_group(act, p, g, par, last):
    for c in range(2, NCH):
        sw_silu(act, p, g, c)
        if c == 8 and not last:
            x_high(act, p, g + 1, 1 - par, p.bk[6])
        if c == 12 and not last:
            router_exp(act, p, g + 1)
            router_shared_exp(act, p, g + 1)
    if not last:
        for c in range(2):
            sw_silu(act, p, g + 1, c)


def sw_act(act, p):
    x_high(act, p, 0, 0, p.bk[6])
    router_exp(act, p, 0)
    router_shared_exp(act, p, 0)
    for c in range(2):
        sw_silu(act, p, 0, c)
    with act.Fori(0, NG // 2 - 1) as i:
        sw_act_group(act, p, 2 * i, 0, False)
        sw_act_group(act, p, 2 * i + 1, 1, False)
    sw_act_group(act, p, NG - 2, 0, False)
    sw_act_group(act, p, NG - 1, 1, True)


def router_shared_gate(dve, p, g, gate):
    dve.wait_ge(p.rtg.sem, p.rtg.at(g + 1))
    dve.tensor_scalar(p.rt_g[:], p.rt_g[:], 2.0, 2.0, ALU.mult, ALU.add).then_inc(p.rt3.sem, 1)
    dve.wait_ge(p.rt3.sem, p.rt3.at(2 * g + 1))
    dve.reciprocal(gate[:, :, E], p.rt_g[:]).then_inc(p.rt3.sem, 1)


def sw_product(dve, p, g, c):
    n, m = NCH * g + c, rows_of(c).stop - c * P
    dve.wait_ge(p.silu_d.sem, p.silu_d.at(n + 1))
    dve.wait_ge(p.up_rows.sem, p.up_rows.at(n + 1))
    dve.tensor_tensor(p.hT[0:m, c % HRING, :], p.sg[0:m, c % 2, :], p.bk[2 + c % 2][0:m, :], ALU.mult)\
       .then_inc(p.hid_d.sem, 1)


def sw_add(dve, p, g, e, par):
    n = E1 * g + e
    dve.wait_ge(p.exp_d.sem, p.exp_d.at(n + 1))
    dve.wait_ge(p.exp_add.sem, p.exp_add.at(TG * n))
    if e == 0:
        dve.wait_ge(p.rt2.sem, p.rt2.at(7 * g + 7))
        dve.wait_ge(p.rt3.sem, p.rt3.at(2 * g + 2))
    for j in range(TG):
        x = p.X[:, g * TG + j, :]
        dve.scalar_tensor_tensor(out=x, in0=p.bk[DBANK[e % 3]][:, j * P:(j + 1) * P],
                                 scalar=p.gate1[:, par, j, e:e + 1], in1=x, op0=ALU.mult, op1=ALU.add)\
           .then_inc(p.exp_add.sem, 1)


def sw_router(dve, p, g, par):
    router_top(dve, p, g, p.bk[6], NL)
    router_gate(dve, p, g, p.gate1[:, par], False)
    router_shared_gate(dve, p, g, p.gate1[:, par])


def sw_dve_group(dve, p, g, par, last, after):
    for c in range(2, NCH):
        sw_product(dve, p, g, c)
        if c < 2 + TOP and not last and after:
            combine_dve(dve, p, g + 1, p.sw_taken, (c - 2,))
        if c == 2 + TOP and not last:
            if after:
                dve.wait_ge(p.comb.sem, p.comb.at(TOP * TG * (g + 2)))
            ln_stats(dve, p, g + 1)
        if c == 6 and not last:
            ln_apply(dve, p, g + 1, p.xf, P)
        if c == 9 and not last:
            x_low(dve, p, g + 1, 1 - par, p.bk[6])
        if c == 12 and not last:
            sw_router(dve, p, g + 1, 1 - par)
        for e in range(E1):
            if LAST[e] == c - 3:
                sw_add(dve, p, g, e, par)
    for c in range(2):
        if not last:
            sw_product(dve, p, g + 1, c)
        for e in range(E1):
            if LAST[e] == NCH - 3 + c:
                sw_add(dve, p, g, e, par)
    sw_add(dve, p, g, E, par)


def sw_dve(dve, p, after):
    if after:
        combine_dve(dve, p, 0, p.sw_taken)
        dve.wait_ge(p.comb.sem, p.comb.at(TOP * TG))
    ln_stats(dve, p, 0)
    ln_apply(dve, p, 0, p.xf, P)
    x_low(dve, p, 0, 0, p.bk[6])
    sw_router(dve, p, 0, 0)
    for c in range(2):
        sw_product(dve, p, 0, c)
    with dve.Fori(0, NG // 2 - 1) as i:
        sw_dve_group(dve, p, 2 * i, 0, False, after)
        sw_dve_group(dve, p, 2 * i + 1, 1, False, after)
    sw_dve_group(dve, p, NG - 2, 0, False, after)
    sw_dve_group(dve, p, NG - 1, 1, True, after)


def sw_pool(pool, p, after):
    if after:
        combine_begin_pool(pool, p, p.sw_taken)
        with pool.Fori(0, NG - 1) as g:
            ln_scale(pool, p, g)
            combine_group_pool(pool, p, g + 1, p.sw_taken)
        ln_scale(pool, p, NG - 1)
    else:
        with pool.Fori(0, NG) as g:
            ln_scale(pool, p, g)


def sw_weights_dve(dve, p):
    dve.wait_ge(p.dma_sw.sem, p.dma_sw.at(48))
    s = p.wsw
    for w, h, l in ((p.sa[:, 0:ROWS], p.wgh, p.wgl), (p.sa[:, ROWS:2 * ROWS], p.wuh, p.wul),
                    (p.wr1_f[:], p.wr1h, p.wr1l)):
        dve.tensor_copy(h[:], w).then_inc(s.sem, 1)
    dve.wait_ge(s.sem, s.at(3))
    for w, h, l in ((p.sa[:, 0:ROWS], p.wgh, p.wgl), (p.sa[:, ROWS:2 * ROWS], p.wuh, p.wul),
                    (p.wr1_f[:], p.wr1h, p.wr1l)):
        dve.tensor_tensor(l[:], w, f32(h[:]), ALU.subtract).then_inc(s.sem, 1)


QK, H, GROUP, MAXREL = 32, 256, 64, 32
NB2 = 2
NQ = 2 * QK


def ga_project_pe(pe, p, b):
    pe.wait_ge(p.ga_xc.sem, p.ga_xc.at(b + 1))
    pe.wait_ge(p.ga_qk.sem, p.ga_qk.at(b))
    pe.matmul(p.bk[0][0:NQ, S:2 * S], p.ga_w[:, 0:NQ], p.ga_xa[:], start=True, stop=True).then_inc(p.ga_qkp.sem, 1)
    pe.wait_ge(p.ga_vg.sem, p.ga_vg.at(NB2 * b))
    for t in range(NB2):
        pe.matmul(p.bk[1 + t][:], p.ga_xa[:, t * P:(t + 1) * P], p.ga_w[:, NQ:], start=True, stop=True)\
          .then_inc(p.ga_vgp.sem, 1)


def ga_swap_pe(pe, p, b):
    pe.wait_ge(p.ga_hd.sem, p.ga_hd.at(2 * b + 2))
    pe.sem_inc(p.pe_passed.sem, 1)
    pe.matmul(p.bk[3][0:NQ, :], p.ga_perm[:], flat(p.ga_h[:]), start=True, stop=True).then_inc(p.ga_sw.sem, 1)


def ga_x_pe(pe, p, b):
    pe.wait_ge(p.ga_xc.sem, p.ga_xc.at(b))
    x_transpose(pe, p, b, p.xn[:, 0], p.bk[0], NB2)


def ga_turn_out_pe(pe, p, b):
    pe.wait_ge(p.ga_o.sem, p.ga_o.at(b + 1))
    pe.wait_ge(p.ga_y.sem, p.ga_y.at(5 * b))
    for q in range(NB2 * 2):
        ins = pe.transpose(p.bk[7][:, q * P:(q + 1) * P], p.ga_g[:, q // 2, (q % 2) * P:(q % 2 + 1) * P], p.ident)
    ins.then_inc(p.ga_otp.sem, 1)


def ga_out_pe(pe, p, b):
    pe.wait_ge(p.ga_ot.sem, p.ga_ot.at(b + 1))
    for t in range(NB2):
        for c in range(2):
            q = t * 2 + c
            ins = pe.matmul(p.bk[7][:, t * P:(t + 1) * P], p.ga_t[:, q * P:(q + 1) * P],
                            p.ga_wo[:, c * P:(c + 1) * P], start=(c == 0), stop=(c == 1))
    ins.then_inc(p.ga_wop.sem, 1)


def ga_pe_element(pe, p, b, par, behind=True, last=False):
    rp, vg = p.ga_r[:, par], p.ga_v[:, par]
    pe.wait_ge(p.ga_rp.sem, p.ga_rp.at(3 * b + 3))
    pe.wait_ge(p.ga_at.sem, p.ga_at.at(2 * b))
    for t in range(NB2):
        c = slice(t * P, (t + 1) * P)
        ins = pe.matmul(p.bk[5][:, c], rp[0:QK, 1, c], rp[0:QK, 0, c], start=True, stop=True)
    ins.then_inc(p.ga_scp.sem, 1)
    pe.wait_ge(p.ga_o.sem, p.ga_o.at(b))
    pe.sem_inc(p.pe_passed.sem, 1)
    for t in range(NB2):
        ins = pe.transpose(p.bk[6][:, t * NQ:(t + 1) * NQ], rp[:, 1, t * P:(t + 1) * P], p.ident[0:NQ, 0:NQ])
    ins.then_inc(p.ga_lkp.sem, 1)
    if not last:
        ga_x_pe(pe, p, b + 1)
    if behind:
        ga_turn_out_pe(pe, p, b - 1)
    pe.wait_ge(p.ga_lk.sem, p.ga_lk.at(b + 1))
    pe.wait_ge(p.ga_kv.sem, p.ga_kv.at(b))
    pe.wait_ge(p.ga_vg.sem, p.ga_vg.at(NB2 * b + NB2))
    for t in range(NB2):
        ins = pe.matmul(p.bk[4][0:NQ, 0:H], p.ga_k[:, t * NQ:(t + 1) * NQ], vg[:, t, 0:H],
                        start=(t == 0), stop=(t == NB2 - 1))
    ins.then_inc(p.ga_kvp.sem, 1)
    if not last:
        ga_project_pe(pe, p, b + 1)
    if behind:
        ga_out_pe(pe, p, b - 1)
    if not last:
        ga_swap_pe(pe, p, b + 1)
    pe.wait_ge(p.ga_at.sem, p.ga_at.at(2 * b + 2))
    pe.wait_ge(p.ga_kv.sem, p.ga_kv.at(b + 1))
    for t in range(NB2):
        o, c = p.bk[6][:, t * H:(t + 1) * H], slice(t * P, (t + 1) * P)
        pe.matmul(o, p.ga_a[:, t, :], vg[:, t, 0:H], start=True, stop=False)
        ins = pe.matmul(o, rp[QK:NQ, 0, c], p.ga_s[QK:NQ, :], start=False, stop=True)
    ins.then_inc(p.ga_op.sem, 1)


def ga_pe(pe, p):
    ga_x_pe(pe, p, 0)
    ga_project_pe(pe, p, 0)
    ga_swap_pe(pe, p, 0)
    ga_pe_element(pe, p, 0, 0, behind=False)
    ga_pe_element(pe, p, 1, 1)
    with pe.Fori(1, B // 2 - 1) as i:
        ga_pe_element(pe, p, 2 * i, 0)
        ga_pe_element(pe, p, 2 * i + 1, 1)
    ga_pe_element(pe, p, B - 2, 0)
    ga_pe_element(pe, p, B - 1, 1, last=True)
    ga_turn_out_pe(pe, p, B - 1)
    ga_out_pe(pe, p, B - 1)


def ga_x_act(act, p, b):
    act.wait_ge(p.xt.sem, p.xt.at(b + 1))
    act.wait_ge(p.ga_vgp.sem, p.ga_vgp.at(NB2 * b))
    act.activation(p.ga_xa[:], p.bk[0][:, 0:S], ACT.Copy).then_inc(p.ga_xc.sem, 1)


def ga_silu_act(act, p, b, par):
    act.wait_ge(p.ga_qkp.sem, p.ga_qkp.at(b + 1))
    act.wait_ge(p.ga_hd.sem, p.ga_hd.at(2 * b))
    act.activation(p.ga_q[:], p.bk[0][0:NQ, S:2 * S], ACT.Silu).then_inc(p.ga_qk.sem, 1)
    if not isinstance(b, int) or b >= 1:
        act.wait_ge(p.ga_o.sem, p.ga_o.at(b - 1))
    for t in range(NB2):
        act.wait_ge(p.ga_vgp.sem, p.ga_vgp.at(NB2 * b + t + 1))
        act.activation(p.ga_v[:, par, t, :], p.bk[1 + t][:], ACT.Silu).then_inc(p.ga_vg.sem, 1)


def ga_turn_out_act(act, p, b):
    act.wait_ge(p.ga_otp.sem, p.ga_otp.at(b + 1))
    act.activation(p.ga_t, p.bk[7][:], ACT.Copy).then_inc(p.ga_ot.sem, 1)


def ga_act_element(act, p, b, par, behind=True, last=False):
    act.wait_ge(p.ga_lkp.sem, p.ga_lkp.at(b + 1))
    act.activation(p.ga_k, p.bk[6][:, 0:P], ACT.Copy).then_inc(p.ga_lk.sem, 1)
    if not last:
        ga_x_act(act, p, b + 1)
    if behind:
        ga_turn_out_act(act, p, b - 1)
    act.wait_ge(p.ga_kvp.sem, p.ga_kvp.at(b + 1))
    act.activation(p.ga_s, p.bk[4][0:NQ, 0:H], ACT.Copy, scale=1.0 / S).then_inc(p.ga_kv.sem, 1)
    if not last:
        ga_silu_act(act, p, b + 1, 1 - par)


def ga_act(act, p):
    ga_x_act(act, p, 0)
    ga_silu_act(act, p, 0, 0)
    ga_act_element(act, p, 0, 0, behind=False)
    ga_act_element(act, p, 1, 1)
    with act.Fori(1, B // 2 - 1) as i:
        ga_act_element(act, p, 2 * i, 0)
        ga_act_element(act, p, 2 * i + 1, 1)
    ga_act_element(act, p, B - 2, 0)
    ga_act_element(act, p, B - 1, 1, last=True)
    ga_turn_out_act(act, p, B - 1)


def ga_heads_dve(dve, p, b):
    dve.wait_ge(p.ga_qk.sem, p.ga_qk.at(b + 1))
    dve.wait_ge(p.ga_sw.sem, p.ga_sw.at(b))
    for n in range(2):
        dve.tensor_scalar(p.ga_h[:, n, :], p.ga_q[:], p.ga_gb[:, 2 * n:2 * n + 1], p.ga_gb[:, 2 * n + 1:2 * n + 2],
                          ALU.mult, ALU.add).then_inc(p.ga_hd.sem, 1)


def by_position(table):
    return table[:].unsqueeze(1).to_broadcast([NQ, 2, S])


def ga_cos_dve(dve, p, b):
    dve.wait_ge(p.ga_hd.sem, p.ga_hd.at(2 * b + 2))
    dve.tensor_tensor(p.ga_r1[:], p.ga_h[:], by_position(p.ga_cos), ALU.mult).then_inc(p.ga_rp.sem, 1)


def ga_sin_dve(dve, p, b, par):
    dve.wait_ge(p.ga_sw.sem, p.ga_sw.at(b + 1))
    dve.tensor_tensor(p.ga_r2[:], p.bk[3][0:NQ, :].rearrange("p (a s) -> p a s", a=2), by_position(p.ga_sin), ALU.mult)\
       .then_inc(p.ga_rp.sem, 1)
    dve.wait_ge(p.ga_rp.sem, p.ga_rp.at(3 * b + 2))
    dve.tensor_tensor(p.ga_r[:, par], p.ga_r1[:], p.ga_r2[:], ALU.add).then_inc(p.ga_rp.sem, 1)


def ga_moments_dve(dve, p, b):
    dve.wait_ge(p.ga_wop.sem, p.ga_wop.at(b + 1))
    dve.wait_ge(p.ga_x.sem, p.ga_x.at(NB2 * b))
    dve.tensor_tensor(p.ga_yy, p.bk[7][:, 0:S].rearrange("p (t d) -> p t d", t=NB2),
                      p.ga_bo[:].unsqueeze(1).to_broadcast([P, NB2, D]), ALU.add).then_inc(p.ga_y.sem, 1)
    dve.wait_ge(p.ga_y.sem, p.ga_y.at(5 * b + 1))
    for t in range(NB2):
        dve.bn_stats(p.ga_st[:, t, :], p.ga_yy[:, t, :]).then_inc(p.ga_y.sem, 1)
    dve.wait_ge(p.ga_y.sem, p.ga_y.at(5 * b + 3))
    dve.sem_inc(p.dve_passed.sem, 1)
    for t in range(NB2):
        dve.bn_aggr(p.ga_mv[:, t, :], p.ga_st[:, t, :]).then_inc(p.ga_y.sem, 1)
    dve.wait_ge(p.ga_y.sem, p.ga_y.at(5 * b + 5))
    for t in range(NB2):
        dve.scalar_tensor_tensor(out=p.ga_z[:, t, :], in0=p.ga_yy[:, t, :], scalar=p.ga_mv[:, t, 0:1], in1=p.ga_w2[:],
                                 op0=ALU.subtract, op1=ALU.mult).then_inc(p.ga_yn.sem, 1)


def ga_residual_dve(dve, p, b):
    dve.wait_ge(p.ga_yn.sem, p.ga_yn.at(NB2 * b + NB2))
    dve.wait_ge(p.ga_rs.sem, p.ga_rs.at(2 * b + 2))
    dve.wait_ge(p.ga_px.sem, p.ga_px.at(b + 1))
    for t in range(NB2):
        x = p.X[:, b * NB2 + t, :]
        dve.scalar_tensor_tensor(out=x, in0=p.ga_z[:, t, :], scalar=p.ga_sc[:, t:t + 1], in1=x,
                                 op0=ALU.mult, op1=ALU.add).then_inc(p.ga_x.sem, 1)


def ga_dve_element(dve, p, b, par, behind=2, last=False, more=True, group=None):
    dve.wait_ge(p.ga_scp.sem, p.ga_scp.at(b + 1))
    dve.scalar_tensor_tensor(out=p.ga_a1, in0=p.bk[5][:, 0:S].rearrange("p (t k) -> p t k", t=NB2),
                             scalar=1.0 / GROUP, in1=p.ga_bias[:].unsqueeze(1).to_broadcast([P, NB2, P]),
                             op0=ALU.mult, op1=ALU.add).then_inc(p.ga_at.sem, 1)
    dve.wait_ge(p.ga_at.sem, p.ga_at.at(2 * b + 1))
    dve.scalar_tensor_tensor(out=p.ga_a, in0=p.ga_a1, scalar=0.0, in1=p.ga_a1,
                             op0=ALU.max, op1=ALU.mult).then_inc(p.ga_at.sem, 1)
    if behind >= 2:
        ga_residual_dve(dve, p, b - 2)
    if not last:
        ga_heads_dve(dve, p, b + 1)
        ga_cos_dve(dve, p, b + 1)
    if group is not None:
        combine_dve(dve, p, group, p.ga_taken)
        dve.wait_ge(p.comb.sem, p.comb.at(TOP * TG * (group + 1)))
    if more:
        ln_stats(dve, p, b + 2, NB2)
    if not last:
        ga_sin_dve(dve, p, b + 1, 1 - par)
    dve.wait_ge(p.ga_op.sem, p.ga_op.at(b + 1))
    dve.wait_ge(p.ga_otp.sem, p.ga_otp.at(b))
    dve.tensor_tensor(p.ga_g, p.bk[6][:].rearrange("p (t h) -> p t h", t=NB2), p.ga_v[:, par, :, H:], ALU.mult)\
       .then_inc(p.ga_o.sem, 1)
    if more:
        ln_apply(dve, p, b + 2, p.xn[:, 0], P - 1, NB2, True)
    if behind >= 1:
        ga_moments_dve(dve, p, b - 1)


def ga_dve_pair(dve, p, i, first=False, last=False):
    ga_dve_element(dve, p, 2 * i, 0, behind=0 if first else 2, more=not last, group=None if last else i + 1)
    ga_dve_element(dve, p, 2 * i + 1, 1, behind=1 if first else 2, last=last, more=not last)


def ga_dve(dve, p):
    combine_dve(dve, p, 0, p.ga_taken)
    dve.wait_ge(p.comb.sem, p.comb.at(TOP * TG))
    ln_stats(dve, p, 0, NB2)
    ln_apply(dve, p, 0, p.xn[:, 0], P - 1, NB2, True)
    ln_stats(dve, p, 1, NB2)
    ga_heads_dve(dve, p, 0)
    ga_cos_dve(dve, p, 0)
    ga_sin_dve(dve, p, 0, 0)
    ln_apply(dve, p, 1, p.xn[:, 0], P - 1, NB2, True)
    ga_dve_pair(dve, p, 0, first=True)
    with dve.Fori(1, B // 2 - 1) as i:
        ga_dve_pair(dve, p, i)
    ga_dve_pair(dve, p, B // 2 - 1, last=True)
    ga_residual_dve(dve, p, B - 2)
    ga_moments_dve(dve, p, B - 1)
    ga_residual_dve(dve, p, B - 1)


def ga_out_pool(pool, p, b):
    pool.wait_ge(p.ga_y.sem, p.ga_y.at(5 * b + 5))
    pool.tensor_tensor(p.ga_ve, p.ga_mv[:, :, 1], p.eps8[:, 0:NB2], ALU.add).then_inc(p.ga_rs.sem, 1)
    pool.wait_ge(p.ga_rs.sem, p.ga_rs.at(2 * b + 1))
    pool.tensor_tensor(p.ga_sc, p.ga_ve, p.neg_half[:, 0:NB2], ALU.pow).then_inc(p.ga_rs.sem, 1)
    x = p.X[:, bass.ds(b * NB2, NB2), :]
    pool.tensor_tensor(x, x, p.ga_b2[:].unsqueeze(1).to_broadcast([P, NB2, D]), ALU.add).then_inc(p.ga_px.sem, 1)


def ga_pool_pair(pool, p, i, first=False, ahead=True, more=True):
    if ahead:
        combine_rows_pool(pool, p, i + 2)
    for k in range(TOP):
        if more:
            ln_scale(pool, p, 2 * i + k + 2, NB2, True)
        if ahead:
            combine_pool(pool, p, i + 2, p.ga_taken, k)
        if not (first and k == 0):
            ga_out_pool(pool, p, 2 * i + k - 1)


def ga_pool(pool, p):
    combine_begin_pool(pool, p, p.ga_taken)
    ln_scale(pool, p, 0, NB2, True)
    ln_scale(pool, p, 1, NB2, True)
    combine_group_pool(pool, p, 1, p.ga_taken)
    ga_pool_pair(pool, p, 0, first=True)
    with pool.Fori(1, NG - 2) as i:
        ga_pool_pair(pool, p, i)
    ga_pool_pair(pool, p, NG - 2, ahead=False)
    ga_pool_pair(pool, p, NG - 1, ahead=False, more=False)
    ga_out_pool(pool, p, B - 1)


def ga_bias_pool(pool, p):
    pool.wait_ge(p.dma_ga.sem, p.dma_ga.at(p.nga))
    pool.tensor_tensor(p.ga_bias[:], p.ga_bias[:], p.ga_mask[:], ALU.add).then_inc(p.gab.sem, 1)


def ga_weights_pe(pe, p):
    pe.wait_ge(p.dma_ga.sem, p.dma_ga.at(p.nga))
    for n, c in enumerate((slice(0, NQ), slice(NQ, NQ + 2 * H))):
        out = p.bk[n][:, 0:c.stop - c.start]
        pe.matmul(out, p.ga_ln_b[:], p.ga_w[:, c], start=True, stop=False)
        ins = pe.matmul(out, p.e_last[:], p.ga_brow[:, c], start=False, stop=True)
    ins.then_inc(p.gaw.sem, 1)
    pe.wait_ge(p.gaw.sem, p.gaw.at(6))


def ga_weights_dve(dve, p):
    dve.wait_ge(p.dma_ga.sem, p.dma_ga.at(p.nga))
    dve.wait_ge(p.gaw.sem, p.gaw.at(1))
    dve.tensor_scalar(p.ga_w[:], p.ga_w[:], p.ga_ln_w[:, 0:1], None, ALU.mult).then_inc(p.gaw.sem, 1)
    dve.tensor_scalar(p.ga_last[:], p.ga_last[:], p.ga_ln_w[:, 1:2], None, ALU.mult).then_inc(p.gaw.sem, 1)
    dve.wait_ge(p.gaw.sem, p.gaw.at(3))
    dve.tensor_tensor(p.ga_w[:], p.ga_w[:], p.ga_last[:], ALU.subtract).then_inc(p.gaw.sem, 1)
    dve.wait_ge(p.gaw.sem, p.gaw.at(4))
    dve.tensor_tensor(p.ga_w[:, 0:NQ], p.ga_w[:, 0:NQ], p.bk[0][:, 0:NQ], ALU.add).then_inc(p.gaw.sem, 1)
    dve.tensor_tensor(p.ga_w[:, NQ:], p.ga_w[:, NQ:], p.bk[1][:], ALU.add).then_inc(p.gaw.sem, 1)


NH, HD = 16, 8
HR = 32
HQ = P // HR
NHQ = NH // HQ
NPROD = 3 * HD
LATENT = 64
ATT_SCALE = 1.0 / float(np.sqrt(NH + 2 * LATENT))
SEARCH_BANKS = (1, 2, 5)
HALF_BANKS = (6, 0)
OUT_BANKS = (5, 6)
LAG = 2
NS1 = 12


def at_x_pe(pe, p, b):
    pe.wait_ge(p.at_kr.sem, p.at_kr.at(b))
    x_transpose(pe, p, b, p.xn[:, 0], p.bk[0], NB2)


def at_latent_pe(pe, p, b):
    pe.wait_ge(p.at_xc.sem, p.at_xc.at(b + 1))
    pe.matmul(p.bk[0][:, S:2 * S], p.at_w[:, 0:P], p.at_xa, start=True, stop=True).then_inc(p.at_ctp.sem, 1)


def at_kr_pe(pe, p, b):
    pe.wait_ge(p.at_ct.sem, p.at_ct.at(b + 1))
    for t in range(NB2):
        c = slice(t * P, (t + 1) * P)
        ins = pe.matmul(p.bk[0][:, c], p.at_xa[:, c], p.at_w[:, P:2 * P], start=True, stop=True)
    ins.then_inc(p.at_krp.sem, 1)


def at_project_pe(pe, p, b):
    pe.wait_ge(p.at_mx.sem, p.at_mx.at(NH * b))
    for n in range(2):
        r = slice(n * LATENT, (n + 1) * LATENT)
        for t in range(NB2):
            ins = pe.matmul(p.bk[1 + n][:, 2 * t * D:2 * (t + 1) * D], p.at_c[r, t * P:(t + 1) * P], p.at_u[r, :],
                            start=True, stop=True)
        ins.then_inc(p.at_prp.sem, 1)


def at_turn_pe(pe, p, t, which, bank):
    for q in range(NHQ):
        src = p.at_sk[:, which, t, q * HQ:(q + 1) * HQ, :].rearrange("p h r -> p (h r)")
        ins = pe.transpose(bank[:, q * P:(q + 1) * P], src, p.ident)
    return ins


def at_keys_pe(pe, p, b):
    pe.wait_ge(p.at_q.sem, p.at_q.at(NS1 * (b + 1)))
    pe.wait_ge(p.at_hc.sem, p.at_hc.at(2 * b + 2))
    for t in range(NB2):
        at_turn_pe(pe, p, t, 1, p.bk[1 + t]).then_inc(p.at_ktp.sem, 1)


def at_queries_pe(pe, p, b):
    for t in range(NB2):
        pe.wait_ge(p.at_kt.sem, p.at_kt.at(NB2 * b + t + 1))
        at_turn_pe(pe, p, t, 0, p.bk[1 + t]).then_inc(p.at_qtp.sem, 1)


def at_maxima_rows_pe(pe, p, b, half):
    pe.wait_ge(p.at_nm.sem, p.at_nm.at(4 * b + 2 * half + 2))
    bank = p.bk[HALF_BANKS[half]]
    for q in range(NHQ // 2):
        for t in range(NB2):
            src = p.at_sk[:, 0, t, half * NH // 2 + q * HQ:half * NH // 2 + (q + 1) * HQ, :].rearrange("p h r -> p (h r)")
            ins = pe.transpose(bank[:, q * S + t * P:q * S + (t + 1) * P], src, p.ident)
    ins.then_inc(p.at_q2p.sem, 1)


def searched(f):
    half, f = divmod(f, NH // 2)
    t, m = divmod(f, HQ)
    return t, half * HQ + m


def head_rows(h, n):
    return slice(HR * (h % HQ), HR * (h % HQ) + n)


def at_search_pe(pe, p, b, par, f):
    t, pair = searched(f)
    if f == 0:
        pe.wait_ge(p.at_qt.sem, p.at_qt.at(NB2 * b + NB2))
    if f >= 3:
        pe.wait_ge(p.at_mx.sem, p.at_mx.at(NH * b + f - 2))
    for n in range(2):
        h = pair % HQ + HQ * (2 * (pair // HQ) + n)
        r = head_rows(h, NPROD)
        ins = pe.matmul(p.bk[SEARCH_BANKS[f % 3]][:, n * S:(n + 1) * S], p.at_qT[r, h // HQ, t * P:(t + 1) * P],
                        p.at_kT[par][r, h // HQ, :], start=True, stop=True)
    ins.then_inc(p.at_s1.sem, 1)


def at_scores_pe(pe, p, b, par, h):
    if h % (NH // 2) == 0:
        pe.wait_ge(p.at_q2.sem, p.at_q2.at(2 * b + 2 * h // NH + 1))
    if h >= 2:
        pe.wait_ge(p.at_ex.sem, p.at_ex.at(NH * b + h - 1))
    r = head_rows(h, NPROD + 2)
    for t in range(NB2):
        ins = pe.matmul(p.bk[3 + h % 2][:, t * S:(t + 1) * S], p.at_kT[par][r, h // HQ, t * P:(t + 1) * P],
                        p.at_qT2[r, h // HQ, :], start=True, stop=True)
    ins.then_inc(p.at_s2.sem, 1)


def at_values_pe(pe, p, b, par, a):
    pe.wait_ge(p.at_ex.sem, p.at_ex.at(NH * b + a + 1))
    if a % 8 == 0:
        pe.wait_ge(p.at_op.sem, p.at_op.at(2 * b + a // 8))
    o = p.bk[7][HR * (a % HQ):HR * (a % HQ + 1), (a // HQ) % 2 * S:((a // HQ) % 2 + 1) * S]
    for t in range(NB2):
        ins = pe.matmul(o, p.at_v[:, par, t, a, :], p.at_e[:, a % 4, t * S:(t + 1) * S],
                        start=(t == 0), stop=(t == NB2 - 1))
    ins.then_inc(p.at_av.sem, 1)


def at_out_turn_pe(pe, p, b):
    if not isinstance(b, int) or b >= 1:
        pe.wait_ge(p.at_x.sem, p.at_x.at(b))
    pe.wait_ge(p.at_op.sem, p.at_op.at(2 * b + 2))
    for t in range(NB2):
        for q in range(NHQ):
            ins = pe.transpose(p.bk[OUT_BANKS[t]][:, q * P:(q + 1) * P], p.at_o[:, q, t * P:(t + 1) * P], p.ident)
    ins.then_inc(p.at_otp.sem, 1)


def at_out_back_pe(pe, p, b):
    pe.wait_ge(p.at_on.sem, p.at_on.at(4 * b + 4))
    for t in range(NB2):
        ins = pe.transpose(p.bk[6][:, t * P:(t + 1) * P], p.at_n[:, t, :], p.ident)
    ins.then_inc(p.at_tp.sem, 1)


def at_out_pe(pe, p, b):
    pe.wait_ge(p.at_ot.sem, p.at_ot.at(b + 1))
    for t in range(NB2):
        ins = pe.matmul(p.bk[6][:, S + t * P:S + (t + 1) * P], p.at_t[:, t * P:(t + 1) * P], p.at_wo, start=True, stop=True)
    ins.then_inc(p.at_wp.sem, 1)


def at_pe_element(pe, p, b, par, behind=True, ahead=2):
    for h in range(NH + LAG):
        if h < NH:
            at_scores_pe(pe, p, b, par, h)
        if h >= LAG:
            at_values_pe(pe, p, b, par, h - LAG)
        if h == 1:
            pe.wait_ge(p.at_kr.sem, p.at_kr.at(b + min(ahead, 1) + 1))
            at_maxima_rows_pe(pe, p, b, 1)
        if behind:
            if h == 2:
                at_out_turn_pe(pe, p, b - 1)
            elif h == 6:
                at_out_back_pe(pe, p, b - 1)
            elif h == 8:
                at_out_pe(pe, p, b - 1)
        if ahead >= 1:
            if h == 3:
                at_keys_pe(pe, p, b + 1)
            elif h == 5:
                at_queries_pe(pe, p, b + 1)
            if 7 <= h < NH - 1:
                for f in range(2 * (h - 7), 2 * (h - 6)):
                    at_search_pe(pe, p, b + 1, 1 - par, f)
            if h == 12:
                at_maxima_rows_pe(pe, p, b + 1, 0)
        if ahead >= 2:
            if h == 4:
                pe.wait_ge(p.at_q2.sem, p.at_q2.at(2 * b + 2))
                at_x_pe(pe, p, b + 2)
            elif h == 7:
                at_latent_pe(pe, p, b + 2)
            elif h == 9:
                at_kr_pe(pe, p, b + 2)
            elif h == NH + LAG - 1:
                at_project_pe(pe, p, b + 2)


def at_pe(pe, p):
    for b in range(2):
        at_x_pe(pe, p, b)
        at_latent_pe(pe, p, b)
        at_kr_pe(pe, p, b)
        if b == 0:
            pe.wait_ge(p.at_init.sem, p.at_init.at(5))
            at_project_pe(pe, p, 0)
            at_keys_pe(pe, p, 0)
            at_queries_pe(pe, p, 0)
    for f in range(NH):
        at_search_pe(pe, p, 0, 0, f)
    at_project_pe(pe, p, 1)
    at_maxima_rows_pe(pe, p, 0, 0)
    at_pe_element(pe, p, 0, 0, behind=False)
    at_pe_element(pe, p, 1, 1)
    with pe.Fori(1, B // 2 - 1) as i:
        at_pe_element(pe, p, 2 * i, 0)
        at_pe_element(pe, p, 2 * i + 1, 1)
    at_pe_element(pe, p, B - 2, 0, ahead=1)
    at_pe_element(pe, p, B - 1, 1, ahead=0)
    at_out_turn_pe(pe, p, B - 1)
    at_out_back_pe(pe, p, B - 1)
    at_out_pe(pe, p, B - 1)


def at_x_act(act, p, b):
    act.wait_ge(p.xt.sem, p.xt.at(b + 1))
    act.wait_ge(p.at_krp.sem, p.at_krp.at(b))
    act.activation(p.at_xa, p.bk[0][:, 0:S], ACT.Copy).then_inc(p.at_xc.sem, 1)


def at_latent_act(act, p, b):
    act.wait_ge(p.at_ctp.sem, p.at_ctp.at(b + 1))
    act.wait_ge(p.at_prp.sem, p.at_prp.at(2 * b))
    act.activation(p.at_c, p.bk[0][:, S:2 * S], ACT.Copy).then_inc(p.at_ct.sem, 1)


def at_kr_act(act, p, b):
    act.wait_ge(p.at_krp.sem, p.at_krp.at(b + 1))
    act.wait_ge(p.at_q.sem, p.at_q.at(NS1 * b))
    act.activation(p.at_r[:, 1], p.bk[0][:, 0:S].rearrange("p (t d) -> p t d", t=NB2), ACT.Copy)\
       .then_inc(p.at_kr.sem, 1)


def at_parts_act(act, p, b):
    act.wait_ge(p.at_q.sem, p.at_q.at(NS1 * b + 10))
    for which, c in ((0, HD), (1, 2 * HD)):
        act.activation(p.at_sk_r[:, which, :, :, c:c + HD], p.at_sk[:, which, :, :, 0:HD], ACT.Copy)\
           .then_inc(p.at_hc.sem, 1)


def at_turned_act(act, src, dst, t):
    return act.activation(dst[:, :, t * P:(t + 1) * P], src[:].rearrange("p (q t) -> p q t", q=NHQ), ACT.Copy)


def at_keys_act(act, p, b, par):
    for t in range(NB2):
        act.wait_ge(p.at_ktp.sem, p.at_ktp.at(NB2 * b + t + 1))
        at_turned_act(act, p.bk[1 + t], p.at_kT[par], t).then_inc(p.at_kt.sem, 1)


def at_queries_act(act, p, b):
    for t in range(NB2):
        act.wait_ge(p.at_qtp.sem, p.at_qtp.at(NB2 * b + t + 1))
        at_turned_act(act, p.bk[1 + t], p.at_qT, t).then_inc(p.at_qt.sem, 1)


def at_maxima_rows_act(act, p, b, half):
    act.wait_ge(p.at_q2p.sem, p.at_q2p.at(2 * b + half + 1))
    act.activation(flat(p.at_qT2[:, half * NHQ // 2:(half + 1) * NHQ // 2, :]), p.bk[HALF_BANKS[half]][:], ACT.Copy)\
       .then_inc(p.at_q2.sem, 1)


def at_heads_out_act(act, p, b, half):
    act.wait_ge(p.at_av.sem, p.at_av.at(NH * b + 8 * half + 8))
    act.activation(flat(p.at_o[:, 2 * half:2 * half + 2, :]), p.bk[7][:], ACT.Copy).then_inc(p.at_op.sem, 1)


def at_out_act(act, p, b):
    act.wait_ge(p.at_tp.sem, p.at_tp.at(b + 1))
    act.activation(p.at_t, p.bk[6][:, 0:S], ACT.Copy).then_inc(p.at_ot.sem, 1)


def at_act_element(act, p, b, par, behind=True, ahead=2):
    for h in range(NH):
        act.wait_ge(p.at_s2.sem, p.at_s2.at(NH * b + h + 1))
        if h >= 4:
            act.wait_ge(p.at_av.sem, p.at_av.at(NH * b + h - 3))
        act.activation(p.at_e[:, h % 4, :], p.bk[3 + h % 2][:], ACT.Exp, scale=ATT_SCALE).then_inc(p.at_ex.sem, 1)
        if h == 1:
            at_maxima_rows_act(act, p, b, 1)
        if h == 7 + LAG:
            at_heads_out_act(act, p, b, 0)
        if ahead >= 1:
            if h == 2:
                at_parts_act(act, p, b + 1)
            elif h == 4:
                at_keys_act(act, p, b + 1, 1 - par)
            elif h == 6:
                at_queries_act(act, p, b + 1)
            elif h == 12:
                at_maxima_rows_act(act, p, b + 1, 0)
        if ahead >= 2:
            if h == 5:
                at_x_act(act, p, b + 2)
            elif h == 8:
                at_latent_act(act, p, b + 2)
            elif h == 10:
                at_kr_act(act, p, b + 2)
        if behind and h == 7:
            at_out_act(act, p, b - 1)
    at_heads_out_act(act, p, b, 1)


def at_act(act, p):
    for b in range(2):
        at_x_act(act, p, b)
        at_latent_act(act, p, b)
        at_kr_act(act, p, b)
        if b == 0:
            act.wait_ge(p.at_init.sem, p.at_init.at(5))
            at_parts_act(act, p, 0)
            at_keys_act(act, p, 0, 0)
            at_queries_act(act, p, 0)
    at_maxima_rows_act(act, p, 0, 0)
    at_act_element(act, p, 0, 0, behind=False)
    at_act_element(act, p, 1, 1)
    with act.Fori(1, B // 2 - 1) as i:
        at_act_element(act, p, 2 * i, 0)
        at_act_element(act, p, 2 * i + 1, 1)
    at_act_element(act, p, B - 2, 0, ahead=1)
    at_act_element(act, p, B - 1, 1, ahead=0)
    at_out_act(act, p, B - 1)


def at_project_dve(dve, p, b, par):
    n = NS1 * b
    heads = "p t (h d) -> p t h d"
    for m, dst in ((0, p.at_r[:, 0]), (1, p.at_s[:, 0]), (2, p.at_s[:, 1]), (3, p.at_v[:, par, :, :, 0:HD])):
        dve.wait_ge(p.at_prp.sem, p.at_prp.at(2 * b + m // 2 + 1))
        src = p.bk[1 + m // 2][:].rearrange("p (t d) -> p t d", t=NB2)[:, :, (m % 2) * D:(m % 2 + 1) * D]
        bias = p.at_b[:, m * D:(m + 1) * D].unsqueeze(1).to_broadcast([P, NB2, D])
        if m == 3:
            src, bias = src.rearrange(heads, d=HD), bias.rearrange(heads, d=HD)
        dve.tensor_tensor(dst, src, bias, ALU.add).then_inc(p.at_q.sem, 1)
    dve.wait_ge(p.at_kr.sem, p.at_kr.at(b + 1))
    dve.wait_ge(p.at_q.sem, p.at_q.at(n + 4))
    r, t1, t2 = (x.rearrange("p w t d -> p w (t d)") for x in (p.at_r, p.at_t1, p.at_t2))
    pairs = "p w (i two) -> p w i two"
    rp, tp = r.rearrange(pairs, two=2), t2.rearrange(pairs, two=2)
    dve.tensor_tensor(t1, r, p.at_cos.unsqueeze(1).to_broadcast([P, 2, S]), ALU.mult).then_inc(p.at_q.sem, 1)
    for k in range(2):
        sin = p.at_sin[:, k, :].unsqueeze(1).to_broadcast([P, 2, S // 2])
        dve.tensor_tensor(tp[:, :, :, k], rp[:, :, :, 1 - k], sin, ALU.mult).then_inc(p.at_q.sem, 1)
    dve.wait_ge(p.at_q.sem, p.at_q.at(n + 7))
    dve.tensor_tensor(t1, t1, t2, ALU.add).then_inc(p.at_q.sem, 1)
    dve.wait_ge(p.at_q.sem, p.at_q.at(n + 8))
    dve.tensor_tensor(t1, t1, p.at_s.rearrange("p w t d -> p w (t d)"), ALU.add).then_inc(p.at_q.sem, 1)


def at_parts_dve(dve, p, b):
    n = NS1 * b
    dve.wait_ge(p.at_q.sem, p.at_q.at(n + 9))
    dve.wait_ge(p.at_q2p.sem, p.at_q2p.at(2 * b))
    qk = p.at_t1.rearrange("p w t (h d) -> p w t h d", d=HD)
    dve.tensor_copy(p.at_sk_r.rearrange("p w t h r -> p (w t h) r")[:, :, 0:HD],
                    p.at_t1.rearrange("p w t (h d) -> p (w t h) d", d=HD)).then_inc(p.at_q.sem, 1)
    dve.wait_ge(p.at_q.sem, p.at_q.at(n + 10))
    for which, c in ((0, 2 * HD), (1, HD)):
        dve.tensor_tensor(p.at_sk_r[:, which, :, :, c:c + HD], qk[:, which], p.at_sk[:, which, :, :, 0:HD],
                          ALU.subtract).then_inc(p.at_q.sem, 1)


def at_search_dve(dve, p, b, f):
    t, pair = searched(f)
    q = 2 * (pair // HQ)
    dve.wait_ge(p.at_s1.sem, p.at_s1.at(NH * b + f + 1))
    dve.tensor_reduce(p.at_m[:, t, :].rearrange("p (q r) -> p q r", r=HQ)[:, q:q + 2, pair % HQ],
                      p.bk[SEARCH_BANKS[f % 3]][:].rearrange("p (h k) -> p h k", h=2), AX.X, ALU.max, negate=True)\
       .then_inc(p.at_mx.sem, 1)


def at_maxima_rows_dve(dve, p, b, half):
    h = slice(half * NH // 2, (half + 1) * NH // 2)
    dve.wait_ge(p.at_mx.sem, p.at_mx.at(NH * b + (half + 1) * NH // 2))
    dve.tensor_copy(p.at_sk_r[:, 0, :, h, NPROD], p.at_m[:, :, h]).then_inc(p.at_nm.sem, 1)
    dve.wait_ge(p.at_nm.sem, p.at_nm.at(4 * b + 2 * half + 1))
    dve.tensor_tensor(p.at_sk_r[:, 0, :, h, NPROD + 1], p.at_m[:, :, h], p.at_sk[:, 0, :, h, NPROD], ALU.subtract)\
       .then_inc(p.at_nm.sem, 1)


def at_searches_dve(dve, p, b, fs):
    for f in fs:
        at_search_dve(dve, p, b, f)
        if f % (NH // 2) == NH // 2 - 1:
            at_maxima_rows_dve(dve, p, b, f // (NH // 2))


def at_norm_dve(dve, p, b):
    dve.wait_ge(p.at_otp.sem, p.at_otp.at(b + 1))
    for t in range(NB2):
        o = p.bk[OUT_BANKS[t]][:].rearrange("p (h r) -> p h r", r=HR)
        dve.reciprocal(p.at_rc[:, t, :], o[:, :, HD]).then_inc(p.at_on.sem, 1)
    dve.wait_ge(p.at_on.sem, p.at_on.at(4 * b + 2))
    for t in range(NB2):
        o = p.bk[OUT_BANKS[t]][:].rearrange("p (h r) -> p h r", r=HR)
        dve.tensor_tensor(p.at_n[:, t, :].rearrange("p (h d) -> p h d", d=HD), o[:, :, 0:HD],
                          p.at_rc[:, t, :].unsqueeze(2).to_broadcast([P, NH, HD]), ALU.mult).then_inc(p.at_on.sem, 1)


def at_bias_dve(dve, p, b):
    x = p.X[:, bass.ds(b * NB2, NB2), :]
    dve.tensor_tensor(x, x, p.at_bo.unsqueeze(1).to_broadcast([P, NB2, D]), ALU.add).then_inc(p.at_x1.sem, 1)


def at_out_dve(dve, p, b):
    x = p.X[:, bass.ds(b * NB2, NB2), :]
    dve.wait_ge(p.at_wp.sem, p.at_wp.at(b + 1))
    dve.wait_ge(p.at_x1.sem, p.at_x1.at(b + 1))
    dve.tensor_tensor(x, x, p.bk[6][:, S:2 * S].rearrange("p (t d) -> p t d", t=NB2), ALU.add).then_inc(p.at_x.sem, 1)


def at_dve_element(dve, p, b, par, behind=True, ahead=2, stats=True):
    if ahead >= 1:
        at_parts_dve(dve, p, b + 1)
    if ahead >= 2:
        ln_apply(dve, p, b + 2, p.xn[:, 0], P - 1, NB2)
    if behind:
        at_norm_dve(dve, p, b - 1)
        at_bias_dve(dve, p, b - 1)
    if stats:
        ln_stats(dve, p, b + 3, NB2)
    if ahead >= 1:
        at_searches_dve(dve, p, b + 1, range(0, 2))
    if behind:
        at_out_dve(dve, p, b - 1)
    if ahead >= 1:
        at_searches_dve(dve, p, b + 1, range(2, NH))
    if ahead >= 2:
        at_project_dve(dve, p, b + 2, par)


def at_dve(dve, p):
    for b in range(2):
        ln_stats(dve, p, b, NB2)
        ln_apply(dve, p, b, p.xn[:, 0], P - 1, NB2)
    ln_stats(dve, p, 2, NB2)
    dve.wait_ge(p.at_init.sem, p.at_init.at(5))
    at_project_dve(dve, p, 0, 0)
    at_parts_dve(dve, p, 0)
    at_searches_dve(dve, p, 0, range(NH))
    at_project_dve(dve, p, 1, 1)
    at_dve_element(dve, p, 0, 0, behind=False)
    at_dve_element(dve, p, 1, 1)
    with dve.Fori(1, B // 2 - 2) as i:
        at_dve_element(dve, p, 2 * i, 0)
        at_dve_element(dve, p, 2 * i + 1, 1)
    at_dve_element(dve, p, B - 4, 0)
    at_dve_element(dve, p, B - 3, 1, stats=False)
    at_dve_element(dve, p, B - 2, 0, ahead=1, stats=False)
    at_dve_element(dve, p, B - 1, 1, ahead=0, stats=False)
    at_norm_dve(dve, p, B - 1)
    at_bias_dve(dve, p, B - 1)
    at_out_dve(dve, p, B - 1)


def at_pool(pool, p):
    pool.memset(p.at_sk[:], 0.0).then_inc(p.at_init.sem, 1)
    pool.memset(p.at_v[:], 0.0).then_inc(p.at_init.sem, 1)
    pool.wait_ge(p.at_init.sem, p.at_init.at(2))
    pool.memset(p.at_sk[:, 1, :, :, NPROD:NPROD + 2], 1.0).then_inc(p.at_init.sem, 1)
    for par in range(2):
        pool.memset(p.at_v[:, par, :, :, HD], 1.0).then_inc(p.at_init.sem, 1)
    with pool.Fori(0, B) as b:
        ln_scale(pool, p, b, NB2)


def at_weights_dve(dve, p):
    dve.wait_ge(p.dma_at.sem, p.dma_at.at(p.nat))
    dve.scalar_tensor_tensor(out=p.at_w, in0=p.at_last, scalar=p.neg_but_last, in1=p.at_w,
                             op0=ALU.mult, op1=ALU.add).then_inc(p.atw.sem, 1)


ENGINES = 4
_PREP = dict(ln_free=NG, ln_stat=2 * NT, ln_rs=2 * NG, xt=NG, xhd=NG, xld=NG, lg=NG, rt1=10 * NG, rt2=7 * NG, rte=NG)
_ROUTE = dict(ln_free=NG, ln_stat=2 * NT, ln_rs=2 * NG, route_init=1, route_xt=NG, route_xc=NG, route_lg=NG,
              route_top=10 * NG, route_e=NG, route_sel=3 * NG, route_pos=NG, route_cnt=2 * NG, route_row=4 * NG,
              route_w=3 * NG, sent_even=8 * TOP * NT, sent_odd=8 * TOP * NT, route_n=1, fin=NFIN, zeroed=16 * E,
              loaded_even=8 * SLOT_TILES, loaded_odd=8 * SLOT_TILES, ystored_even=8 * UNITS, ystored_odd=8 * UNITS,
              comb_row=3,
              xt=UNITS, xhd=UNITS, xld=UNITS)
_COMB = dict(comb_idx=NG, got=16 * TOP * NT, comb=TOP * NT)
USES = {
    "moe": dict(_ROUTE, act_r=4 * UNITS, act_t=4 * UNITS, hid=4 * UNITS, hidT=4 * UNITS, outl=4 * UNITS,
                dve_a=NA * UNITS, dve_b=NB * UNITS, dve_c=NC * UNITS, pl_r=NR * UNITS, pl_g=NGT * UNITS,
                pl_u=NU * (UNITS - 1), dve_u=NU),
    "gau": dict(_COMB, ln_free=B, ln_stat=2 * NT, ln_rs=6 * B, xt=B, ln_both=B, ga_xc=B, ga_qk=B, ga_qkp=B, ga_vg=2 * B,
                ga_vgp=2 * B, ga_hd=2 * B, ga_sw=B, ga_rp=3 * B, ga_lk=B, ga_lkp=B, ga_scp=B, ga_at=2 * B, ga_kv=B,
                ga_kvp=B, ga_o=B, ga_op=B, ga_ot=B, ga_otp=B, ga_y=5 * B, ga_wop=B, ga_rs=2 * B, ga_yn=NB2 * B, ga_px=B, ga_x=NB2 * B),
    "mla": dict(ln_free=B, ln_stat=2 * NT, ln_rs=2 * B, xt=B, at_xc=B, at_ctp=B, at_ct=B, at_krp=B, at_kr=B,
                at_prp=2 * B, at_q=NS1 * B, at_hc=2 * B, at_ktp=2 * B, at_kt=2 * B, at_qtp=2 * B, at_qt=2 * B,
                at_s1=NH * B, at_mx=NH * B, at_nm=4 * B, at_q2p=2 * B, at_q2=2 * B, at_s2=NH * B, at_ex=NH * B,
                at_av=NH * B, at_op=2 * B, at_otp=B, at_on=4 * B, at_tp=B, at_ot=B, at_wp=B, at_x1=B, at_x=B,
                at_init=5),
    "swiglu": dict(_PREP, **_COMB, gt_rows=NCH * NG, up_rows=NCH * NG, silu_d=NCH * NG, hid_d=NCH * NG, exp_d=E1 * NG,
                   exp_add=TG * E1 * NG, rtg=NG, rt3=2 * NG),
}


PHASES = ["moe", "gau", "moe", "swiglu", "mla", "swiglu"]
LOADS = ["xload0", "xload", "dma_tables", "dma_first", "dma_rest", "dma_norm", "dma_sw", "dma_ga", "dma_at"]
ONCE = ["const", "tail0", "wrouter", "wts", "wcopy", "wlast", "wshift", "wpe", "wsw", "gab", "gaw", "atw", "phase_end", "stored",
        "pe_passed", "dve_passed", "pool_passed"]
NW = NQ + 2 * H

TABLES = dict(ident=P, before=P, iota8=E, region0=E, tile0=NT, upto8=E * E, iota72=SLOT_TILES, places=2 * TG,
              neg_but_last=1, wr_f=E, wr_last=E, g1=E * FC, be1=E * FC)

TENSORS = {
    "X": ([P, NT, D], F32),
    "w1h": ([P, E * F], F32R), "w1l": ([P, E * F], F32R), "w2c": ([P, E * F], F32),
    "sa": ([P, E * F], F32), "sb_": ([P, E * F], F32), "sc": ([P, E * F], F32),
    "c2b": ([P, E * D], F32), "g2b": ([P, E * D], F32),
    "be2b": ([P, E * D], F32),
    "tables": ([P, sum(TABLES.values())], F32), "ones_f": ([P, P], F32), "ones_1": ([P, P], F32),
    "neg_half": ([P, 8], F32), "eps8": ([P, 8], F32), "zeros": ([P, D], F32),
    "ln_st": ([P, TG, 6], F32), "ln_mv": ([P, TG, 2], F32), "ln_ve": ([P, TG], F32), "ln_r": ([P, TG], F32),
    "ln_r2": ([P, TG], F32), "route_st": ([P, 2, TG, 6], F32),
    "route_mv": ([P, 2, TG, 2], F32), "route_ve": ([P, 2, TG], F32), "route_r": ([P, 2, TG], F32), "xn": ([P, 2, TG, D], F32), "xf": ([P, TG, D], F32),
    "xh": ([P, 2, W], F32R), "xl": ([P, 2, W], F32R),
    "rt_l": ([P, TG, NL], F32), "rt_m": ([P, TG, 8], F32), "rt_i": ([P, TG, 8], U32), "rt_d": ([P, TG, E], F32),
    "rt_e": ([P, TG, E], F32), "rt_s0": ([P, TG, E], F32), "rt_s1": ([P, TG, E], F32), "rt_z": ([P, TG], F32),
    "rt_r": ([P, TG], F32), "rt_g": ([P, TG], F32),
    "rt_q": ([P, TG, E], F32), "rt_c": ([P, E], F32), "rt_t": ([P, TOP, TG, E], F32), "chosen": ([P, TG, E], F32),
    "counts": ([P, E], F32), "sel": ([P, TOP, NT, E], F32), "row": ([P, TOP, NT], F32), "weight": ([P, NT, TOP], F32),
    "send_row": ([P, 2, TOP, TG], U32), "take_row": ([P, TOP, TG], U32), "out_row": ([P, TOP, NT], U32),
    "en": ([P, E], F32), "e_gt": ([P, E, NT], F32), "e_zero": ([P, E], F32), "e_nt": ([P, E], F32),
    "e_upto": ([P, E, E], F32), "e_skip": ([P, E], F32), "e_cum": ([P, E], F32), "e_first": ([P, E], F32),
    "e_move": ([P, E], F32), "zero_row": ([P, E], I32),
    "t_ex": ([P, SLOT_TILES], F32), "t_exw": ([P, SLOT_TILES + 2 * TG], F32),
    "t_row": ([P, SLOT_TILES], F32), "tile_row": ([P, SLOT_TILES], I32), "t_pack": ([P, 2, UNITS, TG], F32),
    "t_word": ([P, 2, UNITS], F32), "word": ([P, UNITS], I32),
    "c_row": ([P, TOP * NT], F32),
    "gate1": ([P, 2, TG, E1], F32),
    "st1": ([P, 2, TG, 6], F32), "mv1": ([P, 2, TG, 2], F32), "rs1": ([P, 2, TG], F32), "ve1": ([P, 2, TG], F32),
    "st2": ([P, TG, 6], F32), "mv2": ([P, 2, TG, 2], F32), "ve2": ([P, TG], F32), "rs2": ([P, 2, TG], F32),
    "wgh": ([P, ROWS], F32R), "wgl": ([P, ROWS], F32R), "wuh": ([P, ROWS], F32R), "wul": ([P, ROWS], F32R),
    "wd": ([P, len(PIECES) * D], F32), "wr1_f": ([P, NL], F32), "wr1h": ([P, NL], F32R), "wr1l": ([P, NL], F32R),
    "ga_w": ([P, NW], F32), "ga_last": ([P, NW], F32), "ga_ln_w": ([P, 2], F32), "ga_ln_b": ([P, P], F32),
    "ga_brow": ([1, NW], F32), "e_last": ([1, P], F32), "ga_gb": ([NQ, 4], F32), "ga_cos": ([NQ, S], F32),
    "ga_sin": ([NQ, S], F32), "ga_perm": ([NQ, NQ], F32), "ga_wo": ([P, 2 * D], F32), "ga_bo": ([P, D], F32),
    "ga_w2": ([P, D], F32), "ga_b2": ([P, D], F32), "ga_bias": ([P, P], F32), "ga_mask": ([P, P], F32),
}


def named(what, **parts):
    return namedtuple(what, parts)(**parts)


def work_space(t):
    at = Space(t.tables)
    w = {n: at.take(P, cols) for n, cols in TABLES.items()}
    at = Space(t.sb_)
    w.update(r=at.take(P, TG, F), rT=at.take(P, 2, F), y=at.take(P, 2, TG, D))
    at = Space(t.sc)
    w.update(yo=at.take(P, 2, TG, D), slots=at.take(P, 2, TG, D), t_ge=at.take(P, SLOT_TILES, E),
             t_skip=at.take(P, SLOT_TILES, E), c_move=at.take(P, TOP * NT, E), xT=flat(t.xf[:]), be1s=t.wd[:, 0:F], w1_last=t.sb_[0:1, :],
             c2s=t.sc[:].rearrange("p (e f) -> p e f", f=F)[:, :, 0:D],
             ga_taken=(flat(t.xf[:]), t.sel[:].rearrange("p k t e -> p (k t e)")))
    at = Space(t.sb_, 2 * W)
    w.update(sw_taken=(at.take(P, W), at.take(P, W)))

    w.update(hT=Space(t.sc).take(P, HRING, W), sg=Space(t.sb_).take(P, 2, W))

    at = Space(t.sb_)
    w.update(ga_xa=at.take(P, S), ga_q=at.take(NQ, S), ga_h=at.take(NQ, 2, S), ga_r1=at.take(NQ, 2, S),
             ga_r2=at.take(NQ, 2, S), ga_r=at.take(NQ, 2, 2, S), ga_k=at.take(P, P), ga_s=at.take(NQ, H))
    at = Space(t.sc)
    w.update(ga_v=at.take(P, 2, NB2, 2 * H), ga_a1=at.take(P, NB2, P), ga_a=at.take(P, NB2, P),
             ga_g=at.take(P, NB2, H), ga_t=at.take(P, 4 * P))
    at = Space(t.sa, 2 * ROWS)
    w.update(ga_yy=at.take(P, NB2, D), ga_z=at.take(P, NB2, D), ga_st=at.take(P, NB2, 6), ga_mv=at.take(P, NB2, 2),
             ga_ve=at.take(P, NB2), ga_sc=at.take(P, NB2))

    at = Space(t.w2c)
    w.update(at_w=at.take(P, 2 * P), at_last=at.take(P, 2 * P), at_u=at.take(P, 2 * D), at_b=at.take(P, 4 * D),
             at_wo=at.take(P, D), at_bo=at.take(P, D), at_cos=at.take(P, S), at_sin=at.take(P, 2, S // 2))
    at = Space(t.w1h)
    w.update(at_qT=at.take(P, NHQ, S), at_qT2=at.take(P, NHQ, S))
    at = Space(t.sa)
    w.update(at_e=at.take(P, 4, NB2 * S), at_sk=at.take(P, 2, NB2, NH, HR))
    w.update(at_sk_r=w["at_sk"].bitcast(F32R))
    at = Space(t.sb_)
    w.update(at_v=at.take(P, 2, NB2, NH, HR), at_xa=at.take(P, S), at_c=at.take(P, S), at_r=at.take(P, 2, NB2, D),
             at_s=at.take(P, 2, NB2, D), at_t1=at.take(P, 2, NB2, D))
    at = Space(t.sc)
    w.update(at_t2=at.take(P, 2, NB2, D), at_o=at.take(P, NHQ, S), at_n=at.take(P, NB2, D), at_t=at.take(P, S),
             at_m=at.take(P, NB2, NH), at_rc=at.take(P, NB2, NH))
    w.update(at_kT=[x[:].rearrange("p a (b s) -> p (a b) s", s=S) for x in (t.xh, t.xl)])
    return w


def load(sp, dst, src, sem):
    shape = list(dst.shape)
    sp.dma_start(dst, src if src.shape[0] == shape[0] else src.to_broadcast(shape)).then_inc(sem, 16)


def build(nc, io, phases=PHASES):
    with ExitStack() as ctx:
        tally = {n: Tally(ctx.enter_context(nc.semaphore(n)))
                 for n in LOADS + ONCE + sorted({n for uses in USES.values() for n in uses})}
        tensors = {n: ctx.enter_context(nc.sbuf_tensor("sb_" + n, shape, dt)) for n, (shape, dt) in TENSORS.items()}
        t = named("Tensors", **tensors)
        w = work_space(t)
        ga_loads = [(t.ga_w[:], "ga_raw"), (t.ga_last[:], "ga_last"), (t.ga_ln_w[:, 0:1], "ga_ln_w"),
                    (t.ga_ln_w[:, 1:2], "ga_ln_w_last"), (t.ga_ln_b[:], "ga_ln_b"), (t.ga_brow[:], "ga_brow"),
                    (t.e_last[:], "e_last"), (t.ga_gb[:], "ga_gb"), (t.ga_cos[:], "ga_cos"), (t.ga_sin[:], "ga_sin"),
                    (t.ga_perm[:], "ga_perm"), (t.ga_wo[:], "ga_wo"), (t.ga_bo[:], "ga_bo"), (t.ga_w2[:], "ga_w2"),
                    (t.ga_b2[:], "ga_b2"), (t.ga_bias[:], "ga_bias"), (t.ga_mask[:], "ga_mask")]
        at_loads = [(w["at_w"], "at_w"), (w["at_last"], "at_last"), (w["at_u"], "at_u"), (w["at_b"], "at_b"),
                    (w["at_wo"], "at_wo"), (w["at_bo"], "at_bo"), (w["at_cos"], "at_cos"), (w["at_sin"], "at_sin")]
        scratch = {"xs": nc.dram_tensor("xs", (XS_ROWS, D), F32).ap(), "ys": nc.dram_tensor("ys", (SLOT_TILES * P, D), F32).ap()}
        pairs = {n: (tally[n + "_even"], tally[n + "_odd"]) for n in ("sent", "loaded", "ystored")}
        p = named("Program", phases=phases, tally=tally, nga=16 * len(ga_loads),
                  nat=16 * len(at_loads), bk=[ctx.enter_context(nc.psum_tensor(f"bk{i}", [P, 512], F32)) for i in range(8)],
                  **tally, **tensors, **scratch, **pairs, **w)

        block = ctx.enter_context(nc.Block())

        @block.sync
        def _(sp):
            sp.dma_start(p.tables[:], io["tables"]).then_inc(p.dma_tables.sem, 16)
            sp.dma_start(p.w1_last, io["w1_last"]).then_inc(p.dma_tables.sem, 16)
            first, rest = slice(0, F), slice(F, E * F)
            for c, sem in ((first, p.dma_first), (rest, p.dma_rest)):
                sp.dma_start(p.sa[:, c], io["w1"][:, c]).then_inc(sem.sem, 16)
                sp.dma_start(p.sc[:, c], io["w2"][:, c]).then_inc(sem.sem, 16)
            load(sp, p.c2b[:], io["b2"], p.dma_rest.sem)
            load(sp, p.g2b[:], io["g2"], p.dma_norm.sem)
            load(sp, p.be2b[:], io["be2"], p.dma_norm.sem)
            sp.wait_ge(p.const.sem, p.const.at(NCONST))
            for q in range(E):
                sp.dma_start(p.xs[E * REGION + q * P:E * REGION + (q + 1) * P, :], p.zeros[:]).then_inc(p.tail0.sem, 16)
            for dst, n in ga_loads:
                load(sp, dst, io[n], p.dma_ga.sem)
            sp.wait_ge(p.tail0.sem, p.tail0.at(16 * E))
            for n, phase in enumerate(p.phases):
                begin(sp, p, n)
                if "moe" not in p.phases[n:] and (n == 0 or p.phases[n - 1] == "moe"):
                    for dst, src in at_loads:
                        load(sp, dst, io[src], p.dma_at.sem)
                if phase == "moe":
                    moe_sp(sp, p)
                    if "moe" not in p.phases[:n]:
                        sp.wait_ge(p.wts.sem, p.wts.at(NWT * E))
                        sp.wait_ge(p.wcopy.sem, p.wcopy.at(3 * E))
                        sp.dma_start(p.sa[:, 0:2 * ROWS], io["w_gu"]).then_inc(p.dma_sw.sem, 16)
                        sp.dma_start(p.wr1_f[:], io["w_r1"]).then_inc(p.dma_sw.sem, 16)
                        sp.dma_start(p.wd[:], io["w_d"]).then_inc(p.dma_sw.sem, 16)
            sp.wait_ge(p.phase_end.sem, p.phase_end.at(ENGINES * len(p.phases)))
            out = io["out"].rearrange("(t p) d -> p t d", p=P)
            sp.dma_start(out, p.X[:]).then_inc(p.stored.sem, 16)
            sp.wait_ge(p.stored.sem, p.stored.at(16))

        @block.gpsimd
        def _(pool):
            pool.memset(p.neg_half[:], -0.5).then_inc(p.const.sem, 1)
            pool.memset(p.ones_f[:], 1.0 / F).then_inc(p.const.sem, 1)
            pool.memset(p.xn[:], 1.0).then_inc(p.const.sem, 1)
            pool.memset(p.eps8[:], EPS).then_inc(p.const.sem, 1)
            pool.memset(p.ones_1[:], 1.0).then_inc(p.const.sem, 1)
            pool.memset(p.zeros[:], 0.0).then_inc(p.const.sem, 1)
            pool.memset(p.t_exw[:], 0.0).then_inc(p.const.sem, 1)
            pool.wait_ge(p.const.sem, p.const.at(NCONST))
            for n, phase in enumerate(p.phases):
                begin(pool, p, n)
                if phase == "moe":
                    moe_pool(pool, p)
                elif phase == "gau":
                    ga_bias_pool(pool, p)
                    ga_pool(pool, p)
                elif phase == "swiglu":
                    sw_pool(pool, p, p.phases[n - 1] == "moe")
                elif phase == "mla":
                    at_pool(pool, p)
                end(pool, p)

        @block.scalar
        def _(act):
            xs = io["x"].rearrange("(t p) d -> p t d", p=P)
            act.dma_start(p.X[:, 0:TG, :], xs[:, 0:TG, :]).then_inc(p.xload0.sem, 16)
            act.dma_start(p.X[:, TG:NT, :], xs[:, TG:NT, :]).then_inc(p.xload.sem, 16)
            for n, phase in enumerate(p.phases):
                begin(act, p, n)
                if phase == "moe":
                    moe_act(act, p, phase not in p.phases[:n])
                elif phase == "gau":
                    ga_act(act, p)
                elif phase == "swiglu":
                    sw_act(act, p)
                elif phase == "mla":
                    at_act(act, p)
                end(act, p)

        @block.vector
        def _(dve):
            dve.wait_ge(p.const.sem, p.const.at(NCONST))
            dve.wait_ge(p.dma_tables.sem, p.dma_tables.at(32))
            dve.wait_ge(p.xload0.sem, p.xload0.at(16))
            for n, phase in enumerate(p.phases):
                begin(dve, p, n)
                if phase == "gau":
                    dve.wait_ge(p.gab.sem, p.gab.at(1))
                    ga_weights_dve(dve, p)
                if phase == "mla":
                    at_weights_dve(dve, p)
                if phase == "moe":
                    moe_dve(dve, p, phase not in p.phases[:n], p.phases[n + 1] == "swiglu")
                elif phase == "gau":
                    ga_dve(dve, p)
                elif phase == "swiglu":
                    sw_dve(dve, p, p.phases[n - 1] == "moe")
                elif phase == "mla":
                    at_dve(dve, p)
                end(dve, p)

        @block.tensor
        def _(pe):
            pe.wait_ge(p.dma_tables.sem, p.dma_tables.at(32))
            pe.wait_ge(p.const.sem, p.const.at(NCONST))
            for n, phase in enumerate(p.phases):
                begin(pe, p, n)
                if phase == "swiglu" and phase not in p.phases[:n]:
                    pe.wait_ge(p.wsw.sem, p.wsw.at(6))
                if phase == "gau":
                    ga_weights_pe(pe, p)
                if phase == "mla":
                    pe.wait_ge(p.atw.sem, p.atw.at(1))
                if phase == "moe":
                    if phase not in p.phases[:n]:
                        pe.wait_ge(p.wrouter.sem, p.wrouter.at(1))
                    moe_pe(pe, p, phase not in p.phases[:n])
                elif phase == "gau":
                    ga_pe(pe, p)
                elif phase == "swiglu":
                    sw_pe(pe, p)
                elif phase == "mla":
                    at_pe(pe, p)
                end(pe, p)


def first_mixture_layout(inp):
    w1 = inp["L0_ffn_W1"].transpose(1, 0, 2).reshape(D, E * F)
    neg = -np.ones((P, 1), np.float32)
    neg[P - 1] = 0
    n = np.arange(P, dtype=np.float32)
    def rows(a):
        return np.broadcast_to(a, (P, a.size))
    tables = dict(
        ident=np.eye(P, dtype=np.float32), before=(n[:, None] < n[None]).astype(np.float32), iota8=rows(n[:E]),
        region0=rows(REGION * n[:E]), tile0=rows(P * n[:NT]), iota72=rows(n[:SLOT_TILES]),
        upto8=rows((n[None, :E] <= n[:E, None]).astype(np.float32).reshape(-1)),
        places=rows(np.where(np.arange(2 * TG) < TG + 3, float(E) ** np.arange(2 * TG), 0).astype(np.float32)),
        neg_but_last=neg, wr_f=np.concatenate([inp["L0_ffn_Wr"][:P - 1], inp["L0_ffn_br"][None]], 0),
        wr_last=np.broadcast_to(inp["L0_ffn_Wr"][P - 1:P], (P, E)), g1=inp["L0_ffn_g1"].reshape(E * FC, P).T,
        be1=inp["L0_ffn_be1"].reshape(E * FC, P).T)
    return dict(
        tables=np.concatenate([tables[t] for t in TABLES], 1),
        w1=np.concatenate([w1[:P - 1], inp["L0_ffn_b1"].reshape(1, E * F)], 0), w1_last=w1[P - 1:P],
        w2=inp["L0_ffn_W2"].reshape(E, FC, P, D).transpose(2, 0, 1, 3).reshape(P, E * F),
        b2=inp["L0_ffn_b2"].reshape(1, E * D), g2=inp["L0_ffn_g2"].reshape(1, E * D),
        be2=inp["L0_ffn_be2"].reshape(1, E * D))


def second_mixture_layout(inp):
    eg, h = inp["L1_ffn_experts_gate_up"], E * I1
    gate = np.concatenate([eg[:, :I1].reshape(h, D), inp["L1_ffn_shared_gate_w"]], 0).T
    up = np.concatenate([eg[:, I1:].reshape(h, D), inp["L1_ffn_shared_up_w"]], 0).T
    down = np.concatenate([inp["L1_ffn_experts_down"].transpose(0, 2, 1).reshape(h, D), inp["L1_ffn_shared_down_w"].T], 0)
    router = np.zeros((P, NL), np.float32)
    router[:, :E] = inp["L1_ffn_gate_w"].T
    router[:, E] = inp["L1_ffn_shared_expert_gate_w"][0]
    pieces = np.zeros((P, len(PIECES), D), np.float32)
    for q, (c, e) in enumerate(PIECES):
        a, z = max(c * P, e * I1), min(c * P + P, e * I1 + I1 if e < E else ROWS)
        pieces[a - c * P:z - c * P, q] = down[a:z]
    return dict(w_gu=np.concatenate([gate, up], 1), w_r1=router, w_d=pieces.reshape(P, -1))


def gated_unit_layout(inp):
    f = {n[8:]: a for n, a in inp.items() if n.startswith("L0_attn_")}
    qk = f["Wqk"].T
    w = np.concatenate([qk, qk, f["Wv"].T, f["Wg"].T], 1)
    ln_b = np.zeros((P, P), np.float32)
    ln_b[:, P - 1] = f["ln1_b"]
    e_last = np.zeros((1, P), np.float32)
    e_last[0, P - 1] = 1
    ga, be = f["gamma"], f["beta"]
    half = QK // 2
    freq = (10000.0 ** (-np.arange(half, dtype=np.float32) / half)).astype(np.float32)
    angle = np.arange(S, dtype=np.float32)[:, None] * freq[None]
    sin, cos = np.sin(angle).T.astype(np.float32), np.cos(angle).T.astype(np.float32)
    perm = np.zeros((NQ, NQ), np.float32)
    for i in range(NQ):
        perm[i // QK * QK + (i + half) % QK, i] = 1
    i = np.arange(P)
    same = (i[:, None] // GROUP) == (i[None] // GROUP)
    pos = f["pos_emb"][:MAXREL + 1]
    far = np.broadcast_to(pos[MAXREL], P - 1 - MAXREL)
    by_distance = np.concatenate([far, pos[:0:-1], pos, far])
    return dict(
        ga_raw=w, ga_last=w[P - 1:P], ga_ln_w=f["ln1_w"].reshape(P, 1), ga_ln_w_last=f["ln1_w"].reshape(P, 1)[P - 1:P],
        ga_ln_b=ln_b, ga_brow=np.concatenate([f["bqk"], f["bqk"], f["bv"], f["bg"]])[None], e_last=e_last,
        ga_gb=np.stack([np.concatenate([ga[0], ga[1]]), np.concatenate([be[0], be[1]]),
                        np.concatenate([ga[2], ga[3]]), np.concatenate([be[2], be[3]])], 1),
        ga_cos=np.concatenate([cos] * 4, 0), ga_sin=np.concatenate([-sin, sin] * 2, 0), ga_perm=perm,
        ga_wo=f["Wo"].T.reshape(2, P, D).transpose(1, 0, 2).reshape(P, 2 * D), ga_bo=f["bo"][None],
        ga_w2=f["ln2_w"][None], ga_b2=f["ln2_b"][None], ga_bias=np.stack([by_distance[P - 1 - r:2 * P - 1 - r] for r in i]),
        ga_mask=np.where(same, 0, -1e30).astype(np.float32))


def latent_attention_layout(inp):
    f = {n[8:]: a for n, a in inp.items() if n.startswith("L1_attn_")}
    w = np.concatenate([f["Wd_q_w"], f["Wd_kv_w"], f["Wk_r_w"]], 1)
    b = np.concatenate([f["Wd_q_b"], f["Wd_kv_b"], f["Wk_r_b"]])
    half = D // 2
    theta = (np.float32(10000.0) ** (-2.0 * np.arange(half, dtype=np.float32)) / half).astype(np.float32)
    angle = np.arange(S, dtype=np.float32)[:, None] * theta[None]
    cos, sin = np.cos(angle).astype(np.float32), np.sin(angle).astype(np.float32)
    sin = sin.reshape(NB2, P, half).transpose(1, 0, 2).reshape(P, NB2 * half)
    return dict(
        at_w=np.concatenate([w[:P - 1], b[None]], 0), at_last=w[P - 1:P],
        at_u=np.concatenate([np.concatenate([f["Wq_r_w"], f["Wu_q_w"]], 1),
                             np.concatenate([f["Wu_k_w"], f["Wu_v_w"]], 1)], 0),
        at_b=np.concatenate([f["Wq_r_b"], f["Wu_q_b"], f["Wu_k_b"], f["Wu_v_b"]])[None],
        at_wo=f["Wo_w"], at_bo=f["Wo_b"][None], at_sin=np.stack([-sin, sin], 1),
        at_cos=np.repeat(cos, 2, 1).reshape(NB2, P, D).transpose(1, 0, 2).reshape(P, NB2 * D))


def layout(inputs):
    inp = {n: np.asarray(a) for n, a in inputs.items()}
    out = {"x": inp["L0_attn_x"].reshape(B * S, D)}
    for part in (first_mixture_layout, second_mixture_layout, gated_unit_layout, latent_attention_layout):
        out.update(part(inp))
    return {n: np.ascontiguousarray(a) for n, a in out.items()}


def kernel(**inputs):
    import concourse.bacc as bacc
    from concourse.bass_utils import run_bass_kernel_spmd

    arrays = layout(inputs)
    nc = bacc.Bacc("TRN2", target_bir_lowering=False, num_devices=1)
    io = {n: nc.dram_tensor(n, a.shape, mybir.dt.from_np(a.dtype), kind="ExternalInput").ap() for n, a in arrays.items()}
    io["out"] = nc.dram_tensor("out", (B * S, D), F32, kind="ExternalOutput").ap()
    build(nc, io)
    r = run_bass_kernel_spmd(nc, [arrays], core_ids=[0])
    return r.results[0]["out"].reshape(B, S, D)
```
